# Optimizing a Trainium2 kernel written in Bass

```python
import numpy as np
import jax
import jax.numpy as jnp

def _softmax(x, axis=-1):
    return jax.nn.softmax(x, axis=axis)

def _gelu(x):
    return jax.nn.gelu(x, approximate=True)

def _silu(x):
    return jax.nn.silu(x)

def _sigmoid(x):
    return jax.nn.sigmoid(x)

def _layernorm(x, axis=-1, eps=1e-05):
    m = jnp.mean(x, axis=axis, keepdims=True)
    v = jnp.var(x, axis=axis, keepdims=True)
    return (x - m) / jnp.sqrt(v + eps)

def _scatter_add(tgt, idx, src, axis=0):
    return tgt.at[idx].add(src)

def _segment_sum(src, seg, n):
    return jax.ops.segment_sum(src, seg, n)
kernel_name = 'mk_decoder_preln_d2_seqx_r8_63eee2'

def setup_inputs(seed: int=0):
    np.random.seed(seed)
    _w = jnp.asarray

    def _rec_inputs():
        import jax
        import jax.numpy as jnp
        _rk = jax.random.key(seed)
        x = -0.0002928 + 1 * jax.random.normal(jax.random.fold_in(_rk, 1), (64, 64, 256), jnp.float32)
        _lenS = 64 - jax.random.randint(jax.random.fold_in(_rk, 7), (64,), 0, max(1, 64 // 4) + 1, jnp.int32)
        _lenS2 = 64 - jax.random.randint(jax.random.fold_in(_rk, 8), (64,), 0, max(1, 64 // 4) + 1, jnp.int32)
        _ctx_2048P = jax.random.normal(jax.random.fold_in(_rk, 11), (64, 16, 256), jnp.float32)
        _ctx_2048c = jax.random.dirichlet(jax.random.fold_in(_rk, 511), 0.3 * jnp.ones((16,), jnp.float32), (64, 64))
        _ctx_2048t = jnp.einsum('bsk,bkd->bsd', _ctx_2048c, _ctx_2048P)
        _ctx_2048t = _ctx_2048t * jax.lax.rsqrt(jnp.mean(jnp.square(_ctx_2048t)) + 1e-12) * 0.953939
        ctx_2048 = -1.39393e-06 + 0.999914 * (_ctx_2048t + 0.3 * jax.random.normal(jax.random.fold_in(_rk, 611), (64, 64, 256), jnp.float32))
        _validS = jnp.arange(64)[None, :] < _lenS[:, None]
        _validS2 = jnp.arange(64)[None, :] < _lenS2[:, None]
        _causal = jnp.tril(jnp.ones((64, 64), dtype=bool))
        mask_BxS2_bf1 = jnp.ones((64, 64), dtype=bool)
        return (x, ctx_2048, mask_BxS2_bf1)
    x, ctx_2048, mask_BxS2_bf1 = _rec_inputs()

    def _L0_attn_setup():
        import jax, jax.numpy as jnp
        import numpy as np
        B, T, HID = (1, 128, 256)
        H, DK, DV, M, KW = (16, 128, 128, 128, 4)
        SCALE = DK ** (-0.5)
        EPS = 1e-05

        def short_conv(x, w):
            K = w.shape[1]
            xp = jnp.pad(x, ((0, 0), (K - 1, 0), (0, 0)))
            t = x.shape[1]
            y = sum((xp[:, i:i + t] * w[:, i] for i in range(K)))
            return jax.nn.silu(y)

        def l2norm(x):
            return x * jax.lax.rsqrt(jnp.sum(x * x, axis=-1, keepdims=True) + 1e-06)

        def gsa2_scan(q, k, v, w, g, beta):
            b = q.shape[0]
            tm = lambda x: jnp.moveaxis(x, 1, 0)
            Sk0 = jnp.zeros((b, H, DK, M), q.dtype)
            Sv0 = jnp.zeros((b, H, M, DV), q.dtype)

            def step(carry, xs):
                Sk, Sv = carry
                q_t, k_t, v_t, w_t, g_t, b_t = xs
                gt = jnp.exp(g_t)
                bw = b_t[:, :, None] * w_t
                Sk = Sk * gt[:, :, None, :] + k_t[..., :, None] * bw[:, :, None, :]
                Sv = Sv * gt[..., None] + bw[..., None] * v_t[:, :, None, :]
                s = jnp.einsum('bhd,bhdm->bhm', q_t, Sk) * SCALE
                a = jax.nn.softmax(s, axis=-1)
                o_t = jnp.einsum('bhm,bhmd->bhd', a, Sv)
                return ((Sk, Sv), o_t)
            (_, _), o = jax.lax.scan(step, (Sk0, Sv0), (tm(q), tm(k), tm(v), tm(w), tm(g), tm(beta)))
            return jnp.moveaxis(o, 0, 1)
        key = jax.random.key(seed)
        ks = jax.random.split(key, 16)
        s = 0.02
        return {'hidden_states': jax.random.normal(ks[0], (B, T, HID), jnp.float32), 'Wq': jax.random.normal(ks[1], (HID, H * DK), jnp.float32) * s, 'Wk': jax.random.normal(ks[2], (HID, H * DK), jnp.float32) * s, 'Wv': jax.random.normal(ks[3], (HID, H * DV), jnp.float32) * s, 'Ww': jax.random.normal(ks[4], (HID, H * M), jnp.float32) * s, 'cq': jax.random.normal(ks[5], (H * DK, KW), jnp.float32) * 0.2, 'ck': jax.random.normal(ks[6], (H * DK, KW), jnp.float32) * 0.2, 'cv': jax.random.normal(ks[7], (H * DV, KW), jnp.float32) * 0.2, 'Wf1': jax.random.normal(ks[8], (HID, DV), jnp.float32) * s, 'Wf2': jax.random.normal(ks[9], (DV, H * M), jnp.float32) * s, 'Wb': jax.random.normal(ks[10], (HID, H), jnp.float32) * s, 'Wg1': jax.random.normal(ks[11], (HID, DV), jnp.float32) * s, 'Wg2': jax.random.normal(ks[12], (DV, H * DV), jnp.float32) * s, 'bg2': jnp.zeros((H * DV,), jnp.float32), 'norm_w': jnp.ones((DV,), jnp.float32), 'Wo': jax.random.normal(ks[13], (H * DV, HID), jnp.float32) * s}
    _L0_attn_all = _L0_attn_setup()
    _L0_attn_in = {k: v for k, v in _L0_attn_all.items() if k in ('Wq', 'Wk', 'Wv', 'Ww', 'cq', 'ck', 'cv', 'Wf1', 'Wf2', 'Wb', 'Wg1', 'Wg2', 'bg2', 'norm_w', 'Wo')}
    del _L0_attn_all

    def _L0_xattn_setup():
        import jax, jax.numpy as jnp
        import numpy as np
        B, S, E, NH = (2, 128, 256, 16)
        DH = E // NH
        EPS = 1e-06

        def _mlstm_forward(q, k, v, Wi, bi, Wf, bf, ln_scale):
            b, s, e = q.shape
            nh = Wi.shape[1]
            dh = e // nh
            x = jnp.concatenate([q, k, v], axis=-1)
            ig = (x @ Wi + bi).transpose(0, 2, 1)[..., None]
            fg = (x @ Wf + bf).transpose(0, 2, 1)[..., None]
            split = lambda t: t.reshape(b, s, nh, dh).transpose(0, 2, 1, 3)
            qh, kh, vh = (split(q), split(k), split(v))
            log_f = jax.nn.log_sigmoid(fg)
            log_f_cum = jnp.concatenate([jnp.zeros((b, nh, 1, 1), q.dtype), jnp.cumsum(log_f, axis=2)], axis=2)
            fg_mat = log_f_cum - jnp.transpose(log_f_cum, (0, 1, 3, 2))
            ltr = jnp.tril(jnp.ones((s, s), dtype=bool))
            log_fg = jnp.where(ltr, fg_mat[:, :, 1:, 1:], -jnp.inf)
            log_D = log_fg + jnp.transpose(ig, (0, 1, 3, 2))
            max_log_D = jnp.max(log_D, axis=-1, keepdims=True)
            D = jnp.exp(log_D - max_log_D)
            qk = jnp.einsum('bhsd,bhtd->bhst', qh, kh) / jnp.sqrt(jnp.asarray(dh, q.dtype))
            C = qk * D
            normalizer = jnp.maximum(jnp.abs(C.sum(-1, keepdims=True)), jnp.exp(-max_log_D))
            Cn = C / (normalizer + EPS)
            h = jnp.einsum('bhst,bhtd->bhsd', Cn, vh)
            mu = h.mean(-1, keepdims=True)
            var = ((h - mu) ** 2).mean(-1, keepdims=True)
            hn = (h - mu) * jax.lax.rsqrt(var + EPS)
            hn = hn * ln_scale.reshape(1, nh, 1, dh)
            return hn.transpose(0, 2, 1, 3).reshape(b, s, e)
        key = jax.random.key(seed)
        ks = jax.random.split(key, 6)
        q = jax.random.normal(ks[0], (B, S, E), dtype=jnp.float32)
        k = jax.random.normal(ks[1], (B, S, E), dtype=jnp.float32)
        v = jax.random.normal(ks[2], (B, S, E), dtype=jnp.float32)
        Wi = jax.random.normal(ks[3], (3 * E, NH), dtype=jnp.float32) * 0.02
        bi = jax.random.normal(ks[4], (NH,), dtype=jnp.float32) * 0.1
        Wf = jax.random.normal(ks[5], (3 * E, NH), dtype=jnp.float32) * 0.02
        bf = jnp.linspace(3.0, 6.0, NH, dtype=jnp.float32)
        ln_scale = jnp.ones((E,), dtype=jnp.float32)
        return {'q': q, 'k': k, 'v': v, 'Wi': Wi, 'bi': bi, 'Wf': Wf, 'bf': bf, 'ln_scale': ln_scale}
    _L0_xattn_all = _L0_xattn_setup()
    _L0_xattn_in = {k: v for k, v in _L0_xattn_all.items() if k in ('Wi', 'bi', 'Wf', 'bf', 'ln_scale')}
    del _L0_xattn_all

    def _L0_ffn_setup():
        import jax, jax.numpy as jnp
        import numpy as np
        HID = 256
        N_HEADS = 16
        N_KV = 16
        HEAD_DIM = HID // N_HEADS
        N_EXP = 8
        TOP_K = 2
        MOE_I = 176
        SH_I = 704
        EPS = 1e-06
        ROPE_THETA = 1000000.0

        def _rms(x, w):
            v = jnp.mean(jnp.square(x), axis=-1, keepdims=True)
            return x * jax.lax.rsqrt(v + EPS) * w

        def _rope(q, k):
            S, D = (q.shape[1], q.shape[-1])
            inv = 1.0 / ROPE_THETA ** (jnp.arange(0, D, 2, dtype=jnp.float32) / D)
            freqs = jnp.arange(S, dtype=jnp.float32)[:, None] * inv[None, :]
            emb = jnp.concatenate([freqs, freqs], axis=-1)
            cos = jnp.cos(emb)[None, :, None, :]
            sin = jnp.sin(emb)[None, :, None, :]

            def rot(t):
                t1, t2 = (t[..., :D // 2], t[..., D // 2:])
                return jnp.concatenate([-t2, t1], axis=-1)
            return (q * cos + rot(q) * sin, k * cos + rot(k) * sin)
        key = jax.random.key(seed)
        ks = jax.random.split(key, 20)
        s = 0.02
        d = {'x': jax.random.normal(ks[0], (2, 128, HID), jnp.float32), 'w_ln1': jnp.ones((HID,), jnp.float32), 'wq': jax.random.normal(ks[1], (HID, N_HEADS * HEAD_DIM), jnp.float32) * s, 'bq': jnp.zeros((N_HEADS * HEAD_DIM,), jnp.float32), 'wk': jax.random.normal(ks[2], (HID, N_KV * HEAD_DIM), jnp.float32) * s, 'bk': jnp.zeros((N_KV * HEAD_DIM,), jnp.float32), 'wv': jax.random.normal(ks[3], (HID, N_KV * HEAD_DIM), jnp.float32) * s, 'bv': jnp.zeros((N_KV * HEAD_DIM,), jnp.float32), 'wo': jax.random.normal(ks[4], (N_HEADS * HEAD_DIM, HID), jnp.float32) * s, 'w_ln2': jnp.ones((HID,), jnp.float32), 'w_router': jax.random.normal(ks[5], (HID, N_EXP), jnp.float32) * s, 'w_gate_e': jax.random.normal(ks[6], (N_EXP, HID, MOE_I), jnp.float32) * s, 'w_up_e': jax.random.normal(ks[7], (N_EXP, HID, MOE_I), jnp.float32) * s, 'w_down_e': jax.random.normal(ks[8], (N_EXP, MOE_I, HID), jnp.float32) * s, 'w_sh_gate': jax.random.normal(ks[9], (HID, SH_I), jnp.float32) * s, 'w_sh_up': jax.random.normal(ks[10], (HID, SH_I), jnp.float32) * s, 'w_sh_down': jax.random.normal(ks[11], (SH_I, HID), jnp.float32) * s, 'w_sh_eg': jax.random.normal(ks[12], (HID, 1), jnp.float32) * s}
        return d
    _L0_ffn_all = _L0_ffn_setup()
    _L0_ffn_in = {k: v for k, v in _L0_ffn_all.items() if k in ('w_ln1', 'wq', 'bq', 'wk', 'bk', 'wv', 'bv', 'wo', 'w_ln2', 'w_router', 'w_gate_e', 'w_up_e', 'w_down_e', 'w_sh_gate', 'w_sh_up', 'w_sh_down', 'w_sh_eg')}
    del _L0_ffn_all

    def _L1_attn_setup():
        import jax, jax.numpy as jnp
        import numpy as np
        NUM_HEADS = 16
        EPS = 1e-06

        def elu_plus_one(x):
            return jax.nn.elu(x) + 1.0

        def _retrieve(q, memories, memory_norms):
            sigma_q = elu_plus_one(q)
            a_mem = jnp.einsum('bsd,mde->mbse', sigma_q, memories)
            raw = jnp.einsum('bsd,md->mbs', sigma_q, memory_norms)
            per_mem = a_mem / jnp.clip(raw, EPS, None)[..., None]
            rel = raw.mean(axis=-1)
            w = jax.nn.softmax(rel, axis=0)
            return jnp.einsum('mbse,mb->bse', per_mem, w)

        def _local_causal_attention(q, k, v):
            B, S, D = q.shape
            hd = D // NUM_HEADS
            qh = q.reshape(B, S, NUM_HEADS, hd).transpose(0, 2, 1, 3)
            kh = k.reshape(B, S, NUM_HEADS, hd).transpose(0, 2, 1, 3)
            vh = v.reshape(B, S, NUM_HEADS, hd).transpose(0, 2, 1, 3)
            scores = jnp.einsum('bhqd,bhkd->bhqk', qh, kh) * hd ** (-0.5)
            causal = jnp.tril(jnp.ones((S, S), dtype=bool))
            scores = jnp.where(causal, scores, jnp.float32(-1000000000.0))
            attn = jax.nn.softmax(scores, axis=-1)
            out = jnp.einsum('bhqk,bhkd->bhqd', attn, vh)
            return out.transpose(0, 2, 1, 3).reshape(B, S, D)
        key = jax.random.key(seed)
        ks = jax.random.split(key, 8)
        B, S, H, D, M = (2, 256, 256, 256, 4)
        x = jax.random.normal(ks[0], (B, S, H), jnp.float32)
        w_q = jax.random.normal(ks[1], (D, H), jnp.float32) * 0.02
        w_k = jax.random.normal(ks[2], (D, H), jnp.float32) * 0.02
        w_v = jax.random.normal(ks[3], (D, H), jnp.float32) * 0.02
        w_o = jax.random.normal(ks[4], (H, D), jnp.float32) * 0.02
        gate = jnp.zeros((1,), jnp.float32)
        memories = jax.random.normal(ks[5], (M, D, D), jnp.float32) * 0.02
        memory_norms = jax.random.uniform(ks[6], (M, D), jnp.float32) * float(S)
        return {'x': x, 'w_q': w_q, 'w_k': w_k, 'w_v': w_v, 'w_o': w_o, 'gate': gate, 'memories': memories, 'memory_norms': memory_norms}
    _L1_attn_all = _L1_attn_setup()
    _L1_attn_in = {k: v for k, v in _L1_attn_all.items() if k in ('w_q', 'w_k', 'w_v', 'w_o', 'gate', 'memories', 'memory_norms')}
    del _L1_attn_all

    def _L1_xattn_setup():
        import jax, jax.numpy as jnp
        import numpy as np
        import math
        D_MODEL = 256
        N_Q_HEADS = 16
        N_KV_HEADS = 4
        HEAD_DIM = D_MODEL // N_Q_HEADS
        B = 4
        S = 128

        def _alibi_slopes(num_heads):
            n = 2 ** int(math.floor(math.log2(num_heads)))
            m0 = 2.0 ** (-8.0 / n)
            return m0 ** jnp.arange(1, n + 1, dtype=jnp.float32)
        key = jax.random.key(seed)
        ks = jax.random.split(key, 8)
        xavier = lambda k, fi, fo: jax.random.normal(k, (fi, fo), jnp.float32) * math.sqrt(2.0 / (fi + fo))
        return {'query': jax.random.normal(ks[0], (B, S, D_MODEL), jnp.float32), 'key': jax.random.normal(ks[1], (B, S, D_MODEL), jnp.float32), 'value': jax.random.normal(ks[2], (B, S, D_MODEL), jnp.float32), 'mask': jnp.ones((B, S), dtype=bool), 'Wq': xavier(ks[3], D_MODEL, N_Q_HEADS * HEAD_DIM), 'Wk': xavier(ks[4], D_MODEL, N_KV_HEADS * HEAD_DIM), 'Wv': xavier(ks[5], D_MODEL, N_KV_HEADS * HEAD_DIM), 'Wo': xavier(ks[6], D_MODEL, D_MODEL)}
    _L1_xattn_all = _L1_xattn_setup()
    _L1_xattn_in = {k: v for k, v in _L1_xattn_all.items() if k in ('Wq', 'Wk', 'Wv', 'Wo')}
    del _L1_xattn_all

    def _L1_ffn_setup():
        import jax, jax.numpy as jnp
        import numpy as np
        B, S, H = (2, 128, 256)
        E, K, F = (8, 2, 176)
        N_SHARED = 2
        FS = F * N_SHARED
        ROUTED_SCALE = 1.0

        def _swiglu_mlp(x, wg, wu, wd):
            return jax.nn.silu(x @ wg.T) * (x @ wu.T) @ wd.T
        key = jax.random.key(seed)
        ks = jax.random.split(key, 8)

        def w(k, shape, fan_in):
            return jax.random.normal(k, shape, jnp.float32) * (1.0 / np.sqrt(fan_in))
        return {'hidden_states': jax.random.normal(ks[0], (B, S, H), jnp.float32), 'gate_weight': w(ks[1], (E, H), H), 'w_gate': w(ks[2], (E, F, H), H), 'w_up': w(ks[3], (E, F, H), H), 'w_down': w(ks[4], (E, H, F), F), 'sw_gate': w(ks[5], (FS, H), H), 'sw_up': w(ks[6], (FS, H), H), 'sw_down': w(ks[7], (H, FS), FS)}
    _L1_ffn_all = _L1_ffn_setup()
    _L1_ffn_in = {k: v for k, v in _L1_ffn_all.items() if k in ('gate_weight', 'w_gate', 'w_up', 'w_down', 'sw_gate', 'sw_up', 'sw_down')}
    del _L1_ffn_all
    return {'x': x, 'ctx_2048': ctx_2048, 'mask_BxS2_bf1': mask_BxS2_bf1, 'L0_attn_Wq': _L0_attn_in['Wq'], 'L0_attn_Wk': _L0_attn_in['Wk'], 'L0_attn_Wv': _L0_attn_in['Wv'], 'L0_attn_Ww': _L0_attn_in['Ww'], 'L0_attn_cq': _L0_attn_in['cq'], 'L0_attn_ck': _L0_attn_in['ck'], 'L0_attn_cv': _L0_attn_in['cv'], 'L0_attn_Wf1': _L0_attn_in['Wf1'], 'L0_attn_Wf2': _L0_attn_in['Wf2'], 'L0_attn_Wb': _L0_attn_in['Wb'], 'L0_attn_Wg1': _L0_attn_in['Wg1'], 'L0_attn_Wg2': _L0_attn_in['Wg2'], 'L0_attn_bg2': _L0_attn_in['bg2'], 'L0_attn_norm_w': _L0_attn_in['norm_w'], 'L0_attn_Wo': _L0_attn_in['Wo'], 'L0_xattn_Wi': _L0_xattn_in['Wi'], 'L0_xattn_bi': _L0_xattn_in['bi'], 'L0_xattn_Wf': _L0_xattn_in['Wf'], 'L0_xattn_bf': _L0_xattn_in['bf'], 'L0_xattn_ln_scale': _L0_xattn_in['ln_scale'], 'L0_ffn_w_ln1': _L0_ffn_in['w_ln1'], 'L0_ffn_wq': _L0_ffn_in['wq'], 'L0_ffn_bq': _L0_ffn_in['bq'], 'L0_ffn_wk': _L0_ffn_in['wk'], 'L0_ffn_bk': _L0_ffn_in['bk'], 'L0_ffn_wv': _L0_ffn_in['wv'], 'L0_ffn_bv': _L0_ffn_in['bv'], 'L0_ffn_wo': _L0_ffn_in['wo'], 'L0_ffn_w_ln2': _L0_ffn_in['w_ln2'], 'L0_ffn_w_router': _L0_ffn_in['w_router'], 'L0_ffn_w_gate_e': _L0_ffn_in['w_gate_e'], 'L0_ffn_w_up_e': _L0_ffn_in['w_up_e'], 'L0_ffn_w_down_e': _L0_ffn_in['w_down_e'], 'L0_ffn_w_sh_gate': _L0_ffn_in['w_sh_gate'], 'L0_ffn_w_sh_up': _L0_ffn_in['w_sh_up'], 'L0_ffn_w_sh_down': _L0_ffn_in['w_sh_down'], 'L0_ffn_w_sh_eg': _L0_ffn_in['w_sh_eg'], 'L1_attn_w_q': _L1_attn_in['w_q'], 'L1_attn_w_k': _L1_attn_in['w_k'], 'L1_attn_w_v': _L1_attn_in['w_v'], 'L1_attn_w_o': _L1_attn_in['w_o'], 'L1_attn_gate': _L1_attn_in['gate'], 'L1_attn_memories': _L1_attn_in['memories'], 'L1_attn_memory_norms': _L1_attn_in['memory_norms'], 'L1_xattn_Wq': _L1_xattn_in['Wq'], 'L1_xattn_Wk': _L1_xattn_in['Wk'], 'L1_xattn_Wv': _L1_xattn_in['Wv'], 'L1_xattn_Wo': _L1_xattn_in['Wo'], 'L1_ffn_gate_weight': _L1_ffn_in['gate_weight'], 'L1_ffn_w_gate': _L1_ffn_in['w_gate'], 'L1_ffn_w_up': _L1_ffn_in['w_up'], 'L1_ffn_w_down': _L1_ffn_in['w_down'], 'L1_ffn_sw_gate': _L1_ffn_in['sw_gate'], 'L1_ffn_sw_up': _L1_ffn_in['sw_up'], 'L1_ffn_sw_down': _L1_ffn_in['sw_down']}

def reference(x, ctx_2048, mask_BxS2_bf1, L0_attn_Wq, L0_attn_Wk, L0_attn_Wv, L0_attn_Ww, L0_attn_cq, L0_attn_ck, L0_attn_cv, L0_attn_Wf1, L0_attn_Wf2, L0_attn_Wb, L0_attn_Wg1, L0_attn_Wg2, L0_attn_bg2, L0_attn_norm_w, L0_attn_Wo, L0_xattn_Wi, L0_xattn_bi, L0_xattn_Wf, L0_xattn_bf, L0_xattn_ln_scale, L0_ffn_w_ln1, L0_ffn_wq, L0_ffn_bq, L0_ffn_wk, L0_ffn_bk, L0_ffn_wv, L0_ffn_bv, L0_ffn_wo, L0_ffn_w_ln2, L0_ffn_w_router, L0_ffn_w_gate_e, L0_ffn_w_up_e, L0_ffn_w_down_e, L0_ffn_w_sh_gate, L0_ffn_w_sh_up, L0_ffn_w_sh_down, L0_ffn_w_sh_eg, L1_attn_w_q, L1_attn_w_k, L1_attn_w_v, L1_attn_w_o, L1_attn_gate, L1_attn_memories, L1_attn_memory_norms, L1_xattn_Wq, L1_xattn_Wk, L1_xattn_Wv, L1_xattn_Wo, L1_ffn_gate_weight, L1_ffn_w_gate, L1_ffn_w_up, L1_ffn_w_down, L1_ffn_sw_gate, L1_ffn_sw_up, L1_ffn_sw_down):
    import jax
    import jax.numpy as jnp

    def _L0_attn_ref(hidden_states, Wq, Wk, Wv, Ww, cq, ck, cv, Wf1, Wf2, Wb, Wg1, Wg2, bg2, norm_w, Wo):
        import jax, jax.numpy as jnp
        import numpy as np
        B, T, HID = (1, 128, 256)
        H, DK, DV, M, KW = (16, 128, 128, 128, 4)
        SCALE = DK ** (-0.5)
        EPS = 1e-05

        def short_conv(x, w):
            K = w.shape[1]
            xp = jnp.pad(x, ((0, 0), (K - 1, 0), (0, 0)))
            t = x.shape[1]
            y = sum((xp[:, i:i + t] * w[:, i] for i in range(K)))
            return jax.nn.silu(y)

        def l2norm(x):
            return x * jax.lax.rsqrt(jnp.sum(x * x, axis=-1, keepdims=True) + 1e-06)

        def gsa2_scan(q, k, v, w, g, beta):
            b = q.shape[0]
            tm = lambda x: jnp.moveaxis(x, 1, 0)
            Sk0 = jnp.zeros((b, H, DK, M), q.dtype)
            Sv0 = jnp.zeros((b, H, M, DV), q.dtype)

            def step(carry, xs):
                Sk, Sv = carry
                q_t, k_t, v_t, w_t, g_t, b_t = xs
                gt = jnp.exp(g_t)
                bw = b_t[:, :, None] * w_t
                Sk = Sk * gt[:, :, None, :] + k_t[..., :, None] * bw[:, :, None, :]
                Sv = Sv * gt[..., None] + bw[..., None] * v_t[:, :, None, :]
                s = jnp.einsum('bhd,bhdm->bhm', q_t, Sk) * SCALE
                a = jax.nn.softmax(s, axis=-1)
                o_t = jnp.einsum('bhm,bhmd->bhd', a, Sv)
                return ((Sk, Sv), o_t)
            (_, _), o = jax.lax.scan(step, (Sk0, Sv0), (tm(q), tm(k), tm(v), tm(w), tm(g), tm(beta)))
            return jnp.moveaxis(o, 0, 1)
        h = hidden_states
        q = short_conv(h @ Wq, cq)
        k = short_conv(h @ Wk, ck)
        v = short_conv(h @ Wv, cv)
        w = short_conv(h @ Ww, cv)
        g = jax.nn.log_sigmoid(h @ Wf1 @ Wf2)
        beta = jax.nn.sigmoid(h @ Wb)
        rs = lambda x, d: x.reshape(x.shape[0], x.shape[1], -1, d)
        q, k = (rs(q, DK), rs(k, DK))
        v = rs(v, DV)
        w = l2norm(rs(w, M))
        g = rs(g, M)
        o = gsa2_scan(q, k, v, w, g, beta)
        gate = rs(h @ Wg1 @ Wg2 + bg2, DV)
        o = o * jax.lax.rsqrt(jnp.mean(o * o, axis=-1, keepdims=True) + EPS)
        o = o * norm_w * jax.nn.sigmoid(gate)
        o = o.reshape(o.shape[0], o.shape[1], -1)
        return o @ Wo

    def _L0_xattn_ref(q, k, v, Wi, bi, Wf, bf, ln_scale):
        import jax, jax.numpy as jnp
        import numpy as np
        B, S, E, NH = (2, 128, 256, 16)
        DH = E // NH
        EPS = 1e-06

        def _mlstm_forward(q, k, v, Wi, bi, Wf, bf, ln_scale):
            b, s, e = q.shape
            nh = Wi.shape[1]
            dh = e // nh
            x = jnp.concatenate([q, k, v], axis=-1)
            ig = (x @ Wi + bi).transpose(0, 2, 1)[..., None]
            fg = (x @ Wf + bf).transpose(0, 2, 1)[..., None]
            split = lambda t: t.reshape(b, s, nh, dh).transpose(0, 2, 1, 3)
            qh, kh, vh = (split(q), split(k), split(v))
            log_f = jax.nn.log_sigmoid(fg)
            log_f_cum = jnp.concatenate([jnp.zeros((b, nh, 1, 1), q.dtype), jnp.cumsum(log_f, axis=2)], axis=2)
            fg_mat = log_f_cum - jnp.transpose(log_f_cum, (0, 1, 3, 2))
            ltr = jnp.tril(jnp.ones((s, s), dtype=bool))
            log_fg = jnp.where(ltr, fg_mat[:, :, 1:, 1:], -jnp.inf)
            log_D = log_fg + jnp.transpose(ig, (0, 1, 3, 2))
            max_log_D = jnp.max(log_D, axis=-1, keepdims=True)
            D = jnp.exp(log_D - max_log_D)
            qk = jnp.einsum('bhsd,bhtd->bhst', qh, kh) / jnp.sqrt(jnp.asarray(dh, q.dtype))
            C = qk * D
            normalizer = jnp.maximum(jnp.abs(C.sum(-1, keepdims=True)), jnp.exp(-max_log_D))
            Cn = C / (normalizer + EPS)
            h = jnp.einsum('bhst,bhtd->bhsd', Cn, vh)
            mu = h.mean(-1, keepdims=True)
            var = ((h - mu) ** 2).mean(-1, keepdims=True)
            hn = (h - mu) * jax.lax.rsqrt(var + EPS)
            hn = hn * ln_scale.reshape(1, nh, 1, dh)
            return hn.transpose(0, 2, 1, 3).reshape(b, s, e)
        return _mlstm_forward(q, k, v, Wi, bi, Wf, bf, ln_scale)

    def _L0_ffn_ref(x, w_ln1, wq, bq, wk, bk, wv, bv, wo, w_ln2, w_router, w_gate_e, w_up_e, w_down_e, w_sh_gate, w_sh_up, w_sh_down, w_sh_eg):
        import jax, jax.numpy as jnp
        import numpy as np
        HID = 256
        N_HEADS = 16
        N_KV = 16
        HEAD_DIM = HID // N_HEADS
        N_EXP = 8
        TOP_K = 2
        MOE_I = 176
        SH_I = 704
        EPS = 1e-06
        ROPE_THETA = 1000000.0

        def _rms(x, w):
            v = jnp.mean(jnp.square(x), axis=-1, keepdims=True)
            return x * jax.lax.rsqrt(v + EPS) * w

        def _rope(q, k):
            S, D = (q.shape[1], q.shape[-1])
            inv = 1.0 / ROPE_THETA ** (jnp.arange(0, D, 2, dtype=jnp.float32) / D)
            freqs = jnp.arange(S, dtype=jnp.float32)[:, None] * inv[None, :]
            emb = jnp.concatenate([freqs, freqs], axis=-1)
            cos = jnp.cos(emb)[None, :, None, :]
            sin = jnp.sin(emb)[None, :, None, :]

            def rot(t):
                t1, t2 = (t[..., :D // 2], t[..., D // 2:])
                return jnp.concatenate([-t2, t1], axis=-1)
            return (q * cos + rot(q) * sin, k * cos + rot(k) * sin)
        B, S, H = x.shape
        h = _rms(x, w_ln1)
        q = (h @ wq + bq).reshape(B, S, N_HEADS, HEAD_DIM)
        k = (h @ wk + bk).reshape(B, S, N_KV, HEAD_DIM)
        v = (h @ wv + bv).reshape(B, S, N_KV, HEAD_DIM)
        q, k = _rope(q, k)
        rep = N_HEADS // N_KV
        if rep > 1:
            k = jnp.repeat(k, rep, axis=2)
            v = jnp.repeat(v, rep, axis=2)
        scores = jnp.einsum('bqhd,bkhd->bhqk', q, k) * HEAD_DIM ** (-0.5)
        causal = jnp.tril(jnp.ones((S, S), bool))
        scores = jnp.where(causal[None, None], scores, jnp.finfo(scores.dtype).min)
        attn = jax.nn.softmax(scores, axis=-1)
        ctx = jnp.einsum('bhqk,bkhd->bqhd', attn, v).reshape(B, S, N_HEADS * HEAD_DIM)
        x = x + ctx @ wo
        h = _rms(x, w_ln2).reshape(B * S, H)
        logits = h @ w_router
        probs = jax.nn.softmax(logits, axis=-1)
        top_w, top_i = jax.lax.top_k(probs, TOP_K)
        combine = jnp.sum(jax.nn.one_hot(top_i, N_EXP, dtype=h.dtype) * top_w[..., None], axis=1)
        g = jnp.einsum('th,ehi->eti', h, w_gate_e)
        u = jnp.einsum('th,ehi->eti', h, w_up_e)
        y = jnp.einsum('eti,eih->eth', jax.nn.silu(g) * u, w_down_e)
        routed = jnp.einsum('eth,te->th', y, combine)
        sh = jax.nn.silu(h @ w_sh_gate) * (h @ w_sh_up) @ w_sh_down
        sh = sh * jax.nn.sigmoid(h @ w_sh_eg)
        x = x + (routed + sh).reshape(B, S, H)
        return x

    def _L1_attn_ref(x, w_q, w_k, w_v, w_o, gate, memories, memory_norms):
        import jax, jax.numpy as jnp
        import numpy as np
        NUM_HEADS = 16
        EPS = 1e-06

        def elu_plus_one(x):
            return jax.nn.elu(x) + 1.0

        def _retrieve(q, memories, memory_norms):
            sigma_q = elu_plus_one(q)
            a_mem = jnp.einsum('bsd,mde->mbse', sigma_q, memories)
            raw = jnp.einsum('bsd,md->mbs', sigma_q, memory_norms)
            per_mem = a_mem / jnp.clip(raw, EPS, None)[..., None]
            rel = raw.mean(axis=-1)
            w = jax.nn.softmax(rel, axis=0)
            return jnp.einsum('mbse,mb->bse', per_mem, w)

        def _local_causal_attention(q, k, v):
            B, S, D = q.shape
            hd = D // NUM_HEADS
            qh = q.reshape(B, S, NUM_HEADS, hd).transpose(0, 2, 1, 3)
            kh = k.reshape(B, S, NUM_HEADS, hd).transpose(0, 2, 1, 3)
            vh = v.reshape(B, S, NUM_HEADS, hd).transpose(0, 2, 1, 3)
            scores = jnp.einsum('bhqd,bhkd->bhqk', qh, kh) * hd ** (-0.5)
            causal = jnp.tril(jnp.ones((S, S), dtype=bool))
            scores = jnp.where(causal, scores, jnp.float32(-1000000000.0))
            attn = jax.nn.softmax(scores, axis=-1)
            out = jnp.einsum('bhqk,bhkd->bhqd', attn, vh)
            return out.transpose(0, 2, 1, 3).reshape(B, S, D)
        q = x @ w_q.T
        k = x @ w_k.T
        v = x @ w_v.T
        mem_out = _retrieve(q, memories, memory_norms)
        local_out = _local_causal_attention(q, k, v)
        g = jax.nn.sigmoid(gate)
        out = g * mem_out + (1.0 - g) * local_out
        return out @ w_o.T

    def _L1_xattn_ref(query, key, value, mask, Wq, Wk, Wv, Wo):
        import jax, jax.numpy as jnp
        import numpy as np
        import math
        D_MODEL = 256
        N_Q_HEADS = 16
        N_KV_HEADS = 4
        HEAD_DIM = D_MODEL // N_Q_HEADS
        B = 4
        S = 128

        def _alibi_slopes(num_heads):
            n = 2 ** int(math.floor(math.log2(num_heads)))
            m0 = 2.0 ** (-8.0 / n)
            return m0 ** jnp.arange(1, n + 1, dtype=jnp.float32)
        b, q_len, d = query.shape
        kv_len = key.shape[1]
        G = N_KV_HEADS
        Hpg = N_Q_HEADS // G
        dh = HEAD_DIM
        Q = (query @ Wq).reshape(b, q_len, G, Hpg, dh)
        K = (key @ Wk).reshape(b, kv_len, G, dh)
        V = (value @ Wv).reshape(b, kv_len, G, dh)
        Q = Q / math.sqrt(dh)
        scores = jnp.einsum('bqghd,bkgd->bghqk', Q, K)
        rel = jnp.arange(kv_len, dtype=jnp.float32)[None, :] - jnp.arange(q_len, dtype=jnp.float32)[:, None]
        m = _alibi_slopes(N_Q_HEADS).reshape(1, G, Hpg, 1, 1)
        scores = scores + m * rel[None, None, None]
        neg = jnp.finfo(scores.dtype).min
        scores = jnp.where(mask[:, None, None, None, :], scores, neg)
        w = jax.nn.softmax(scores, axis=-1)
        out = jnp.einsum('bghqk,bkgd->bqghd', w, V)
        out = out.reshape(b, q_len, G * Hpg * dh)
        return out @ Wo

    def _L1_ffn_ref(hidden_states, gate_weight, w_gate, w_up, w_down, sw_gate, sw_up, sw_down):
        import jax, jax.numpy as jnp
        import numpy as np
        B, S, H = (2, 128, 256)
        E, K, F = (8, 2, 176)
        N_SHARED = 2
        FS = F * N_SHARED
        ROUTED_SCALE = 1.0

        def _swiglu_mlp(x, wg, wu, wd):
            return jax.nn.silu(x @ wg.T) * (x @ wu.T) @ wd.T
        b, s, h = hidden_states.shape
        x = hidden_states.reshape(-1, h)
        T = x.shape[0]
        logits = x.astype(jnp.float32) @ gate_weight.astype(jnp.float32).T
        scores = jax.nn.softmax(logits, axis=-1)
        topk_w, topk_idx = jax.lax.top_k(scores, K)
        topk_w = topk_w / (jnp.sum(topk_w, axis=-1, keepdims=True) + 1e-20)
        topk_w = topk_w * ROUTED_SCALE
        cw = jnp.zeros((T, E), jnp.float32).at[jnp.arange(T)[:, None], topk_idx].add(topk_w)
        g = jax.nn.silu(jnp.einsum('th,efh->tef', x, w_gate)) * jnp.einsum('th,efh->tef', x, w_up)
        expert_out = jnp.einsum('tef,ehf->teh', g, w_down)
        y = jnp.einsum('te,teh->th', cw, expert_out).reshape(b, s, h)
        y = y + _swiglu_mlp(x, sw_gate, sw_up, sw_down).reshape(b, s, h)
        return y
    x = x + _L0_attn_ref(_layernorm(x, axis=-1), L0_attn_Wq, L0_attn_Wk, L0_attn_Wv, L0_attn_Ww, L0_attn_cq, L0_attn_ck, L0_attn_cv, L0_attn_Wf1, L0_attn_Wf2, L0_attn_Wb, L0_attn_Wg1, L0_attn_Wg2, L0_attn_bg2, L0_attn_norm_w, L0_attn_Wo)
    x = x + _L0_xattn_ref(_layernorm(x, axis=-1), ctx_2048, ctx_2048, L0_xattn_Wi, L0_xattn_bi, L0_xattn_Wf, L0_xattn_bf, L0_xattn_ln_scale)
    x = x + _L0_ffn_ref(_layernorm(x, axis=-1), L0_ffn_w_ln1, L0_ffn_wq, L0_ffn_bq, L0_ffn_wk, L0_ffn_bk, L0_ffn_wv, L0_ffn_bv, L0_ffn_wo, L0_ffn_w_ln2, L0_ffn_w_router, L0_ffn_w_gate_e, L0_ffn_w_up_e, L0_ffn_w_down_e, L0_ffn_w_sh_gate, L0_ffn_w_sh_up, L0_ffn_w_sh_down, L0_ffn_w_sh_eg)
    x = x + _L1_attn_ref(_layernorm(x, axis=-1), L1_attn_w_q, L1_attn_w_k, L1_attn_w_v, L1_attn_w_o, L1_attn_gate, L1_attn_memories, L1_attn_memory_norms)
    x = x + _L1_xattn_ref(_layernorm(x, axis=-1), ctx_2048, ctx_2048, mask_BxS2_bf1, L1_xattn_Wq, L1_xattn_Wk, L1_xattn_Wv, L1_xattn_Wo)
    x = x + _L1_ffn_ref(_layernorm(x, axis=-1), L1_ffn_gate_weight, L1_ffn_w_gate, L1_ffn_w_up, L1_ffn_w_down, L1_ffn_sw_gate, L1_ffn_sw_up, L1_ffn_sw_down)
    return x

_drawn_inputs = setup_inputs


def setup_inputs(seed=0):
    import zlib

    import numpy as np

    out = dict(_drawn_inputs(seed))
    spreads = {'L0_attn_bg2': (0.0, 0.8),
     'L0_attn_norm_w': (1.0, 0.6),
     'L0_xattn_ln_scale': (1.0, 0.2),
     'L0_ffn_w_ln1': (1.0, 0.6),
     'L0_ffn_bq': (0.0, 0.8),
     'L0_ffn_bk': (0.0, 0.8),
     'L0_ffn_bv': (0.0, 0.478),
     'L0_ffn_w_ln2': (1.0, 0.6)}
    factors = {'L0_attn_Wq': 8.0,
     'L0_attn_Wk': 8.0,
     'L0_attn_cq': 8.0,
     'L0_attn_ck': 8.0,
     'L0_attn_Wf1': 8.0,
     'L0_attn_Wf2': 8.0,
     'L0_attn_Wb': 4.524,
     'L0_attn_Wg1': 8.0,
     'L0_attn_Wg2': 8.0,
     'L0_xattn_bi': 30.024,
     'L0_xattn_Wf': 3.291,
     'L0_ffn_wq': 8.0,
     'L0_ffn_wk': 8.0,
     'L0_ffn_wv': 4.132,
     'L0_ffn_wo': 2.856,
     'L0_ffn_w_router': 8.0,
     'L0_ffn_w_gate_e': 8.0,
     'L0_ffn_w_up_e': 8.0,
     'L0_ffn_w_down_e': 8.0,
     'L0_ffn_w_sh_gate': 6.192,
     'L0_ffn_w_sh_up': 6.34,
     'L0_ffn_w_sh_down': 5.719,
     'L0_ffn_w_sh_eg': 8.0,
     'L1_attn_w_q': 8.0,
     'L1_attn_w_k': 8.0,
     'L1_attn_w_v': 6.773,
     'L1_attn_w_o': 6.362,
     'L1_attn_memories': 64.0,
     'L1_attn_memory_norms': 64.0,
     'L1_xattn_Wq': 3.103,
     'L1_xattn_Wk': 3.076,
     'L1_ffn_gate_weight': 3.186,
     'L1_ffn_w_gate': 2.975,
     'L1_ffn_w_up': 2.781,
     'L1_ffn_w_down': 2.778}
    for name, (base, spread) in spreads.items():
        noise = np.random.default_rng([zlib.crc32(name.encode()), seed]).standard_normal(out[name].shape)
        drawn = base * np.exp(spread * noise) if base else spread * noise
        out[name] = jnp.asarray(drawn.astype(out[name].dtype))
    for name, factor in factors.items():
        out[name] = (out[name] * factor).astype(out[name].dtype)
    return out
```

```python
import concourse.bass as bass
import numpy as np
from concourse import mybir
from contextlib import ExitStack

F32 = mybir.dt.float32
I32 = mybir.dt.int32
ALU = mybir.AluOpType
ACT = mybir.ActivationFunctionType
AX = mybir.AxisListType


def prep(nc, io, X, PS, IDENT, shared):
    ctx = ExitStack()
    with ctx:
        def sb(name, shape, dt=F32):
            return ctx.enter_context(nc.sbuf_tensor("prep_" + name, shape, dt))

        signals = []

        def signal(name):
            signals.append(nc.alloc_semaphore(name))
            return signals[-1]

        stats = sb("stats", [128, 6])
        mv = sb("mv", [128, 2])
        vare = sb("vare", [128, 1])
        rstd = sb("rstd", [128, 1])
        xn = sb("xn", [128, 256])
        XT, F1T, G1T, BETA = shared
        WF1 = sb("wf1", [128, 2, 128])
        WG1 = sb("wg1", [128, 2, 128])
        WB = sb("wb", [128, 2, 16])
        xTf = sb("xTf", [128, 2, 128])
        eb = sb("eb", [128, 16])
        eb1 = sb("eb1", [128, 16])
        PS0, PS1, PS2, PS3 = PS[0:4]
        NEGHALF = sb("neghalf", [128, 4])

        prep_setup_by_pool = signal("prep_setup_by_pool")
        prep_setup_loads_sp = signal("prep_setup_loads_sp")
        prep_norm_by_dve = signal("prep_norm_by_dve")
        prep_rstd_by_pool = signal("prep_rstd_by_pool")
        prep_normed_by_dve = signal("prep_normed_by_dve")
        prep_turn_by_pe = signal("prep_turn_by_pe")
        prep_turn_by_act = signal("prep_turn_by_act")
        prep_lowrank_by_pe = signal("prep_lowrank_by_pe")
        prep_expb_by_act = signal("prep_expb_by_act")
        prep_beta_by_dve = signal("prep_beta_by_dve")
        prep_pool_passed = signal("prep_pool_passed")
        prep_dve_passed = signal("prep_dve_passed")
        with nc.Block() as block:

            @block.tensor
            def _(pe):
                pe.wait_ge(prep_setup_by_pool, 1)
                pe.wait_ge(prep_setup_loads_sp, 48)
                with pe.Fori(0, 32) as i:
                    n = i
                    pe.wait_ge(prep_normed_by_dve, n * 1 + 1)
                    for c in range(2):
                        last = nc.tensor.transpose(PS0[:, c * 128:(c + 1) * 128], xn[:, c * 128:(c + 1) * 128], IDENT[:, :])
                    last.then_inc(prep_turn_by_pe, 1)
                    pe.wait_ge(prep_turn_by_act, n * 1 + 1)
                    for c in range(2):
                        nc.tensor.matmul(PS1[:, 0:16], xTf[:, c, :], WB[:, c, :], start=(c == 0), stop=(c == 1))
                    for c in range(2):
                        nc.tensor.matmul(PS2[:, 0:128], WF1[:, c, :], xTf[:, c, :], start=(c == 0), stop=(c == 1))
                    for c in range(2):
                        last = nc.tensor.matmul(PS3[:, 0:128], WG1[:, c, :], xTf[:, c, :], start=(c == 0), stop=(c == 1))
                    last.then_inc(prep_lowrank_by_pe, 1)

            @block.vector
            def _(dve):
                dve.wait_ge(prep_setup_by_pool, 1)
                dve.wait_ge(prep_setup_loads_sp, 48)
                with dve.Fori(0, 32) as i:
                    n = i
                    nc.vector.bn_stats(stats[:, :], X[:, bass.ds(n * 256, 256)]).then_inc(prep_norm_by_dve, 1)
                    dve.wait_ge(prep_norm_by_dve, n * 2 + 1)
                    dve.sem_inc(prep_dve_passed, 1)
                    nc.vector.bn_aggr(mv[:, :], stats[:, :]).then_inc(prep_norm_by_dve, 1)
                    dve.wait_ge(prep_rstd_by_pool, n * 2 + 2)
                    nc.vector.tensor_scalar(xn[:, :], X[:, bass.ds(n * 256, 256)], mv[:, 0:1], rstd[:, 0:1], ALU.subtract, ALU.mult).then_inc(prep_normed_by_dve, 1)
                    dve.wait_ge(prep_turn_by_act, n * 1 + 1)
                    nc.vector.tensor_copy(XT[:, :, bass.ds(n * 128, 128)], xTf[:, :, :])
                    dve.wait_ge(prep_expb_by_act, n * 1 + 1)
                    nc.vector.tensor_scalar(eb1[:, :], eb[:, :], 1.0, None, ALU.add).then_inc(prep_beta_by_dve, 1)
                    dve.wait_ge(prep_beta_by_dve, n * 1 + 1)
                    nc.vector.reciprocal(BETA[:, :, bass.ds(n, 1)].rearrange("p h i -> p (h i)"), eb1[:, :])

            @block.scalar
            def _(act):
                act.wait_ge(prep_setup_by_pool, 1)
                act.wait_ge(prep_setup_loads_sp, 48)
                with act.Fori(0, 32) as i:
                    n = i
                    act.wait_ge(prep_turn_by_pe, n * 1 + 1)
                    nc.scalar.activation(xTf[:, :, :].rearrange("p c t -> p (c t)"), PS0[:, 0:256], ACT.Copy).then_inc(prep_turn_by_act, 1)
                    act.wait_ge(prep_lowrank_by_pe, n * 1 + 1)
                    nc.scalar.activation(F1T[:, bass.ds(n * 128, 128)], PS2[:, 0:128], ACT.Copy)
                    nc.scalar.activation(G1T[:, bass.ds(n * 128, 128)], PS3[:, 0:128], ACT.Copy)
                    nc.scalar.activation(eb[:, :], PS1[:, 0:16], ACT.Exp, scale=-1.0).then_inc(prep_expb_by_act, 1)

            @block.gpsimd
            def _(pool):
                nc.gpsimd.memset(NEGHALF[:, :], -0.5).then_inc(prep_setup_by_pool, 1)
                pool.wait_ge(prep_setup_by_pool, 1)
                pool.wait_ge(prep_setup_loads_sp, 48)
                with pool.Fori(0, 32) as i:
                    n = i
                    pool.wait_ge(prep_norm_by_dve, n * 2 + 2)
                    pool.sem_inc(prep_pool_passed, 1)
                    nc.gpsimd.tensor_scalar(vare[:, :], mv[:, 1:2], 1e-5, None, ALU.add).then_inc(prep_rstd_by_pool, 1)
                    pool.wait_ge(prep_rstd_by_pool, n * 2 + 1)
                    nc.gpsimd.tensor_tensor(rstd[:, :], vare[:, :], NEGHALF[:, 0:1], ALU.pow).then_inc(prep_rstd_by_pool, 1)

            @block.sync
            def _(sp):
                nc.sync.dma_start(WF1[:, :, :], io["wf1"]).then_inc(prep_setup_loads_sp, 16)
                nc.sync.dma_start(WG1[:, :, :], io["wg1"]).then_inc(prep_setup_loads_sp, 16)
                nc.sync.dma_start(WB[:, :, :], io["wb"]).then_inc(prep_setup_loads_sp, 16)

        nc.clear_and_free_semaphores(signals)
        nc.all_engine_barrier()

def gsa(nc, io, X, PS, IDENT, shared):
    ctx = ExitStack()
    with ctx:
        def sb(name, shape, dt=F32):
            return ctx.enter_context(nc.sbuf_tensor("gsa_" + name, shape, dt))

        signals = []

        def signal(name):
            signals.append(nc.alloc_semaphore(name))
            return signals[-1]

        XT, F1T, G1T, BETA = shared
        WA = sb("wa", [128, 2, 512])
        WFG = sb("wfg", [128, 256])
        WCV = sb("wcv", [128, 12])
        WO = sb("wo", [128, 256])
        BG = sb("bg", [128, 16])
        NW = sb("nw", [128, 1])
        MASKS = sb("masks", [128, 6, 256])
        EYES = sb("eyes", [128, 512])
        ones = sb("ones", [128, 1])
        NEGHALF = sb("neghalf", [128, 4])
        BETA2 = BETA[:, :, :].rearrange("p h i -> p (h i)")
        qTa = sb("qTa", [128, 512])
        kTa = sb("kTa", [128, 512])
        vTa = sb("vTa", [128, 512])
        wTa = sb("wTa", [128, 512])
        sga = sb("sga", [128, 512])
        oga = sb("oga", [128, 512])
        prea = sb("prea", [128, 512])
        Ra = sb("Ra", [128, 5, 256])
        LBa = sb("lba", [128, 5, 512])
        LTa = sb("lta", [128, 2, 512])
        caa = sb("caa", [128, 512])
        ADa = sb("ada", [128, 512])
        AMa = sb("ama", [128, 6, 256])
        tmpa = sb("tmpa", [128, 2, 256])
        Sa, aTa, Va, PTa, aa, aRa = qTa, kTa, vTa, ADa, caa, AMa
        ssa = sb("ssa", [128, 4])
        c4a = sb("c4a", [128, 4])
        mxa = sb("mxa", [128, 4])
        nmxa = sb("nmxa", [128, 4])
        dena = sb("dena", [128, 4])
        den2a = sb("den2a", [128, 4])
        r0a = sb("r0a", [128, 4])
        r4a = sb("r4a", [128, 4])
        qTb = sb("qTb", [128, 512])
        kTb = sb("kTb", [128, 512])
        vTb = sb("vTb", [128, 512])
        wTb = sb("wTb", [128, 512])
        sgb = sb("sgb", [128, 512])
        ogb = sb("ogb", [128, 512])
        preb = sb("preb", [128, 512])
        Rb = sb("Rb", [128, 5, 256])
        LBb = sb("lbb", [128, 5, 512])
        LTb = sb("ltb", [128, 2, 512])
        cab = sb("cab", [128, 512])
        ADb = sb("adb", [128, 512])
        AMb = sb("amb", [128, 6, 256])
        tmpb = sb("tmpb", [128, 2, 256])
        Sb, aTb, Vb, PTb, ab, aRb = qTb, kTb, vTb, ADb, cab, AMb
        ssb = sb("ssb", [128, 4])
        c4b = sb("c4b", [128, 4])
        mxb = sb("mxb", [128, 4])
        nmxb = sb("nmxb", [128, 4])
        denb = sb("denb", [128, 4])
        den2b = sb("den2b", [128, 4])
        r0b = sb("r0b", [128, 4])
        r4b = sb("r4b", [128, 4])
        SCALE = 128 ** -0.5

        def pairs(t, b):
            return t.rearrange("p (n r b) -> p n r b", r=2, b=b)

        def right(t, b):
            return pairs(t, b)[:, :, 1, :]

        def left(t, b):
            return pairs(t, b)[:, :, 0, :]

        def packed(t, b):
            return t.rearrange("p (n b) -> p n b", b=b)

        def lastof(t, b, side):
            return pairs(t, b)[:, :, side, b - 1:b].to_broadcast([128, 256 // b, b])

        def tile(t, j):
            return t[:, j * 128:(j + 1) * 128]

        def seqs(t):
            return t.rearrange("p (b t) -> p b t", t=64)

        gsa_setup_by_pool = signal("gsa_setup_by_pool")
        gsa_setup_loads_sp = signal("gsa_setup_loads_sp")
        gsa_proj_weights_dma = signal("gsa_proj_weights_dma")
        gsa_conv_weights_dma = signal("gsa_conv_weights_dma")
        gsa_gate_weights_dma = signal("gsa_gate_weights_dma")
        gsa_projected_by_pe = signal("gsa_projected_by_pe")
        gsa_out_weights_dma = signal("gsa_out_weights_dma")
        gsa_conv0_by_act = signal("gsa_conv0_by_act")
        gsa_conv_by_dve = signal("gsa_conv_by_dve")
        gsa_silu_by_act = signal("gsa_silu_by_act")
        gsa_square_by_act = signal("gsa_square_by_act")
        gsa_wnorm_by_pe = signal("gsa_wnorm_by_pe")
        gsa_forget_by_pe = signal("gsa_forget_by_pe")
        gsa_sigmoid_by_act = signal("gsa_sigmoid_by_act")
        gsa_kept_by_act = signal("gsa_kept_by_act")
        gsa_wnorm_by_dve = signal("gsa_wnorm_by_dve")
        gsa_wnorm_by_pool = signal("gsa_wnorm_by_pool")
        gsa_decay_by_dve = signal("gsa_decay_by_dve")
        gsa_strength_by_pool = signal("gsa_strength_by_pool")
        gsa_keyquery_by_act = signal("gsa_keyquery_by_act")
        gsa_keyquery_by_pe = signal("gsa_keyquery_by_pe")
        gsa_values_by_pe = signal("gsa_values_by_pe")
        gsa_masked_by_pool = signal("gsa_masked_by_pool")
        gsa_turned_by_pe = signal("gsa_turned_by_pe")
        gsa_turned_by_act = signal("gsa_turned_by_act")
        gsa_values_by_act = signal("gsa_values_by_act")
        gsa_slots_by_pe = signal("gsa_slots_by_pe")
        gsa_decay_by_act = signal("gsa_decay_by_act")
        gsa_slots_by_act = signal("gsa_slots_by_act")
        gsa_level_by_dve = signal("gsa_level_by_dve")
        gsa_softmax_by_pe = signal("gsa_softmax_by_pe")
        gsa_softmax_by_dve = signal("gsa_softmax_by_dve")
        gsa_softmax_by_act = signal("gsa_softmax_by_act")
        gsa_onorm_by_pool = signal("gsa_onorm_by_pool")
        gsa_reach_by_pool = signal("gsa_reach_by_pool")
        gsa_weights_by_pe = signal("gsa_weights_by_pe")
        gsa_reach_by_dve = signal("gsa_reach_by_dve")
        gsa_weights_by_dve = signal("gsa_weights_by_dve")
        gsa_read_by_pe = signal("gsa_read_by_pe")
        gsa_osquare_by_act = signal("gsa_osquare_by_act")
        gsa_ogate_by_dve = signal("gsa_ogate_by_dve")
        gsa_onorm_by_pe = signal("gsa_onorm_by_pe")
        gsa_output_by_pe = signal("gsa_output_by_pe")
        gsa_onorm_by_dve = signal("gsa_onorm_by_dve")
        gsa_residual_by_dve = signal("gsa_residual_by_dve")
        gsa_dve_passed = signal("gsa_dve_passed")
        gsa_act_passed = signal("gsa_act_passed")
        with nc.Block() as block:

            @block.tensor
            def _(pe):
                pe.sem_inc(gsa_projected_by_pe, 8)
                pe.sem_inc(gsa_forget_by_pe, 3)
                pe.sem_inc(gsa_output_by_pe, 2)
                pe.wait_ge(gsa_setup_by_pool, 1)
                pe.wait_ge(gsa_setup_loads_sp, 64)
                with pe.Fori(0, 16) as h:
                    with pe.Fori(0, 4) as gp:
                        n = h * 4 + gp
                        pe.wait_ge(gsa_proj_weights_dma, n * 16 + 16)
                        pe.wait_ge(gsa_residual_by_dve, n * 2 + 1)
                        for c in range(2):
                            last = nc.tensor.matmul(PS[4][:, :], WA[:, c, 3 * 128:4 * 128], XT[:, c, bass.ds(gp * 1024 + 512, 512)], start=(c == 0), stop=(c == 1))
                        last.then_inc(gsa_projected_by_pe, 1)
                        for c in range(2):
                            last = nc.tensor.matmul(PS[7][:, :], WA[:, c, 2 * 128:3 * 128], XT[:, c, bass.ds(gp * 1024 + 512, 512)], start=(c == 0), stop=(c == 1))
                        last.then_inc(gsa_projected_by_pe, 1)
                        for c in range(2):
                            last = nc.tensor.matmul(PS[5][:, :], WA[:, c, 0 * 128:1 * 128], XT[:, c, bass.ds(gp * 1024 + 512, 512)], start=(c == 0), stop=(c == 1))
                        last.then_inc(gsa_projected_by_pe, 1)
                        pe.wait_ge(gsa_residual_by_dve, n * 2 + 2)
                        for c in range(2):
                            last = nc.tensor.matmul(PS[0][:, :], WA[:, c, 3 * 128:4 * 128], XT[:, c, bass.ds(gp * 1024 + 0, 512)], start=(c == 0), stop=(c == 1))
                        last.then_inc(gsa_projected_by_pe, 1)
                        for c in range(2):
                            last = nc.tensor.matmul(PS[6][:, :], WA[:, c, 1 * 128:2 * 128], XT[:, c, bass.ds(gp * 1024 + 512, 512)], start=(c == 0), stop=(c == 1))
                        last.then_inc(gsa_projected_by_pe, 1)
                        for c in range(2):
                            last = nc.tensor.matmul(PS[3][:, :], WA[:, c, 2 * 128:3 * 128], XT[:, c, bass.ds(gp * 1024 + 0, 512)], start=(c == 0), stop=(c == 1))
                        last.then_inc(gsa_projected_by_pe, 1)
                        for c in range(2):
                            last = nc.tensor.matmul(PS[2][:, :], WA[:, c, 1 * 128:2 * 128], XT[:, c, bass.ds(gp * 1024 + 0, 512)], start=(c == 0), stop=(c == 1))
                        last.then_inc(gsa_projected_by_pe, 1)
                        for c in range(2):
                            last = nc.tensor.matmul(PS[1][:, :], WA[:, c, 0 * 128:1 * 128], XT[:, c, bass.ds(gp * 1024 + 0, 512)], start=(c == 0), stop=(c == 1))
                        last.then_inc(gsa_projected_by_pe, 1)
                        pe.wait_ge(gsa_square_by_act, n * 1 + 1)
                        pe.wait_ge(gsa_conv_by_dve, n * 23 + 29)
                        for j in range(4):
                            last = nc.tensor.matmul(PS[7][:, j:j + 1], tile(cab, j), ones[:, 0:1], start=True, stop=True)
                        last.then_inc(gsa_wnorm_by_pe, 1)
                        pe.wait_ge(gsa_gate_weights_dma, n * 16 + 16)
                        last = nc.tensor.matmul(PS[4][:, :], WFG[:, 0:128], F1T[:, bass.ds(gp * 1024 + 512, 512)], start=True, stop=True)
                        last.then_inc(gsa_forget_by_pe, 1)
                        pe.wait_ge(gsa_silu_by_act, n * 4 + 3)
                        for j in range(4):
                            last = nc.tensor.matmul(tile(PS[6], j), tile(kTb, j), tile(qTb, j), start=True, stop=True)
                        pe.wait_ge(gsa_conv_by_dve, n * 23 + 41)
                        for j in range(4):
                            last = nc.tensor.matmul(PS[3][:, j:j + 1], tile(caa, j), ones[:, 0:1], start=True, stop=True)
                        last.then_inc(gsa_wnorm_by_pe, 1)
                        last = nc.tensor.matmul(PS[0][:, :], WFG[:, 0:128], F1T[:, bass.ds(gp * 1024 + 0, 512)], start=True, stop=True)
                        last.then_inc(gsa_forget_by_pe, 1)
                        last = nc.tensor.matmul(PS[5][:, :], WFG[:, 128:256], G1T[:, bass.ds(gp * 1024 + 512, 512)], start=True, stop=True)
                        pe.wait_ge(gsa_sigmoid_by_act, n * 4 + 1)
                        for j in range(4):
                            last = nc.tensor.transpose(tile(PS[4], j), tile(wTb, j), IDENT[:, :])
                        pe.wait_ge(gsa_silu_by_act, n * 4 + 4)
                        for j in range(4):
                            last = nc.tensor.matmul(tile(PS[2], j), tile(kTa, j), tile(qTa, j), start=True, stop=True)
                        last.then_inc(gsa_keyquery_by_pe, 1)
                        pe.wait_ge(gsa_wnorm_by_dve, n * 2 + 1)
                        for j in range(4):
                            last = nc.tensor.transpose(tile(PS[7], j), tile(vTb, j), IDENT[:, :])
                        last.then_inc(gsa_values_by_pe, 1)
                        last = nc.tensor.matmul(PS[1][:, :], WFG[:, 128:256], G1T[:, bass.ds(gp * 1024 + 0, 512)], start=True, stop=True)
                        last.then_inc(gsa_forget_by_pe, 1)
                        pe.wait_ge(gsa_sigmoid_by_act, n * 4 + 2)
                        for j in range(4):
                            last = nc.tensor.transpose(tile(PS[0], j), tile(wTa, j), IDENT[:, :])
                        last.then_inc(gsa_turned_by_pe, 1)
                        pe.wait_ge(gsa_wnorm_by_dve, n * 2 + 2)
                        for j in range(4):
                            last = nc.tensor.transpose(tile(PS[3], j), tile(vTa, j), IDENT[:, :])
                        last.then_inc(gsa_values_by_pe, 1)
                        pe.wait_ge(gsa_decay_by_dve, n * 16 + 1)
                        pe.wait_ge(gsa_sigmoid_by_act, n * 4 + 3)
                        for j in range(4):
                            last = nc.tensor.transpose(tile(PS[5], j), tile(LBb[:, 0, :], j), IDENT[:, :])
                        last.then_inc(gsa_turned_by_pe, 1)
                        pe.wait_ge(gsa_masked_by_pool, n * 13 + 1)
                        pe.wait_ge(gsa_turned_by_act, n * 10 + 1)
                        for j in range(4):
                            last = nc.tensor.matmul(tile(PS[6], j), tile(LTb[:, 0, :], j), tile(ADb, j), start=True, stop=True)
                        last.then_inc(gsa_slots_by_pe, 1)
                        pe.wait_ge(gsa_masked_by_pool, n * 13 + 2)
                        pe.wait_ge(gsa_values_by_act, n * 2 + 1)
                        for j in range(4):
                            last = nc.tensor.matmul(PS[7][:, j * 64:(j + 1) * 64], tile(LTb[:, 0, :], j), AMb[:, 0, j * 64:(j + 1) * 64], start=True, stop=True)
                        last.then_inc(gsa_slots_by_pe, 1)
                        pe.wait_ge(gsa_decay_by_dve, n * 16 + 3)
                        pe.wait_ge(gsa_sigmoid_by_act, n * 4 + 4)
                        for j in range(4):
                            last = nc.tensor.transpose(tile(PS[1], j), tile(LBa[:, 0, :], j), IDENT[:, :])
                        last.then_inc(gsa_turned_by_pe, 1)
                        pe.wait_ge(gsa_decay_by_act, n * 6 + 1)
                        for j in range(4):
                            last = nc.tensor.transpose(tile(PS[4], j), tile(LBb[:, 1, :], j), IDENT[:, :])
                        pe.wait_ge(gsa_masked_by_pool, n * 13 + 3)
                        pe.wait_ge(gsa_turned_by_act, n * 10 + 2)
                        for j in range(4):
                            last = nc.tensor.matmul(tile(PS[2], j), tile(LTa[:, 0, :], j), tile(ADa, j), start=True, stop=True)
                        last.then_inc(gsa_slots_by_pe, 1)
                        pe.wait_ge(gsa_decay_by_act, n * 6 + 2)
                        for j in range(4):
                            last = nc.tensor.transpose(tile(PS[0], j), tile(LBa[:, 1, :], j), IDENT[:, :])
                        pe.wait_ge(gsa_masked_by_pool, n * 13 + 4)
                        pe.wait_ge(gsa_values_by_act, n * 2 + 2)
                        for j in range(4):
                            last = nc.tensor.matmul(PS[3][:, j * 64:(j + 1) * 64], tile(LTa[:, 0, :], j), AMa[:, 0, j * 64:(j + 1) * 64], start=True, stop=True)
                        last.then_inc(gsa_slots_by_pe, 1)
                        pe.wait_ge(gsa_slots_by_act, n * 2 + 1)
                        for j in range(4):
                            last = nc.tensor.matmul(PS[6][:, j * 64:(j + 1) * 64], tile(LTb[:, 1, :], j), AMb[:, 1, j * 64:(j + 1) * 64], start=True, stop=True)
                        last.then_inc(gsa_slots_by_pe, 1)
                        pe.wait_ge(gsa_decay_by_dve, n * 16 + 6)
                        pe.wait_ge(gsa_decay_by_act, n * 6 + 3)
                        for j in range(4):
                            last = nc.tensor.transpose(tile(PS[5], j), tile(LBb[:, 2, :], j), IDENT[:, :])
                        last.then_inc(gsa_turned_by_pe, 1)
                        pe.wait_ge(gsa_decay_by_dve, n * 16 + 9)
                        pe.wait_ge(gsa_decay_by_act, n * 6 + 4)
                        for j in range(4):
                            last = nc.tensor.transpose(tile(PS[1], j), tile(LBa[:, 2, :], j), IDENT[:, :])
                        pe.wait_ge(gsa_masked_by_pool, n * 13 + 5)
                        pe.wait_ge(gsa_slots_by_act, n * 2 + 2)
                        for j in range(4):
                            last = nc.tensor.matmul(PS[2][:, j * 64:(j + 1) * 64], tile(LTa[:, 1, :], j), AMa[:, 1, j * 64:(j + 1) * 64], start=True, stop=True)
                        last.then_inc(gsa_slots_by_pe, 1)
                        pe.wait_ge(gsa_decay_by_dve, n * 16 + 10)
                        pe.wait_ge(gsa_turned_by_act, n * 10 + 3)
                        for j in range(4):
                            last = nc.tensor.transpose(tile(PS[4], j), tile(LBb[:, 3, :], j), IDENT[:, :])
                        pe.wait_ge(gsa_masked_by_pool, n * 13 + 6)
                        for j in range(4):
                            last = nc.tensor.matmul(PS[7][:, j * 64:(j + 1) * 64], tile(LTb[:, 0, :], j), AMb[:, 2, j * 64:(j + 1) * 64], start=True, stop=True)
                        last.then_inc(gsa_slots_by_pe, 1)
                        pe.wait_ge(gsa_masked_by_pool, n * 13 + 7)
                        pe.wait_ge(gsa_turned_by_act, n * 10 + 4)
                        for j in range(4):
                            last = nc.tensor.matmul(PS[6][:, j * 64:(j + 1) * 64], tile(LTb[:, 1, :], j), AMb[:, 3, j * 64:(j + 1) * 64], start=True, stop=True)
                        last.then_inc(gsa_slots_by_pe, 1)
                        pe.wait_ge(gsa_decay_by_dve, n * 16 + 14)
                        for j in range(4):
                            last = nc.tensor.transpose(tile(PS[5], j), tile(LBb[:, 4, :], j), IDENT[:, :])
                        last.then_inc(gsa_turned_by_pe, 1)
                        pe.wait_ge(gsa_masked_by_pool, n * 13 + 8)
                        pe.wait_ge(gsa_turned_by_act, n * 10 + 5)
                        for j in range(4):
                            last = nc.tensor.matmul(PS[3][:, j * 64:(j + 1) * 64], tile(LTa[:, 0, :], j), AMa[:, 2, j * 64:(j + 1) * 64], start=True, stop=True)
                        last.then_inc(gsa_slots_by_pe, 1)
                        for j in range(4):
                            last = nc.tensor.transpose(tile(PS[0], j), tile(LBa[:, 3, :], j), IDENT[:, :])
                        last.then_inc(gsa_turned_by_pe, 1)
                        pe.wait_ge(gsa_decay_by_dve, n * 16 + 16)
                        pe.wait_ge(gsa_turned_by_act, n * 10 + 6)
                        for j in range(4):
                            last = nc.tensor.transpose(tile(PS[1], j), tile(LBa[:, 4, :], j), IDENT[:, :])
                        pe.wait_ge(gsa_masked_by_pool, n * 13 + 9)
                        for j in range(4):
                            last = nc.tensor.matmul(PS[2][:, j * 64:(j + 1) * 64], tile(LTa[:, 1, :], j), AMa[:, 3, j * 64:(j + 1) * 64], start=True, stop=True)
                        last.then_inc(gsa_slots_by_pe, 1)
                        pe.wait_ge(gsa_masked_by_pool, n * 13 + 10)
                        pe.wait_ge(gsa_turned_by_act, n * 10 + 7)
                        for j in range(4):
                            last = nc.tensor.matmul(PS[7][:, j * 64:(j + 1) * 64], tile(LTb[:, 0, :], j), AMb[:, 4, j * 64:(j + 1) * 64], start=True, stop=True)
                        last.then_inc(gsa_slots_by_pe, 1)
                        pe.wait_ge(gsa_masked_by_pool, n * 13 + 11)
                        pe.wait_ge(gsa_level_by_dve, n * 12 + 4)
                        pe.wait_ge(gsa_turned_by_act, n * 10 + 8)
                        for j in range(4):
                            last = nc.tensor.matmul(PS[6][:, j * 64:(j + 1) * 64], tile(LTb[:, 1, :], j), AMb[:, 5, j * 64:(j + 1) * 64], start=True, stop=True)
                        last.then_inc(gsa_slots_by_pe, 1)
                        pe.wait_ge(gsa_masked_by_pool, n * 13 + 12)
                        pe.wait_ge(gsa_level_by_dve, n * 12 + 5)
                        pe.wait_ge(gsa_turned_by_act, n * 10 + 9)
                        for j in range(4):
                            last = nc.tensor.matmul(PS[3][:, j * 64:(j + 1) * 64], tile(LTa[:, 0, :], j), AMa[:, 4, j * 64:(j + 1) * 64], start=True, stop=True)
                        last.then_inc(gsa_slots_by_pe, 1)
                        pe.wait_ge(gsa_masked_by_pool, n * 13 + 13)
                        pe.wait_ge(gsa_turned_by_act, n * 10 + 10)
                        pe.wait_ge(gsa_level_by_dve, n * 12 + 6)
                        for j in range(4):
                            last = nc.tensor.matmul(PS[2][:, j * 64:(j + 1) * 64], tile(LTa[:, 1, :], j), AMa[:, 5, j * 64:(j + 1) * 64], start=True, stop=True)
                        last.then_inc(gsa_slots_by_pe, 1)
                        pe.wait_ge(gsa_level_by_dve, n * 12 + 9)
                        for j in range(4):
                            last = nc.tensor.transpose(tile(PS[4], j), tile(Sb, j), IDENT[:, :])
                        last.then_inc(gsa_softmax_by_pe, 1)
                        pe.wait_ge(gsa_level_by_dve, n * 12 + 12)
                        for j in range(4):
                            last = nc.tensor.transpose(tile(PS[0], j), tile(Sa, j), IDENT[:, :])
                        last.then_inc(gsa_softmax_by_pe, 1)
                        pe.wait_ge(gsa_softmax_by_act, n * 4 + 1)
                        for j in range(4):
                            last = nc.tensor.transpose(tile(PS[5], j), tile(ab, j), IDENT[:, :])
                        last.then_inc(gsa_softmax_by_pe, 1)
                        pe.wait_ge(gsa_softmax_by_act, n * 4 + 2)
                        for j in range(4):
                            last = nc.tensor.transpose(tile(PS[1], j), tile(aa, j), IDENT[:, :])
                        last.then_inc(gsa_softmax_by_pe, 1)
                        pe.wait_ge(gsa_softmax_by_act, n * 4 + 3)
                        for j in range(4):
                            last = nc.tensor.matmul(tile(PS[6], j), tile(wTb, j), tile(aTb, j), start=True, stop=True)
                        last.then_inc(gsa_weights_by_pe, 1)
                        pe.wait_ge(gsa_softmax_by_act, n * 4 + 4)
                        for j in range(4):
                            last = nc.tensor.matmul(tile(PS[2], j), tile(wTa, j), tile(aTa, j), start=True, stop=True)
                        last.then_inc(gsa_weights_by_pe, 1)
                        pe.wait_ge(gsa_reach_by_dve, n * 3 + 1)
                        for j in range(4):
                            last = nc.tensor.matmul(PS[7][:, j * 64:(j + 1) * 64], tile(wTb, j), aRb[:, 0, j * 64:(j + 1) * 64], start=True, stop=True)
                        last.then_inc(gsa_weights_by_pe, 1)
                        pe.wait_ge(gsa_reach_by_dve, n * 3 + 2)
                        for j in range(4):
                            last = nc.tensor.matmul(PS[3][:, j * 64:(j + 1) * 64], tile(wTa, j), aRa[:, 0, j * 64:(j + 1) * 64], start=True, stop=True)
                        last.then_inc(gsa_weights_by_pe, 1)
                        pe.wait_ge(gsa_reach_by_pool, n * 5 + 1)
                        for j in range(4):
                            last = nc.tensor.matmul(PS[4][:, j * 64:(j + 1) * 64], tile(LBb[:, 0, :], j), aRb[:, 1, j * 64:(j + 1) * 64], start=True, stop=True)
                        last.then_inc(gsa_weights_by_pe, 1)
                        pe.wait_ge(gsa_reach_by_pool, n * 5 + 2)
                        for j in range(4):
                            last = nc.tensor.matmul(PS[0][:, j * 64:(j + 1) * 64], tile(LBa[:, 0, :], j), aRa[:, 1, j * 64:(j + 1) * 64], start=True, stop=True)
                        last.then_inc(gsa_weights_by_pe, 1)
                        for j in range(4):
                            last = nc.tensor.matmul(PS[5][:, j * 64:(j + 1) * 64], tile(LBb[:, 1, :], j), aRb[:, 2, j * 64:(j + 1) * 64], start=True, stop=True)
                        last.then_inc(gsa_weights_by_pe, 1)
                        pe.wait_ge(gsa_reach_by_dve, n * 3 + 3)
                        for j in range(4):
                            last = nc.tensor.matmul(PS[1][:, j * 64:(j + 1) * 64], tile(LBa[:, 1, :], j), aRa[:, 2, j * 64:(j + 1) * 64], start=True, stop=True)
                        last.then_inc(gsa_weights_by_pe, 1)
                        for j in range(4):
                            last = nc.tensor.matmul(PS[6][:, j * 64:(j + 1) * 64], tile(LBb[:, 2, :], j), aRb[:, 3, j * 64:(j + 1) * 64], start=True, stop=True)
                        last.then_inc(gsa_weights_by_pe, 1)
                        pe.wait_ge(gsa_reach_by_pool, n * 5 + 3)
                        for j in range(4):
                            last = nc.tensor.matmul(PS[2][:, j * 64:(j + 1) * 64], tile(LBa[:, 2, :], j), aRa[:, 3, j * 64:(j + 1) * 64], start=True, stop=True)
                        last.then_inc(gsa_weights_by_pe, 1)
                        pe.wait_ge(gsa_weights_by_dve, n * 14 + 3)
                        for j in range(4):
                            last = nc.tensor.matmul(PS[7][:, j * 64:(j + 1) * 64], tile(LBb[:, 3, :], j), aRb[:, 4, j * 64:(j + 1) * 64], start=True, stop=True)
                        last.then_inc(gsa_weights_by_pe, 1)
                        pe.wait_ge(gsa_weights_by_dve, n * 14 + 4)
                        for j in range(4):
                            last = nc.tensor.matmul(PS[3][:, j * 64:(j + 1) * 64], tile(LBa[:, 3, :], j), aRa[:, 4, j * 64:(j + 1) * 64], start=True, stop=True)
                        last.then_inc(gsa_weights_by_pe, 1)
                        pe.wait_ge(gsa_reach_by_pool, n * 5 + 4)
                        pe.wait_ge(gsa_weights_by_dve, n * 14 + 5)
                        for j in range(4):
                            last = nc.tensor.matmul(PS[4][:, j * 64:(j + 1) * 64], tile(LBb[:, 4, :], j), aRb[:, 5, j * 64:(j + 1) * 64], start=True, stop=True)
                        last.then_inc(gsa_weights_by_pe, 1)
                        pe.wait_ge(gsa_reach_by_pool, n * 5 + 5)
                        pe.wait_ge(gsa_weights_by_dve, n * 14 + 6)
                        for j in range(4):
                            last = nc.tensor.matmul(PS[0][:, j * 64:(j + 1) * 64], tile(LBa[:, 4, :], j), aRa[:, 5, j * 64:(j + 1) * 64], start=True, stop=True)
                        last.then_inc(gsa_weights_by_pe, 1)
                        pe.wait_ge(gsa_weights_by_dve, n * 14 + 13)
                        for j in range(4):
                            last = nc.tensor.matmul(tile(PS[6], j), tile(Vb, j), tile(PTb, j), start=True, stop=True)
                        last.then_inc(gsa_read_by_pe, 1)
                        pe.wait_ge(gsa_weights_by_dve, n * 14 + 14)
                        for j in range(4):
                            last = nc.tensor.matmul(tile(PS[2], j), tile(Va, j), tile(PTa, j), start=True, stop=True)
                        last.then_inc(gsa_read_by_pe, 1)
                        pe.wait_ge(gsa_osquare_by_act, n * 2 + 1)
                        for j in range(4):
                            last = nc.tensor.matmul(PS[7][:, j:j + 1], tile(aTb, j), ones[:, 0:1], start=True, stop=True)
                        last.then_inc(gsa_onorm_by_pe, 1)
                        pe.wait_ge(gsa_out_weights_dma, n * 16 + 16)
                        pe.wait_ge(gsa_ogate_by_dve, n * 2 + 1)
                        for j in range(4):
                            last = nc.tensor.matmul(PS[4 + j // 2][:, (j % 2) * 256:(j % 2) * 256 + 256], tile(ogb, j), WO[:, :], start=True, stop=True)
                        last.then_inc(gsa_output_by_pe, 1)
                        pe.wait_ge(gsa_osquare_by_act, n * 2 + 2)
                        for j in range(4):
                            last = nc.tensor.matmul(PS[3][:, j:j + 1], tile(aTa, j), ones[:, 0:1], start=True, stop=True)
                        last.then_inc(gsa_onorm_by_pe, 1)
                        pe.wait_ge(gsa_ogate_by_dve, n * 2 + 2)
                        for j in range(4):
                            last = nc.tensor.matmul(PS[0 + j // 2][:, (j % 2) * 256:(j % 2) * 256 + 256], tile(oga, j), WO[:, :], start=True, stop=True)
                        last.then_inc(gsa_output_by_pe, 1)

            @block.vector
            def _(dve):
                dve.sem_inc(gsa_conv_by_dve, 23)
                dve.sem_inc(gsa_residual_by_dve, 2)
                dve.wait_ge(gsa_setup_by_pool, 1)
                dve.wait_ge(gsa_setup_loads_sp, 64)
                with dve.Fori(0, 16) as h:
                    with dve.Fori(0, 4) as gp:
                        n = h * 4 + gp
                        dve.wait_ge(gsa_conv0_by_act, n * 8 + 1)
                        nc.vector.scalar_tensor_tensor(seqs(wTb[:, :])[:, :, 1:64], seqs(PS[4][:, :])[:, :, 0:63], WCV[:, 10:11],
                                                       seqs(wTb[:, :])[:, :, 1:64], ALU.mult, ALU.add).then_inc(gsa_conv_by_dve, 1)
                        dve.wait_ge(gsa_conv_by_dve, n * 23 + 24)
                        nc.vector.scalar_tensor_tensor(seqs(wTb[:, :])[:, :, 2:64], seqs(PS[4][:, :])[:, :, 0:62], WCV[:, 9:10],
                                                       seqs(wTb[:, :])[:, :, 2:64], ALU.mult, ALU.add).then_inc(gsa_conv_by_dve, 1)
                        dve.wait_ge(gsa_conv_by_dve, n * 23 + 25)
                        nc.vector.scalar_tensor_tensor(seqs(wTb[:, :])[:, :, 3:64], seqs(PS[4][:, :])[:, :, 0:61], WCV[:, 8:9],
                                                       seqs(wTb[:, :])[:, :, 3:64], ALU.mult, ALU.add).then_inc(gsa_conv_by_dve, 1)
                        dve.wait_ge(gsa_conv0_by_act, n * 8 + 2)
                        nc.vector.scalar_tensor_tensor(seqs(vTb[:, :])[:, :, 1:64], seqs(PS[7][:, :])[:, :, 0:63], WCV[:, 10:11],
                                                       seqs(vTb[:, :])[:, :, 1:64], ALU.mult, ALU.add).then_inc(gsa_conv_by_dve, 1)
                        dve.wait_ge(gsa_conv_by_dve, n * 23 + 27)
                        nc.vector.scalar_tensor_tensor(seqs(vTb[:, :])[:, :, 2:64], seqs(PS[7][:, :])[:, :, 0:62], WCV[:, 9:10],
                                                       seqs(vTb[:, :])[:, :, 2:64], ALU.mult, ALU.add).then_inc(gsa_conv_by_dve, 1)
                        dve.wait_ge(gsa_conv_by_dve, n * 23 + 28)
                        nc.vector.scalar_tensor_tensor(seqs(vTb[:, :])[:, :, 3:64], seqs(PS[7][:, :])[:, :, 0:61], WCV[:, 8:9],
                                                       seqs(vTb[:, :])[:, :, 3:64], ALU.mult, ALU.add).then_inc(gsa_conv_by_dve, 1)
                        dve.wait_ge(gsa_conv0_by_act, n * 8 + 3)
                        nc.vector.scalar_tensor_tensor(seqs(qTb[:, :])[:, :, 1:64], seqs(PS[5][:, :])[:, :, 0:63], WCV[:, 2:3],
                                                       seqs(qTb[:, :])[:, :, 1:64], ALU.mult, ALU.add).then_inc(gsa_conv_by_dve, 1)
                        dve.wait_ge(gsa_conv0_by_act, n * 8 + 4)
                        nc.vector.scalar_tensor_tensor(seqs(wTa[:, :])[:, :, 1:64], seqs(PS[0][:, :])[:, :, 0:63], WCV[:, 10:11],
                                                       seqs(wTa[:, :])[:, :, 1:64], ALU.mult, ALU.add).then_inc(gsa_conv_by_dve, 1)
                        dve.wait_ge(gsa_conv_by_dve, n * 23 + 30)
                        nc.vector.scalar_tensor_tensor(seqs(qTb[:, :])[:, :, 2:64], seqs(PS[5][:, :])[:, :, 0:62], WCV[:, 1:2],
                                                       seqs(qTb[:, :])[:, :, 2:64], ALU.mult, ALU.add)
                        dve.wait_ge(gsa_conv_by_dve, n * 23 + 31)
                        nc.vector.scalar_tensor_tensor(seqs(wTa[:, :])[:, :, 2:64], seqs(PS[0][:, :])[:, :, 0:62], WCV[:, 9:10],
                                                       seqs(wTa[:, :])[:, :, 2:64], ALU.mult, ALU.add).then_inc(gsa_conv_by_dve, 1)
                        dve.wait_ge(gsa_conv0_by_act, n * 8 + 5)
                        nc.vector.scalar_tensor_tensor(seqs(kTb[:, :])[:, :, 1:64], seqs(PS[6][:, :])[:, :, 0:63], WCV[:, 6:7],
                                                       seqs(kTb[:, :])[:, :, 1:64], ALU.mult, ALU.add).then_inc(gsa_conv_by_dve, 1)
                        dve.wait_ge(gsa_conv_by_dve, n * 23 + 32)
                        nc.vector.scalar_tensor_tensor(seqs(wTa[:, :])[:, :, 3:64], seqs(PS[0][:, :])[:, :, 0:61], WCV[:, 8:9],
                                                       seqs(wTa[:, :])[:, :, 3:64], ALU.mult, ALU.add).then_inc(gsa_conv_by_dve, 1)
                        dve.wait_ge(gsa_conv_by_dve, n * 23 + 33)
                        nc.vector.scalar_tensor_tensor(seqs(kTb[:, :])[:, :, 2:64], seqs(PS[6][:, :])[:, :, 0:62], WCV[:, 5:6],
                                                       seqs(kTb[:, :])[:, :, 2:64], ALU.mult, ALU.add).then_inc(gsa_conv_by_dve, 1)
                        dve.wait_ge(gsa_conv0_by_act, n * 8 + 6)
                        nc.vector.scalar_tensor_tensor(seqs(vTa[:, :])[:, :, 1:64], seqs(PS[3][:, :])[:, :, 0:63], WCV[:, 10:11],
                                                       seqs(vTa[:, :])[:, :, 1:64], ALU.mult, ALU.add).then_inc(gsa_conv_by_dve, 1)
                        nc.vector.scalar_tensor_tensor(seqs(qTb[:, :])[:, :, 3:64], seqs(PS[5][:, :])[:, :, 0:61], WCV[:, 0:1],
                                                       seqs(qTb[:, :])[:, :, 3:64], ALU.mult, ALU.add).then_inc(gsa_conv_by_dve, 1)
                        dve.wait_ge(gsa_conv_by_dve, n * 23 + 35)
                        nc.vector.scalar_tensor_tensor(seqs(kTb[:, :])[:, :, 3:64], seqs(PS[6][:, :])[:, :, 0:61], WCV[:, 4:5],
                                                       seqs(kTb[:, :])[:, :, 3:64], ALU.mult, ALU.add).then_inc(gsa_conv_by_dve, 1)
                        dve.wait_ge(gsa_conv_by_dve, n * 23 + 36)
                        nc.vector.scalar_tensor_tensor(seqs(vTa[:, :])[:, :, 2:64], seqs(PS[3][:, :])[:, :, 0:62], WCV[:, 9:10],
                                                       seqs(vTa[:, :])[:, :, 2:64], ALU.mult, ALU.add).then_inc(gsa_conv_by_dve, 1)
                        dve.wait_ge(gsa_conv0_by_act, n * 8 + 7)
                        nc.vector.scalar_tensor_tensor(seqs(kTa[:, :])[:, :, 1:64], seqs(PS[2][:, :])[:, :, 0:63], WCV[:, 6:7],
                                                       seqs(kTa[:, :])[:, :, 1:64], ALU.mult, ALU.add).then_inc(gsa_conv_by_dve, 1)
                        dve.wait_ge(gsa_conv_by_dve, n * 23 + 39)
                        nc.vector.scalar_tensor_tensor(seqs(vTa[:, :])[:, :, 3:64], seqs(PS[3][:, :])[:, :, 0:61], WCV[:, 8:9],
                                                       seqs(vTa[:, :])[:, :, 3:64], ALU.mult, ALU.add).then_inc(gsa_conv_by_dve, 1)
                        dve.wait_ge(gsa_conv0_by_act, n * 8 + 8)
                        nc.vector.scalar_tensor_tensor(seqs(qTa[:, :])[:, :, 1:64], seqs(PS[1][:, :])[:, :, 0:63], WCV[:, 2:3],
                                                       seqs(qTa[:, :])[:, :, 1:64], ALU.mult, ALU.add).then_inc(gsa_conv_by_dve, 1)
                        dve.wait_ge(gsa_conv_by_dve, n * 23 + 40)
                        nc.vector.scalar_tensor_tensor(seqs(kTa[:, :])[:, :, 2:64], seqs(PS[2][:, :])[:, :, 0:62], WCV[:, 5:6],
                                                       seqs(kTa[:, :])[:, :, 2:64], ALU.mult, ALU.add).then_inc(gsa_conv_by_dve, 1)
                        dve.wait_ge(gsa_conv_by_dve, n * 23 + 42)
                        nc.vector.scalar_tensor_tensor(seqs(qTa[:, :])[:, :, 2:64], seqs(PS[1][:, :])[:, :, 0:62], WCV[:, 1:2],
                                                       seqs(qTa[:, :])[:, :, 2:64], ALU.mult, ALU.add).then_inc(gsa_conv_by_dve, 1)
                        dve.wait_ge(gsa_conv_by_dve, n * 23 + 43)
                        nc.vector.scalar_tensor_tensor(seqs(kTa[:, :])[:, :, 3:64], seqs(PS[2][:, :])[:, :, 0:61], WCV[:, 4:5],
                                                       seqs(kTa[:, :])[:, :, 3:64], ALU.mult, ALU.add).then_inc(gsa_conv_by_dve, 1)
                        dve.wait_ge(gsa_conv_by_dve, n * 23 + 44)
                        nc.vector.scalar_tensor_tensor(seqs(qTa[:, :])[:, :, 3:64], seqs(PS[1][:, :])[:, :, 0:61], WCV[:, 0:1],
                                                       seqs(qTa[:, :])[:, :, 3:64], ALU.mult, ALU.add).then_inc(gsa_conv_by_dve, 1)
                        dve.wait_ge(gsa_wnorm_by_pe, n * 2 + 1)
                        nc.vector.tensor_scalar(ssb[:, :], PS[7][:, 0:4], 1e-6, None, ALU.add).then_inc(gsa_wnorm_by_dve, 1)
                        dve.wait_ge(gsa_wnorm_by_pe, n * 2 + 2)
                        nc.vector.tensor_scalar(ssa[:, :], PS[3][:, 0:4], 1e-6, None, ALU.add).then_inc(gsa_wnorm_by_dve, 1)
                        dve.wait_ge(gsa_sigmoid_by_act, n * 4 + 1)
                        nc.vector.tensor_tensor(left(LBb[:, 0, :], 1), left(wTb[:, :], 1), lastof(preb[:, :], 1, 1), ALU.mult).then_inc(gsa_decay_by_dve, 1)
                        dve.wait_ge(gsa_kept_by_act, n * 10 + 1)
                        dve.wait_ge(gsa_decay_by_dve, n * 16 + 1)
                        nc.vector.tensor_tensor(right(preb[:, :], 1), right(preb[:, :], 1), lastof(preb[:, :], 1, 0), ALU.mult).then_inc(gsa_decay_by_dve, 1)
                        dve.wait_ge(gsa_decay_by_dve, n * 16 + 2)
                        nc.vector.tensor_tensor(left(LBb[:, 1, :], 2), left(LBb[:, 0, :], 2), lastof(preb[:, :], 2, 1), ALU.mult)
                        dve.wait_ge(gsa_sigmoid_by_act, n * 4 + 2)
                        nc.vector.tensor_tensor(left(LBa[:, 0, :], 1), left(wTa[:, :], 1), lastof(prea[:, :], 1, 1), ALU.mult).then_inc(gsa_decay_by_dve, 1)
                        dve.wait_ge(gsa_decay_by_dve, n * 16 + 3)
                        dve.wait_ge(gsa_kept_by_act, n * 10 + 2)
                        nc.vector.tensor_tensor(right(prea[:, :], 1), right(prea[:, :], 1), lastof(prea[:, :], 1, 0), ALU.mult).then_inc(gsa_decay_by_dve, 1)
                        dve.wait_ge(gsa_decay_by_dve, n * 16 + 4)
                        nc.vector.tensor_tensor(left(LBa[:, 1, :], 2), left(LBa[:, 0, :], 2), lastof(prea[:, :], 2, 1), ALU.mult)
                        dve.wait_ge(gsa_kept_by_act, n * 10 + 3)
                        nc.vector.tensor_tensor(right(preb[:, :], 2), right(preb[:, :], 2), lastof(preb[:, :], 2, 0), ALU.mult).then_inc(gsa_decay_by_dve, 1)
                        dve.wait_ge(gsa_slots_by_pe, n * 14 + 2)
                        nc.vector.tensor_tensor(packed(tmpb[:, 0, :], 1), packed(PS[7][:, 0:256], 1), packed(Rb[:, 0, :], 1), ALU.mult)
                        dve.wait_ge(gsa_decay_by_dve, n * 16 + 5)
                        dve.wait_ge(gsa_decay_by_act, n * 6 + 1)
                        nc.vector.tensor_tensor(left(LBb[:, 2, :], 4), left(LBb[:, 1, :], 4), lastof(preb[:, :], 4, 1), ALU.mult).then_inc(gsa_decay_by_dve, 1)
                        dve.wait_ge(gsa_kept_by_act, n * 10 + 4)
                        nc.vector.tensor_tensor(right(prea[:, :], 2), right(prea[:, :], 2), lastof(prea[:, :], 2, 0), ALU.mult).then_inc(gsa_decay_by_dve, 1)
                        dve.wait_ge(gsa_decay_by_dve, n * 16 + 6)
                        dve.wait_ge(gsa_kept_by_act, n * 10 + 5)
                        nc.vector.tensor_tensor(right(preb[:, :], 4), right(preb[:, :], 4), lastof(preb[:, :], 4, 0), ALU.mult).then_inc(gsa_decay_by_dve, 1)
                        dve.wait_ge(gsa_decay_by_dve, n * 16 + 7)
                        dve.wait_ge(gsa_decay_by_act, n * 6 + 2)
                        nc.vector.tensor_tensor(left(LBa[:, 2, :], 4), left(LBa[:, 1, :], 4), lastof(prea[:, :], 4, 1), ALU.mult).then_inc(gsa_decay_by_dve, 1)
                        dve.wait_ge(gsa_slots_by_pe, n * 14 + 4)
                        nc.vector.tensor_tensor(packed(tmpa[:, 0, :], 1), packed(PS[3][:, 0:256], 1), packed(Ra[:, 0, :], 1), ALU.mult)
                        dve.wait_ge(gsa_slots_by_act, n * 2 + 1)
                        nc.vector.tensor_tensor(right(Sb[:, :], 1), right(Sb[:, :], 1), packed(tmpb[:, 0, :], 1), ALU.add)
                        dve.wait_ge(gsa_decay_by_dve, n * 16 + 8)
                        dve.wait_ge(gsa_decay_by_act, n * 6 + 3)
                        nc.vector.tensor_tensor(left(LBb[:, 3, :], 8), left(LBb[:, 2, :], 8), lastof(preb[:, :], 8, 1), ALU.mult).then_inc(gsa_decay_by_dve, 1)
                        dve.wait_ge(gsa_slots_by_pe, n * 14 + 5)
                        nc.vector.tensor_tensor(packed(tmpb[:, 1, :], 2), packed(PS[6][:, 0:256], 2), packed(Rb[:, 1, :], 2), ALU.mult).then_inc(gsa_level_by_dve, 1)
                        dve.wait_ge(gsa_decay_by_dve, n * 16 + 9)
                        dve.wait_ge(gsa_kept_by_act, n * 10 + 6)
                        nc.vector.tensor_tensor(right(prea[:, :], 4), right(prea[:, :], 4), lastof(prea[:, :], 4, 0), ALU.mult).then_inc(gsa_decay_by_dve, 1)
                        dve.wait_ge(gsa_level_by_dve, n * 12 + 1)
                        nc.vector.tensor_tensor(right(Sb[:, :], 2), right(Sb[:, :], 2), packed(tmpb[:, 1, :], 2), ALU.add)
                        dve.wait_ge(gsa_decay_by_dve, n * 16 + 11)
                        dve.wait_ge(gsa_decay_by_act, n * 6 + 4)
                        nc.vector.tensor_tensor(left(LBa[:, 3, :], 8), left(LBa[:, 2, :], 8), lastof(prea[:, :], 8, 1), ALU.mult).then_inc(gsa_decay_by_dve, 1)
                        dve.wait_ge(gsa_kept_by_act, n * 10 + 7)
                        nc.vector.tensor_tensor(right(preb[:, :], 8), right(preb[:, :], 8), lastof(preb[:, :], 8, 0), ALU.mult).then_inc(gsa_decay_by_dve, 1)
                        dve.wait_ge(gsa_slots_by_act, n * 2 + 2)
                        nc.vector.tensor_tensor(right(Sa[:, :], 1), right(Sa[:, :], 1), packed(tmpa[:, 0, :], 1), ALU.add)
                        dve.wait_ge(gsa_decay_by_dve, n * 16 + 13)
                        dve.wait_ge(gsa_decay_by_act, n * 6 + 5)
                        nc.vector.tensor_tensor(left(LBb[:, 4, :], 16), left(LBb[:, 3, :], 16), lastof(preb[:, :], 16, 1), ALU.mult).then_inc(gsa_decay_by_dve, 1)
                        dve.wait_ge(gsa_slots_by_pe, n * 14 + 6)
                        nc.vector.tensor_tensor(packed(tmpa[:, 1, :], 2), packed(PS[2][:, 0:256], 2), packed(Ra[:, 1, :], 2), ALU.mult).then_inc(gsa_level_by_dve, 1)
                        dve.wait_ge(gsa_level_by_dve, n * 12 + 2)
                        nc.vector.tensor_tensor(right(Sa[:, :], 2), right(Sa[:, :], 2), packed(tmpa[:, 1, :], 2), ALU.add)
                        dve.wait_ge(gsa_kept_by_act, n * 10 + 8)
                        nc.vector.tensor_tensor(right(prea[:, :], 8), right(prea[:, :], 8), lastof(prea[:, :], 8, 0), ALU.mult).then_inc(gsa_decay_by_dve, 1)
                        dve.wait_ge(gsa_slots_by_pe, n * 14 + 7)
                        nc.vector.tensor_tensor(packed(tmpb[:, 0, :], 4), packed(PS[7][:, 0:256], 4), packed(Rb[:, 2, :], 4), ALU.mult).then_inc(gsa_level_by_dve, 1)
                        dve.wait_ge(gsa_level_by_dve, n * 12 + 3)
                        nc.vector.tensor_tensor(right(Sb[:, :], 4), right(Sb[:, :], 4), packed(tmpb[:, 0, :], 4), ALU.add)
                        dve.wait_ge(gsa_decay_by_act, n * 6 + 6)
                        nc.vector.tensor_tensor(left(LBa[:, 4, :], 16), left(LBa[:, 3, :], 16), lastof(prea[:, :], 16, 1), ALU.mult).then_inc(gsa_decay_by_dve, 1)
                        dve.wait_ge(gsa_slots_by_pe, n * 14 + 8)
                        nc.vector.tensor_tensor(packed(tmpb[:, 1, :], 8), packed(PS[6][:, 0:256], 8), packed(Rb[:, 3, :], 8), ALU.mult).then_inc(gsa_level_by_dve, 1)
                        dve.wait_ge(gsa_level_by_dve, n * 12 + 4)
                        nc.vector.tensor_tensor(right(Sb[:, :], 8), right(Sb[:, :], 8), packed(tmpb[:, 1, :], 8), ALU.add)
                        dve.wait_ge(gsa_slots_by_pe, n * 14 + 9)
                        nc.vector.tensor_tensor(packed(tmpa[:, 0, :], 4), packed(PS[3][:, 0:256], 4), packed(Ra[:, 2, :], 4), ALU.mult).then_inc(gsa_level_by_dve, 1)
                        dve.wait_ge(gsa_level_by_dve, n * 12 + 5)
                        nc.vector.tensor_tensor(right(Sa[:, :], 4), right(Sa[:, :], 4), packed(tmpa[:, 0, :], 4), ALU.add)
                        dve.wait_ge(gsa_kept_by_act, n * 10 + 9)
                        nc.vector.tensor_tensor(right(preb[:, :], 16), right(preb[:, :], 16), lastof(preb[:, :], 16, 0), ALU.mult)
                        dve.wait_ge(gsa_slots_by_pe, n * 14 + 10)
                        nc.vector.tensor_tensor(packed(tmpa[:, 1, :], 8), packed(PS[2][:, 0:256], 8), packed(Ra[:, 3, :], 8), ALU.mult).then_inc(gsa_level_by_dve, 1)
                        dve.wait_ge(gsa_kept_by_act, n * 10 + 10)
                        nc.vector.tensor_tensor(right(prea[:, :], 16), right(prea[:, :], 16), lastof(prea[:, :], 16, 0), ALU.mult)
                        dve.wait_ge(gsa_level_by_dve, n * 12 + 6)
                        nc.vector.tensor_tensor(right(Sa[:, :], 8), right(Sa[:, :], 8), packed(tmpa[:, 1, :], 8), ALU.add)
                        dve.wait_ge(gsa_slots_by_pe, n * 14 + 11)
                        nc.vector.tensor_tensor(packed(tmpb[:, 0, :], 16), packed(PS[7][:, 0:256], 16), packed(Rb[:, 4, :], 16), ALU.mult).then_inc(gsa_level_by_dve, 1)
                        dve.wait_ge(gsa_level_by_dve, n * 12 + 7)
                        nc.vector.tensor_tensor(right(Sb[:, :], 16), right(Sb[:, :], 16), packed(tmpb[:, 0, :], 16), ALU.add)
                        dve.wait_ge(gsa_slots_by_pe, n * 14 + 12)
                        nc.vector.tensor_tensor(packed(tmpb[:, 1, :], 32), packed(PS[6][:, 0:256], 32), right(preb[:, :], 32), ALU.mult).then_inc(gsa_level_by_dve, 1)
                        dve.wait_ge(gsa_level_by_dve, n * 12 + 8)
                        nc.vector.tensor_tensor(right(Sb[:, :], 32), right(Sb[:, :], 32), packed(tmpb[:, 1, :], 32), ALU.add).then_inc(gsa_level_by_dve, 1)
                        dve.wait_ge(gsa_slots_by_pe, n * 14 + 13)
                        nc.vector.tensor_tensor(packed(tmpa[:, 0, :], 16), packed(PS[3][:, 0:256], 16), packed(Ra[:, 4, :], 16), ALU.mult).then_inc(gsa_level_by_dve, 1)
                        dve.wait_ge(gsa_level_by_dve, n * 12 + 10)
                        nc.vector.tensor_tensor(right(Sa[:, :], 16), right(Sa[:, :], 16), packed(tmpa[:, 0, :], 16), ALU.add)
                        dve.wait_ge(gsa_slots_by_pe, n * 14 + 14)
                        nc.vector.tensor_tensor(packed(tmpa[:, 1, :], 32), packed(PS[2][:, 0:256], 32), right(prea[:, :], 32), ALU.mult).then_inc(gsa_level_by_dve, 1)
                        dve.wait_ge(gsa_level_by_dve, n * 12 + 11)
                        nc.vector.tensor_tensor(right(Sa[:, :], 32), right(Sa[:, :], 32), packed(tmpa[:, 1, :], 32), ALU.add).then_inc(gsa_level_by_dve, 1)
                        dve.wait_ge(gsa_softmax_by_pe, n * 4 + 1)
                        nc.vector.reduce_max(mxb[:, :], PS[4][:, :].rearrange("p (j m) -> p j m", j=4), AX.X).then_inc(gsa_softmax_by_dve, 1)
                        dve.wait_ge(gsa_softmax_by_dve, n * 4 + 1)
                        nc.vector.tensor_scalar(nmxb[:, :], mxb[:, :], -SCALE, None, ALU.mult).then_inc(gsa_softmax_by_dve, 1)
                        dve.wait_ge(gsa_softmax_by_pe, n * 4 + 2)
                        nc.vector.reduce_max(mxa[:, :], PS[0][:, :].rearrange("p (j m) -> p j m", j=4), AX.X).then_inc(gsa_softmax_by_dve, 1)
                        dve.wait_ge(gsa_softmax_by_dve, n * 4 + 3)
                        nc.vector.tensor_scalar(nmxa[:, :], mxa[:, :], -SCALE, None, ALU.mult).then_inc(gsa_softmax_by_dve, 1)
                        dve.wait_ge(gsa_onorm_by_pool, n * 4 + 1)
                        nc.vector.tensor_scalar(den2b[:, :], den2b[:, :], 1e-5, None, ALU.mult)
                        dve.wait_ge(gsa_onorm_by_pool, n * 4 + 2)
                        nc.vector.tensor_scalar(den2a[:, :], den2a[:, :], 1e-5, None, ALU.mult)
                        dve.wait_ge(gsa_softmax_by_act, n * 4 + 3)
                        nc.vector.tensor_tensor(packed(aRb[:, 0, :], 1), right(aTb[:, :], 1), packed(Rb[:, 0, :], 1), ALU.mult).then_inc(gsa_reach_by_dve, 1)
                        nc.vector.tensor_tensor(packed(aRb[:, 2, :], 4), right(aTb[:, :], 4), packed(Rb[:, 2, :], 4), ALU.mult)
                        nc.vector.tensor_tensor(packed(aRb[:, 4, :], 16), right(aTb[:, :], 16), packed(Rb[:, 4, :], 16), ALU.mult)
                        dve.wait_ge(gsa_softmax_by_act, n * 4 + 4)
                        nc.vector.tensor_tensor(packed(aRa[:, 0, :], 1), right(aTa[:, :], 1), packed(Ra[:, 0, :], 1), ALU.mult).then_inc(gsa_reach_by_dve, 1)
                        dve.wait_ge(gsa_weights_by_pe, n * 14 + 1)
                        nc.vector.tensor_tensor(PTb[:, :], PS[6][:, :], EYES[:, :], ALU.mult).then_inc(gsa_weights_by_dve, 1)
                        dve.wait_ge(gsa_weights_by_pe, n * 14 + 2)
                        nc.vector.tensor_tensor(PTa[:, :], PS[2][:, :], EYES[:, :], ALU.mult).then_inc(gsa_weights_by_dve, 1)
                        nc.vector.tensor_tensor(packed(aRa[:, 2, :], 4), right(aTa[:, :], 4), packed(Ra[:, 2, :], 4), ALU.mult).then_inc(gsa_reach_by_dve, 1)
                        dve.wait_ge(gsa_weights_by_dve, n * 14 + 1)
                        dve.wait_ge(gsa_weights_by_pe, n * 14 + 3)
                        dve.sem_inc(gsa_dve_passed, 1)
                        nc.vector.copy_predicated(right(PTb[:, :], 1), packed(MASKS[:, 0, :].bitcast(I32), 1), packed(PS[7][:, 0:256], 1)).then_inc(gsa_weights_by_dve, 1)
                        nc.vector.tensor_tensor(packed(aRa[:, 4, :], 16), right(aTa[:, :], 16), packed(Ra[:, 4, :], 16), ALU.mult)
                        dve.wait_ge(gsa_weights_by_dve, n * 14 + 2)
                        dve.wait_ge(gsa_weights_by_pe, n * 14 + 4)
                        dve.sem_inc(gsa_dve_passed, 1)
                        nc.vector.copy_predicated(right(PTa[:, :], 1), packed(MASKS[:, 0, :].bitcast(I32), 1), packed(PS[3][:, 0:256], 1)).then_inc(gsa_weights_by_dve, 1)
                        dve.wait_ge(gsa_weights_by_dve, n * 14 + 3)
                        dve.wait_ge(gsa_weights_by_pe, n * 14 + 5)
                        dve.sem_inc(gsa_dve_passed, 1)
                        nc.vector.copy_predicated(right(PTb[:, :], 2), packed(MASKS[:, 1, :].bitcast(I32), 2), packed(PS[4][:, 0:256], 2)).then_inc(gsa_weights_by_dve, 1)
                        dve.wait_ge(gsa_weights_by_dve, n * 14 + 4)
                        dve.wait_ge(gsa_weights_by_pe, n * 14 + 6)
                        dve.sem_inc(gsa_dve_passed, 1)
                        nc.vector.copy_predicated(right(PTa[:, :], 2), packed(MASKS[:, 1, :].bitcast(I32), 2), packed(PS[0][:, 0:256], 2)).then_inc(gsa_weights_by_dve, 1)
                        dve.wait_ge(gsa_weights_by_dve, n * 14 + 5)
                        dve.wait_ge(gsa_weights_by_pe, n * 14 + 7)
                        dve.sem_inc(gsa_dve_passed, 1)
                        nc.vector.copy_predicated(right(PTb[:, :], 4), packed(MASKS[:, 2, :].bitcast(I32), 4), packed(PS[5][:, 0:256], 4)).then_inc(gsa_weights_by_dve, 1)
                        dve.wait_ge(gsa_weights_by_dve, n * 14 + 6)
                        dve.wait_ge(gsa_weights_by_pe, n * 14 + 8)
                        dve.sem_inc(gsa_dve_passed, 1)
                        nc.vector.copy_predicated(right(PTa[:, :], 4), packed(MASKS[:, 2, :].bitcast(I32), 4), packed(PS[1][:, 0:256], 4)).then_inc(gsa_weights_by_dve, 1)
                        dve.wait_ge(gsa_weights_by_dve, n * 14 + 7)
                        dve.wait_ge(gsa_weights_by_pe, n * 14 + 9)
                        dve.sem_inc(gsa_dve_passed, 1)
                        nc.vector.copy_predicated(right(PTb[:, :], 8), packed(MASKS[:, 3, :].bitcast(I32), 8), packed(PS[6][:, 0:256], 8)).then_inc(gsa_weights_by_dve, 1)
                        dve.wait_ge(gsa_weights_by_dve, n * 14 + 8)
                        dve.wait_ge(gsa_weights_by_pe, n * 14 + 10)
                        dve.sem_inc(gsa_dve_passed, 1)
                        nc.vector.copy_predicated(right(PTa[:, :], 8), packed(MASKS[:, 3, :].bitcast(I32), 8), packed(PS[2][:, 0:256], 8)).then_inc(gsa_weights_by_dve, 1)
                        dve.wait_ge(gsa_weights_by_dve, n * 14 + 9)
                        dve.wait_ge(gsa_weights_by_pe, n * 14 + 11)
                        dve.sem_inc(gsa_dve_passed, 1)
                        nc.vector.copy_predicated(right(PTb[:, :], 16), packed(MASKS[:, 4, :].bitcast(I32), 16), packed(PS[7][:, 0:256], 16)).then_inc(gsa_weights_by_dve, 1)
                        dve.wait_ge(gsa_weights_by_dve, n * 14 + 10)
                        dve.wait_ge(gsa_weights_by_pe, n * 14 + 12)
                        dve.sem_inc(gsa_dve_passed, 1)
                        nc.vector.copy_predicated(right(PTa[:, :], 16), packed(MASKS[:, 4, :].bitcast(I32), 16), packed(PS[3][:, 0:256], 16)).then_inc(gsa_weights_by_dve, 1)
                        dve.wait_ge(gsa_weights_by_dve, n * 14 + 11)
                        dve.wait_ge(gsa_weights_by_pe, n * 14 + 13)
                        dve.sem_inc(gsa_dve_passed, 1)
                        nc.vector.copy_predicated(right(PTb[:, :], 32), packed(MASKS[:, 5, :].bitcast(I32), 32), packed(PS[4][:, 0:256], 32)).then_inc(gsa_weights_by_dve, 1)
                        dve.wait_ge(gsa_weights_by_dve, n * 14 + 12)
                        dve.wait_ge(gsa_weights_by_pe, n * 14 + 14)
                        dve.sem_inc(gsa_dve_passed, 1)
                        nc.vector.copy_predicated(right(PTa[:, :], 32), packed(MASKS[:, 5, :].bitcast(I32), 32), packed(PS[0][:, 0:256], 32)).then_inc(gsa_weights_by_dve, 1)
                        dve.wait_ge(gsa_osquare_by_act, n * 2 + 1)
                        nc.vector.scalar_tensor_tensor(ogb[:, :], sgb[:, :], NW[:, 0:1], PS[6][:, :], ALU.mult, ALU.mult).then_inc(gsa_ogate_by_dve, 1)
                        dve.wait_ge(gsa_osquare_by_act, n * 2 + 2)
                        nc.vector.scalar_tensor_tensor(oga[:, :], sga[:, :], NW[:, 0:1], PS[2][:, :], ALU.mult, ALU.mult).then_inc(gsa_ogate_by_dve, 1)
                        dve.wait_ge(gsa_onorm_by_pe, n * 2 + 1)
                        nc.vector.scalar_tensor_tensor(r0b[:, :], PS[7][:, 0:4], 1.0 / 128, den2b[:, :], ALU.mult, ALU.add).then_inc(gsa_onorm_by_dve, 1)
                        dve.wait_ge(gsa_output_by_pe, n * 2 + 3)
                        dve.wait_ge(gsa_onorm_by_pool, n * 4 + 3)
                        for j in range(4):
                            xs = X[:, bass.ds(gp * 2048 + 1024 + j * 256, 256)]
                            last = nc.vector.scalar_tensor_tensor(xs, PS[4 + j // 2][:, (j % 2) * 256:(j % 2) * 256 + 256], r4b[:, j:j + 1], xs, ALU.mult, ALU.add)
                        last.then_inc(gsa_residual_by_dve, 1)
                        dve.wait_ge(gsa_onorm_by_pe, n * 2 + 2)
                        nc.vector.scalar_tensor_tensor(r0a[:, :], PS[3][:, 0:4], 1.0 / 128, den2a[:, :], ALU.mult, ALU.add).then_inc(gsa_onorm_by_dve, 1)
                        dve.wait_ge(gsa_output_by_pe, n * 2 + 4)
                        dve.wait_ge(gsa_onorm_by_pool, n * 4 + 4)
                        for j in range(4):
                            xs = X[:, bass.ds(gp * 2048 + 0 + j * 256, 256)]
                            last = nc.vector.scalar_tensor_tensor(xs, PS[0 + j // 2][:, (j % 2) * 256:(j % 2) * 256 + 256], r4a[:, j:j + 1], xs, ALU.mult, ALU.add)
                        last.then_inc(gsa_residual_by_dve, 1)

            @block.scalar
            def _(act):
                act.wait_ge(gsa_setup_by_pool, 1)
                act.wait_ge(gsa_setup_loads_sp, 64)
                with act.Fori(0, 16) as h:
                    with act.Fori(0, 4) as gp:
                        n = h * 4 + gp
                        act.wait_ge(gsa_conv_weights_dma, n * 16 + 16)
                        act.wait_ge(gsa_projected_by_pe, n * 8 + 9)
                        nc.scalar.activation(wTb[:, :], PS[4][:, :], ACT.Copy, scale=WCV[:, 11:12]).then_inc(gsa_conv0_by_act, 1)
                        act.wait_ge(gsa_projected_by_pe, n * 8 + 10)
                        nc.scalar.activation(vTb[:, :], PS[7][:, :], ACT.Copy, scale=WCV[:, 11:12]).then_inc(gsa_conv0_by_act, 1)
                        act.wait_ge(gsa_conv_by_dve, n * 23 + 26)
                        nc.scalar.activation(wTb[:, :], wTb[:, :], ACT.Silu).then_inc(gsa_silu_by_act, 1)
                        act.wait_ge(gsa_projected_by_pe, n * 8 + 11)
                        nc.scalar.activation(qTb[:, :], PS[5][:, :], ACT.Copy, scale=WCV[:, 3:4]).then_inc(gsa_conv0_by_act, 1)
                        act.wait_ge(gsa_silu_by_act, n * 4 + 1)
                        nc.scalar.activation(cab[:, :], wTb[:, :], ACT.Square).then_inc(gsa_square_by_act, 1)
                        act.wait_ge(gsa_projected_by_pe, n * 8 + 12)
                        nc.scalar.activation(wTa[:, :], PS[0][:, :], ACT.Copy, scale=WCV[:, 11:12]).then_inc(gsa_conv0_by_act, 1)
                        act.wait_ge(gsa_conv_by_dve, n * 23 + 29)
                        nc.scalar.activation(vTb[:, :], vTb[:, :], ACT.Silu)
                        nc.scalar.activation(right(LBb[:, 0, :], 1), right(wTb[:, :], 1), ACT.Copy)
                        act.wait_ge(gsa_projected_by_pe, n * 8 + 13)
                        nc.scalar.activation(kTb[:, :], PS[6][:, :], ACT.Copy, scale=WCV[:, 7:8]).then_inc(gsa_conv0_by_act, 1)
                        act.wait_ge(gsa_projected_by_pe, n * 8 + 14)
                        nc.scalar.activation(vTa[:, :], PS[3][:, :], ACT.Copy, scale=WCV[:, 11:12]).then_inc(gsa_conv0_by_act, 1)
                        act.wait_ge(gsa_conv_by_dve, n * 23 + 34)
                        nc.scalar.activation(wTa[:, :], wTa[:, :], ACT.Silu).then_inc(gsa_silu_by_act, 1)
                        act.wait_ge(gsa_silu_by_act, n * 4 + 2)
                        nc.scalar.activation(caa[:, :], wTa[:, :], ACT.Square)
                        nc.scalar.activation(right(LBa[:, 0, :], 1), right(wTa[:, :], 1), ACT.Copy)
                        act.wait_ge(gsa_projected_by_pe, n * 8 + 15)
                        nc.scalar.activation(kTa[:, :], PS[2][:, :], ACT.Copy, scale=WCV[:, 7:8]).then_inc(gsa_conv0_by_act, 1)
                        act.wait_ge(gsa_conv_by_dve, n * 23 + 37)
                        nc.scalar.activation(qTb[:, :], qTb[:, :], ACT.Silu)
                        act.wait_ge(gsa_projected_by_pe, n * 8 + 16)
                        nc.scalar.activation(qTa[:, :], PS[1][:, :], ACT.Copy, scale=WCV[:, 3:4]).then_inc(gsa_conv0_by_act, 1)
                        act.wait_ge(gsa_conv_by_dve, n * 23 + 38)
                        nc.scalar.activation(kTb[:, :], kTb[:, :], ACT.Silu).then_inc(gsa_silu_by_act, 1)
                        act.wait_ge(gsa_conv_by_dve, n * 23 + 41)
                        nc.scalar.activation(vTa[:, :], vTa[:, :], ACT.Silu)
                        act.wait_ge(gsa_forget_by_pe, n * 3 + 4)
                        nc.scalar.activation(preb[:, :], PS[4][:, :], ACT.Sigmoid).then_inc(gsa_sigmoid_by_act, 1)
                        act.wait_ge(gsa_sigmoid_by_act, n * 4 + 1)
                        nc.scalar.activation(packed(Rb[:, 0, :], 1), right(preb[:, :], 1), ACT.Copy).then_inc(gsa_kept_by_act, 1)
                        act.wait_ge(gsa_conv_by_dve, n * 23 + 45)
                        nc.scalar.activation(kTa[:, :], kTa[:, :], ACT.Silu)
                        act.wait_ge(gsa_conv_by_dve, n * 23 + 46)
                        nc.scalar.activation(qTa[:, :], qTa[:, :], ACT.Silu).then_inc(gsa_silu_by_act, 1)
                        act.wait_ge(gsa_forget_by_pe, n * 3 + 5)
                        nc.scalar.activation(prea[:, :], PS[0][:, :], ACT.Sigmoid).then_inc(gsa_sigmoid_by_act, 1)
                        act.wait_ge(gsa_strength_by_pool, n * 2 + 1)
                        for j in range(4):
                            last = nc.scalar.activation(tile(cab, j), tile(PS[6], j), ACT.Copy, scale=c4b[:, j:j + 1])
                        last.then_inc(gsa_keyquery_by_act, 1)
                        act.wait_ge(gsa_strength_by_pool, n * 2 + 2)
                        act.wait_ge(gsa_keyquery_by_pe, n * 1 + 1)
                        for j in range(4):
                            last = nc.scalar.activation(tile(caa, j), tile(PS[2], j), ACT.Copy, scale=c4a[:, j:j + 1])
                        last.then_inc(gsa_keyquery_by_act, 1)
                        act.wait_ge(gsa_sigmoid_by_act, n * 4 + 2)
                        nc.scalar.activation(packed(Ra[:, 0, :], 1), right(prea[:, :], 1), ACT.Copy).then_inc(gsa_kept_by_act, 1)
                        nc.scalar.activation(sgb[:, :], PS[5][:, :], ACT.Sigmoid, bias=BG[:, bass.ds(h, 1)]).then_inc(gsa_sigmoid_by_act, 1)
                        nc.scalar.activation(LTb[:, 0, :], PS[4][:, :], ACT.Copy).then_inc(gsa_turned_by_act, 1)
                        act.wait_ge(gsa_decay_by_dve, n * 16 + 2)
                        nc.scalar.activation(packed(Rb[:, 1, :], 2), right(preb[:, :], 2), ACT.Copy).then_inc(gsa_kept_by_act, 1)
                        act.wait_ge(gsa_values_by_pe, n * 2 + 1)
                        for j in range(4):
                            last = nc.scalar.activation(tile(Vb, j), tile(PS[7], j), ACT.Copy, scale=c4b[:, j:j + 1])
                        last.then_inc(gsa_values_by_act, 1)
                        act.wait_ge(gsa_forget_by_pe, n * 3 + 6)
                        act.sem_inc(gsa_act_passed, 1)
                        nc.scalar.activation(sga[:, :], PS[1][:, :], ACT.Sigmoid, bias=BG[:, bass.ds(h, 1)]).then_inc(gsa_sigmoid_by_act, 1)
                        nc.scalar.activation(right(LBb[:, 1, :], 2), right(LBb[:, 0, :], 2), ACT.Copy).then_inc(gsa_decay_by_act, 1)
                        act.wait_ge(gsa_decay_by_dve, n * 16 + 4)
                        nc.scalar.activation(packed(Ra[:, 1, :], 2), right(prea[:, :], 2), ACT.Copy).then_inc(gsa_kept_by_act, 1)
                        act.wait_ge(gsa_turned_by_pe, n * 6 + 1)
                        nc.scalar.activation(LTa[:, 0, :], PS[0][:, :], ACT.Copy).then_inc(gsa_turned_by_act, 1)
                        act.wait_ge(gsa_decay_by_dve, n * 16 + 5)
                        nc.scalar.activation(packed(Rb[:, 2, :], 4), right(preb[:, :], 4), ACT.Copy).then_inc(gsa_kept_by_act, 1)
                        nc.scalar.activation(right(LBa[:, 1, :], 2), right(LBa[:, 0, :], 2), ACT.Copy).then_inc(gsa_decay_by_act, 1)
                        act.wait_ge(gsa_values_by_pe, n * 2 + 2)
                        for j in range(4):
                            last = nc.scalar.activation(tile(Va, j), tile(PS[3], j), ACT.Copy, scale=c4a[:, j:j + 1])
                        last.then_inc(gsa_values_by_act, 1)
                        act.wait_ge(gsa_turned_by_pe, n * 6 + 2)
                        nc.scalar.activation(LTb[:, 1, :], PS[5][:, :], ACT.Copy)
                        act.wait_ge(gsa_slots_by_pe, n * 14 + 1)
                        nc.scalar.activation(Sb[:, :], PS[6][:, :], ACT.Copy).then_inc(gsa_slots_by_act, 1)
                        act.wait_ge(gsa_decay_by_act, n * 6 + 1)
                        nc.scalar.activation(right(LBb[:, 2, :], 4), right(LBb[:, 1, :], 4), ACT.Copy).then_inc(gsa_decay_by_act, 1)
                        act.wait_ge(gsa_decay_by_dve, n * 16 + 7)
                        nc.scalar.activation(packed(Ra[:, 2, :], 4), right(prea[:, :], 4), ACT.Copy).then_inc(gsa_kept_by_act, 1)
                        act.wait_ge(gsa_turned_by_pe, n * 6 + 3)
                        nc.scalar.activation(LTa[:, 1, :], PS[1][:, :], ACT.Copy)
                        act.wait_ge(gsa_decay_by_act, n * 6 + 2)
                        nc.scalar.activation(right(LBa[:, 2, :], 4), right(LBa[:, 1, :], 4), ACT.Copy).then_inc(gsa_decay_by_act, 1)
                        act.wait_ge(gsa_decay_by_dve, n * 16 + 8)
                        nc.scalar.activation(packed(Rb[:, 3, :], 8), right(preb[:, :], 8), ACT.Copy).then_inc(gsa_kept_by_act, 1)
                        act.wait_ge(gsa_slots_by_pe, n * 14 + 3)
                        nc.scalar.activation(Sa[:, :], PS[2][:, :], ACT.Copy).then_inc(gsa_slots_by_act, 1)
                        act.wait_ge(gsa_decay_by_act, n * 6 + 3)
                        nc.scalar.activation(right(LBb[:, 3, :], 8), right(LBb[:, 2, :], 8), ACT.Copy).then_inc(gsa_decay_by_act, 1)
                        nc.scalar.activation(LTb[:, 0, :], PS[4][:, :], ACT.Copy).then_inc(gsa_turned_by_act, 1)
                        act.wait_ge(gsa_decay_by_dve, n * 16 + 11)
                        nc.scalar.activation(packed(Ra[:, 3, :], 8), right(prea[:, :], 8), ACT.Copy).then_inc(gsa_kept_by_act, 1)
                        act.wait_ge(gsa_decay_by_act, n * 6 + 5)
                        nc.scalar.activation(right(LBb[:, 4, :], 16), right(LBb[:, 3, :], 16), ACT.Copy)
                        act.wait_ge(gsa_turned_by_pe, n * 6 + 4)
                        nc.scalar.activation(LTb[:, 1, :], PS[5][:, :], ACT.Copy).then_inc(gsa_turned_by_act, 1)
                        nc.scalar.activation(right(LBa[:, 3, :], 8), right(LBa[:, 2, :], 8), ACT.Copy).then_inc(gsa_decay_by_act, 1)
                        nc.scalar.activation(LTa[:, 0, :], PS[0][:, :], ACT.Copy).then_inc(gsa_turned_by_act, 1)
                        act.wait_ge(gsa_decay_by_dve, n * 16 + 12)
                        act.wait_ge(gsa_decay_by_act, n * 6 + 6)
                        nc.scalar.activation(right(LBa[:, 4, :], 16), right(LBa[:, 3, :], 16), ACT.Copy)
                        act.wait_ge(gsa_slots_by_pe, n * 14 + 6)
                        nc.scalar.activation(LTa[:, 1, :], PS[1][:, :], ACT.Copy).then_inc(gsa_turned_by_act, 1)
                        act.wait_ge(gsa_slots_by_pe, n * 14 + 7)
                        nc.scalar.activation(LTb[:, 0, :], PS[4][:, :], ACT.Copy).then_inc(gsa_turned_by_act, 1)
                        act.wait_ge(gsa_turned_by_pe, n * 6 + 5)
                        nc.scalar.activation(LTb[:, 1, :], PS[5][:, :], ACT.Copy).then_inc(gsa_turned_by_act, 1)
                        nc.scalar.activation(packed(Rb[:, 4, :], 16), right(preb[:, :], 16), ACT.Copy).then_inc(gsa_kept_by_act, 1)
                        act.wait_ge(gsa_turned_by_pe, n * 6 + 6)
                        nc.scalar.activation(LTa[:, 0, :], PS[0][:, :], ACT.Copy).then_inc(gsa_turned_by_act, 1)
                        act.wait_ge(gsa_decay_by_dve, n * 16 + 15)
                        nc.scalar.activation(packed(Ra[:, 4, :], 16), right(prea[:, :], 16), ACT.Copy).then_inc(gsa_kept_by_act, 1)
                        act.wait_ge(gsa_slots_by_pe, n * 14 + 10)
                        nc.scalar.activation(LTa[:, 1, :], PS[1][:, :], ACT.Copy).then_inc(gsa_turned_by_act, 1)
                        act.wait_ge(gsa_softmax_by_dve, n * 4 + 2)
                        for j in range(4):
                            last = nc.scalar.activation(tile(ab, j), tile(PS[4], j), ACT.Exp, bias=nmxb[:, j:j + 1], scale=SCALE, accum_out=denb[:, j:j + 1])
                        last.then_inc(gsa_softmax_by_act, 1)
                        act.wait_ge(gsa_softmax_by_dve, n * 4 + 4)
                        for j in range(4):
                            last = nc.scalar.activation(tile(aa, j), tile(PS[0], j), ACT.Exp, bias=nmxa[:, j:j + 1], scale=SCALE, accum_out=dena[:, j:j + 1])
                        last.then_inc(gsa_softmax_by_act, 1)
                        act.wait_ge(gsa_softmax_by_pe, n * 4 + 3)
                        nc.scalar.activation(aTb[:, :], PS[5][:, :], ACT.Copy).then_inc(gsa_softmax_by_act, 1)
                        act.wait_ge(gsa_softmax_by_pe, n * 4 + 4)
                        nc.scalar.activation(aTa[:, :], PS[1][:, :], ACT.Copy).then_inc(gsa_softmax_by_act, 1)
                        act.wait_ge(gsa_read_by_pe, n * 2 + 1)
                        nc.scalar.activation(aTb[:, :], PS[6][:, :], ACT.Square).then_inc(gsa_osquare_by_act, 1)
                        act.wait_ge(gsa_read_by_pe, n * 2 + 2)
                        nc.scalar.activation(aTa[:, :], PS[2][:, :], ACT.Square).then_inc(gsa_osquare_by_act, 1)

            @block.gpsimd
            def _(pool):
                nc.gpsimd.memset(NEGHALF[:, :], -0.5)
                nc.gpsimd.memset(ones[:, :], 1.0).then_inc(gsa_setup_by_pool, 1)
                pool.wait_ge(gsa_setup_by_pool, 1)
                pool.wait_ge(gsa_setup_loads_sp, 64)
                with pool.Fori(0, 16) as h:
                    with pool.Fori(0, 4) as gp:
                        n = h * 4 + gp
                        pool.wait_ge(gsa_wnorm_by_dve, n * 2 + 1)
                        nc.gpsimd.tensor_tensor(ssb[:, :], ssb[:, :], NEGHALF[:, :], ALU.pow).then_inc(gsa_wnorm_by_pool, 1)
                        pool.wait_ge(gsa_wnorm_by_dve, n * 2 + 2)
                        nc.gpsimd.tensor_tensor(ssa[:, :], ssa[:, :], NEGHALF[:, :], ALU.pow).then_inc(gsa_wnorm_by_pool, 1)
                        pool.wait_ge(gsa_wnorm_by_pool, n * 2 + 1)
                        nc.gpsimd.tensor_tensor(c4b[:, :], ssb[:, :], BETA2[:, bass.ds(n * 8 + 4, 4)], ALU.mult).then_inc(gsa_strength_by_pool, 1)
                        pool.wait_ge(gsa_wnorm_by_pool, n * 2 + 2)
                        nc.gpsimd.tensor_tensor(c4a[:, :], ssa[:, :], BETA2[:, bass.ds(n * 8 + 0, 4)], ALU.mult).then_inc(gsa_strength_by_pool, 1)
                        pool.wait_ge(gsa_keyquery_by_act, n * 2 + 1)
                        nc.gpsimd.tensor_tensor(ADb[:, :], cab[:, :], EYES[:, :], ALU.mult).then_inc(gsa_masked_by_pool, 1)
                        nc.gpsimd.tensor_tensor(packed(AMb[:, 0, :], 1), right(cab[:, :], 1), packed(MASKS[:, 0, :], 1), ALU.mult).then_inc(gsa_masked_by_pool, 1)
                        pool.wait_ge(gsa_keyquery_by_act, n * 2 + 2)
                        nc.gpsimd.tensor_tensor(ADa[:, :], caa[:, :], EYES[:, :], ALU.mult).then_inc(gsa_masked_by_pool, 1)
                        nc.gpsimd.tensor_tensor(packed(AMb[:, 1, :], 2), right(cab[:, :], 2), packed(MASKS[:, 1, :], 2), ALU.mult)
                        nc.gpsimd.tensor_tensor(packed(AMa[:, 0, :], 1), right(caa[:, :], 1), packed(MASKS[:, 0, :], 1), ALU.mult).then_inc(gsa_masked_by_pool, 1)
                        nc.gpsimd.tensor_tensor(packed(AMa[:, 1, :], 2), right(caa[:, :], 2), packed(MASKS[:, 1, :], 2), ALU.mult).then_inc(gsa_masked_by_pool, 1)
                        nc.gpsimd.tensor_tensor(packed(AMb[:, 2, :], 4), right(cab[:, :], 4), packed(MASKS[:, 2, :], 4), ALU.mult).then_inc(gsa_masked_by_pool, 1)
                        nc.gpsimd.tensor_tensor(packed(AMb[:, 3, :], 8), right(cab[:, :], 8), packed(MASKS[:, 3, :], 8), ALU.mult).then_inc(gsa_masked_by_pool, 1)
                        nc.gpsimd.tensor_tensor(packed(AMa[:, 2, :], 4), right(caa[:, :], 4), packed(MASKS[:, 2, :], 4), ALU.mult).then_inc(gsa_masked_by_pool, 1)
                        nc.gpsimd.tensor_tensor(packed(AMa[:, 3, :], 8), right(caa[:, :], 8), packed(MASKS[:, 3, :], 8), ALU.mult).then_inc(gsa_masked_by_pool, 1)
                        nc.gpsimd.tensor_tensor(packed(AMb[:, 4, :], 16), right(cab[:, :], 16), packed(MASKS[:, 4, :], 16), ALU.mult).then_inc(gsa_masked_by_pool, 1)
                        nc.gpsimd.tensor_tensor(packed(AMb[:, 5, :], 32), right(cab[:, :], 32), packed(MASKS[:, 5, :], 32), ALU.mult).then_inc(gsa_masked_by_pool, 1)
                        nc.gpsimd.tensor_tensor(packed(AMa[:, 4, :], 16), right(caa[:, :], 16), packed(MASKS[:, 4, :], 16), ALU.mult).then_inc(gsa_masked_by_pool, 1)
                        nc.gpsimd.tensor_tensor(packed(AMa[:, 5, :], 32), right(caa[:, :], 32), packed(MASKS[:, 5, :], 32), ALU.mult).then_inc(gsa_masked_by_pool, 1)
                        pool.wait_ge(gsa_softmax_by_act, n * 4 + 1)
                        nc.gpsimd.tensor_tensor(den2b[:, :], denb[:, :], denb[:, :], ALU.mult).then_inc(gsa_onorm_by_pool, 1)
                        pool.wait_ge(gsa_softmax_by_act, n * 4 + 2)
                        nc.gpsimd.tensor_tensor(den2a[:, :], dena[:, :], dena[:, :], ALU.mult).then_inc(gsa_onorm_by_pool, 1)
                        pool.wait_ge(gsa_softmax_by_act, n * 4 + 3)
                        nc.gpsimd.tensor_tensor(packed(aRb[:, 1, :], 2), right(aTb[:, :], 2), packed(Rb[:, 1, :], 2), ALU.mult).then_inc(gsa_reach_by_pool, 1)
                        nc.gpsimd.tensor_tensor(packed(aRb[:, 3, :], 8), right(aTb[:, :], 8), packed(Rb[:, 3, :], 8), ALU.mult)
                        pool.wait_ge(gsa_softmax_by_act, n * 4 + 4)
                        nc.gpsimd.tensor_tensor(packed(aRa[:, 1, :], 2), right(aTa[:, :], 2), packed(Ra[:, 1, :], 2), ALU.mult).then_inc(gsa_reach_by_pool, 1)
                        nc.gpsimd.tensor_tensor(packed(aRa[:, 3, :], 8), right(aTa[:, :], 8), packed(Ra[:, 3, :], 8), ALU.mult).then_inc(gsa_reach_by_pool, 1)
                        nc.gpsimd.tensor_tensor(packed(aRb[:, 5, :], 32), right(aTb[:, :], 32), right(preb[:, :], 32), ALU.mult).then_inc(gsa_reach_by_pool, 1)
                        nc.gpsimd.tensor_tensor(packed(aRa[:, 5, :], 32), right(aTa[:, :], 32), right(prea[:, :], 32), ALU.mult).then_inc(gsa_reach_by_pool, 1)
                        pool.wait_ge(gsa_onorm_by_dve, n * 2 + 1)
                        nc.gpsimd.tensor_tensor(r4b[:, :], r0b[:, :], NEGHALF[:, :], ALU.pow).then_inc(gsa_onorm_by_pool, 1)
                        pool.wait_ge(gsa_onorm_by_dve, n * 2 + 2)
                        nc.gpsimd.tensor_tensor(r4a[:, :], r0a[:, :], NEGHALF[:, :], ALU.pow).then_inc(gsa_onorm_by_pool, 1)

            @block.sync
            def _(sp):
                nc.sync.dma_start(BG[:, :], io["bg2"]).then_inc(gsa_setup_loads_sp, 16)
                nc.sync.dma_start(NW[:, :], io["norm_w"]).then_inc(gsa_setup_loads_sp, 16)
                nc.sync.dma_start(MASKS[:, :, :], io["masks"]).then_inc(gsa_setup_loads_sp, 16)
                nc.sync.dma_start(EYES[:, :], io["eyes"]).then_inc(gsa_setup_loads_sp, 16)
                sp.wait_ge(gsa_setup_by_pool, 1)
                sp.wait_ge(gsa_setup_loads_sp, 64)
                with sp.Fori(0, 16) as h:
                    with sp.Fori(0, 4) as gp:
                        n = h * 4 + gp
                        sp.wait_ge(gsa_projected_by_pe, n * 8 + 8)
                        nc.sync.dma_start(WA[:, :, :].rearrange("p c n -> p (c n)"), io["w_heads"][:, bass.ds(h * 1024, 1024)]).then_inc(gsa_proj_weights_dma, 16)
                        sp.wait_ge(gsa_conv_by_dve, n * 23 + 23)
                        nc.sync.dma_start(WCV[:, :], io["w_conv"][:, bass.ds(h * 12, 12)]).then_inc(gsa_conv_weights_dma, 16)
                        sp.wait_ge(gsa_forget_by_pe, n * 3 + 3)
                        nc.sync.dma_start(WFG[:, :], io["w_gates"][:, bass.ds(h * 256, 256)]).then_inc(gsa_gate_weights_dma, 16)
                        sp.wait_ge(gsa_output_by_pe, n * 2 + 2)
                        nc.sync.dma_start(WO[:, :], io["wo_heads"][:, bass.ds(h * 256, 256)]).then_inc(gsa_out_weights_dma, 16)

        nc.clear_and_free_semaphores(signals)
        nc.all_engine_barrier()

def mlstm(nc, io, X, PS, IDENT, shared):
    ctx = ExitStack()
    with ctx:
        def sb(name, shape, dt=F32):
            return ctx.enter_context(nc.sbuf_tensor("mlstm_" + name, shape, dt))

        signals = []

        def signal(name):
            signals.append(nc.alloc_semaphore(name))
            return signals[-1]

        statsa = sb("statsa", [128, 6])
        mva = sb("mva", [128, 2])
        varea = sb("varea", [128, 1])
        rstda = sb("rstda", [128, 1])
        xna = sb("xna", [128, 256])
        qTa = sb("qTa", [128, 2, 128])
        HXa = sb("HXa", [128, 16, 128])
        kTa = sb("kTa", [128, 2, 128])
        VXa = sb("VXa", [128, 16, 17])
        SCa = sb("SCa", [128, 16, 128])
        PWa = sb("PWa", [128, 16, 128])
        ctx_a = sb("ctx_a", [128, 256])
        cTa = sb("cTa", [128, 2, 128])
        xTa = sb("xTa", [128, 2, 128])
        rda = sb("rda", [128, 16])
        mxa = sb("mxa", [128, 16])
        nmxa = sb("nmxa", [128, 16])
        cxa = sb("cxa", [128, 256])
        fa = sb("fa", [16, 128])
        f2a = sb("f2a", [16, 128])
        lfa = sb("lfa", [16, 128])
        Fa = sb("Fa", [16, 128])
        ua = sb("ua", [16, 128])
        Ma = sb("Ma", [16, 128])
        FMa = sb("FMa", [16, 128])
        uTa = sb("uTa", [128, 16])
        eTa = sb("eTa", [128, 16])
        rna = sb("rna", [128, 16])
        mua = sb("mua", [128, 16])
        vara = sb("vara", [128, 16])
        rsa = sb("rsa", [128, 16])
        hha = sb("hha", [128, 256])
        hca = sb("hca", [128, 256])
        hqa = sb("hqa", [128, 256])
        statsb = sb("statsb", [128, 6])
        mvb = sb("mvb", [128, 2])
        vareb = sb("vareb", [128, 1])
        rstdb = sb("rstdb", [128, 1])
        xnb = sb("xnb", [128, 256])
        qTb = sb("qTb", [128, 2, 128])
        HXb = sb("HXb", [128, 16, 128])
        kTb = sb("kTb", [128, 2, 128])
        VXb = sb("VXb", [128, 16, 17])
        SCb = sb("SCb", [128, 16, 128])
        PWb = sb("PWb", [128, 16, 128])
        ctx_b = sb("ctx_b", [128, 256])
        cTb = sb("cTb", [128, 2, 128])
        xTb = sb("xTb", [128, 2, 128])
        rdb = sb("rdb", [128, 16])
        mxb = sb("mxb", [128, 16])
        nmxb = sb("nmxb", [128, 16])
        cxb = sb("cxb", [128, 256])
        fb = sb("fb", [16, 128])
        f2b = sb("f2b", [16, 128])
        lfb = sb("lfb", [16, 128])
        Fb = sb("Fb", [16, 128])
        ub = sb("ub", [16, 128])
        Mb = sb("Mb", [16, 128])
        FMb = sb("FMb", [16, 128])
        uTb = sb("uTb", [128, 16])
        eTb = sb("eTb", [128, 16])
        rnb = sb("rnb", [128, 16])
        mub = sb("mub", [128, 16])
        varb = sb("varb", [128, 16])
        rsb = sb("rsb", [128, 16])
        hhb = sb("hhb", [128, 256])
        hcb = sb("hcb", [128, 256])
        hqb = sb("hqb", [128, 256])
        NEGHALF = sb("neghalf", [128, 16])
        HM = sb("hm", [128, 8])
        onerow = sb("onerow", [1, 128])
        WIF = sb("WIF", [128, 6, 32])
        BIF = sb("BIF", [16, 2])
        RST = sb("RST", [16, 256])
        SEL = sb("SEL", [16, 2048])
        NMASK = sb("NMASK", [128, 512])
        LNS = sb("LNS", [1, 256])
        LNB = sb("lnb", [128, 256])
        def by_head(t):
            return t.rearrange("p (h d) -> p h d", d=16)

        mlstm_setup_by_pool = signal("mlstm_setup_by_pool")
        mlstm_setup_loads_sp = signal("mlstm_setup_loads_sp")
        mlstm_setup_by_pe = signal("mlstm_setup_by_pe")
        mlstm_setup_by_dve = signal("mlstm_setup_by_dve")
        mlstm_norm_by_dve = signal("mlstm_norm_by_dve")
        mlstm_context_b_dma = signal("mlstm_context_b_dma")
        mlstm_context_a_dma = signal("mlstm_context_a_dma")
        mlstm_turned_by_pe = signal("mlstm_turned_by_pe")
        mlstm_values_by_dve = signal("mlstm_values_by_dve")
        mlstm_rstd_by_pool = signal("mlstm_rstd_by_pool")
        mlstm_normed_by_dve = signal("mlstm_normed_by_dve")
        mlstm_turned_by_act = signal("mlstm_turned_by_act")
        mlstm_gates_by_pe = signal("mlstm_gates_by_pe")
        mlstm_expand_by_pool = signal("mlstm_expand_by_pool")
        mlstm_gates_by_dve = signal("mlstm_gates_by_dve")
        mlstm_logf_by_act = signal("mlstm_logf_by_act")
        mlstm_scan_by_dve = signal("mlstm_scan_by_dve")
        mlstm_maxima_by_pe = signal("mlstm_maxima_by_pe")
        mlstm_gturn_by_pe = signal("mlstm_gturn_by_pe")
        mlstm_gturn_by_dve = signal("mlstm_gturn_by_dve")
        mlstm_floor_by_act = signal("mlstm_floor_by_act")
        mlstm_masked_by_dve = signal("mlstm_masked_by_dve")
        mlstm_scores_by_pe = signal("mlstm_scores_by_pe")
        mlstm_exp_by_act = signal("mlstm_exp_by_act")
        mlstm_weighted_by_dve = signal("mlstm_weighted_by_dve")
        mlstm_attended_by_pe = signal("mlstm_attended_by_pe")
        mlstm_normalize_by_dve = signal("mlstm_normalize_by_dve")
        mlstm_headnorm_by_dve = signal("mlstm_headnorm_by_dve")
        mlstm_headsq_by_pool = signal("mlstm_headsq_by_pool")
        mlstm_residual_by_dve = signal("mlstm_residual_by_dve")
        mlstm_sp_passed = signal("mlstm_sp_passed")
        mlstm_pe_passed = signal("mlstm_pe_passed")
        mlstm_dve_passed = signal("mlstm_dve_passed")
        with nc.Block() as block:

            @block.tensor
            def _(pe):
                pe.wait_ge(mlstm_setup_loads_sp, 112)
                pe.wait_ge(mlstm_setup_by_pool, 1)
                nc.tensor.matmul(PS[0][:, 0:256], onerow[0:1, :], LNS[0:1, :], start=True, stop=True).then_inc(mlstm_setup_by_pe, 1)
                pe.sem_inc(mlstm_turned_by_pe, 4)
                pe.wait_ge(mlstm_setup_by_pool, 2)
                pe.wait_ge(mlstm_setup_loads_sp, 112)
                pe.wait_ge(mlstm_setup_by_pe, 1)
                pe.wait_ge(mlstm_setup_by_dve, 1)
                with pe.Fori(0, 16) as i:
                    n = i
                    pe.wait_ge(mlstm_context_b_dma, n * 16 + 16)
                    for c in range(2):
                        last = nc.tensor.transpose(PS[5][:, c * 128:(c + 1) * 128], cxb[:, c * 128:(c + 1) * 128], IDENT[:, :])
                    last.then_inc(mlstm_turned_by_pe, 1)
                    pe.wait_ge(mlstm_context_a_dma, n * 16 + 16)
                    for c in range(2):
                        last = nc.tensor.transpose(PS[1][:, c * 128:(c + 1) * 128], cxa[:, c * 128:(c + 1) * 128], IDENT[:, :])
                    last.then_inc(mlstm_turned_by_pe, 1)
                    pe.wait_ge(mlstm_normed_by_dve, n * 2 + 1)
                    for c in range(2):
                        last = nc.tensor.transpose(PS[0][:, c * 128:(c + 1) * 128], xna[:, c * 128:(c + 1) * 128], IDENT[:, :])
                    last.then_inc(mlstm_turned_by_pe, 1)
                    pe.wait_ge(mlstm_normed_by_dve, n * 2 + 2)
                    for c in range(2):
                        last = nc.tensor.transpose(PS[4][:, c * 128:(c + 1) * 128], xnb[:, c * 128:(c + 1) * 128], IDENT[:, :])
                    last.then_inc(mlstm_turned_by_pe, 1)
                    pe.wait_ge(mlstm_turned_by_act, n * 2 + 1)
                    for k, col in ((0, 0), (1, 128)):
                        for c in range(6):
                            src = qTa if c < 2 else kTa
                            last = nc.tensor.matmul(PS[2][0:16, col:col + 128], WIF[:, c, k * 16:(k + 1) * 16], src[:, c % 2, :], start=(c == 0), stop=(c == 5))
                    last.then_inc(mlstm_gates_by_pe, 1)
                    pe.wait_ge(mlstm_turned_by_act, n * 2 + 2)
                    for k, col in ((0, 0), (1, 128)):
                        for c in range(6):
                            src = qTb if c < 2 else kTb
                            last = nc.tensor.matmul(PS[6][0:16, col:col + 128], WIF[:, c, k * 16:(k + 1) * 16], src[:, c % 2, :], start=(c == 0), stop=(c == 5))
                    last.then_inc(mlstm_gates_by_pe, 1)
                    pe.wait_ge(mlstm_scan_by_dve, n * 10 + 4)
                    for k in range(4):
                        head = 0 + k
                        last = nc.tensor.matmul(PS[0][:, k * 128:(k + 1) * 128], SEL[:, head * 128:(head + 1) * 128], Ma[:, :], start=True, stop=True)
                    last.then_inc(mlstm_maxima_by_pe, 1)
                    pe.wait_ge(mlstm_scan_by_dve, n * 10 + 5)
                    pe.sem_inc(mlstm_pe_passed, 1)
                    nc.tensor.transpose(PS[2][:, 256:272], ua[:, :], IDENT[0:16, 0:16])
                    last = nc.tensor.transpose(PS[2][:, 272:288], FMa[:, :], IDENT[0:16, 0:16])
                    last.then_inc(mlstm_gturn_by_pe, 1)
                    for k in range(4):
                        head = 4 + k
                        last = nc.tensor.matmul(PS[1][:, k * 128:(k + 1) * 128], SEL[:, head * 128:(head + 1) * 128], Ma[:, :], start=True, stop=True)
                    last.then_inc(mlstm_maxima_by_pe, 1)
                    for k in range(4):
                        head = 12 + k
                        last = nc.tensor.matmul(PS[3][:, k * 128:(k + 1) * 128], SEL[:, head * 128:(head + 1) * 128], Ma[:, :], start=True, stop=True)
                    last.then_inc(mlstm_maxima_by_pe, 1)
                    pe.wait_ge(mlstm_scan_by_dve, n * 10 + 9)
                    for k in range(4):
                        head = 0 + k
                        last = nc.tensor.matmul(PS[4][:, k * 128:(k + 1) * 128], SEL[:, head * 128:(head + 1) * 128], Mb[:, :], start=True, stop=True)
                    last.then_inc(mlstm_maxima_by_pe, 1)
                    pe.wait_ge(mlstm_scan_by_dve, n * 10 + 10)
                    pe.sem_inc(mlstm_pe_passed, 1)
                    nc.tensor.transpose(PS[6][:, 256:272], ub[:, :], IDENT[0:16, 0:16])
                    last = nc.tensor.transpose(PS[6][:, 272:288], FMb[:, :], IDENT[0:16, 0:16])
                    last.then_inc(mlstm_gturn_by_pe, 1)
                    for k in range(4):
                        head = 4 + k
                        last = nc.tensor.matmul(PS[5][:, k * 128:(k + 1) * 128], SEL[:, head * 128:(head + 1) * 128], Mb[:, :], start=True, stop=True)
                    last.then_inc(mlstm_maxima_by_pe, 1)
                    for k in range(4):
                        head = 12 + k
                        last = nc.tensor.matmul(PS[7][:, k * 128:(k + 1) * 128], SEL[:, head * 128:(head + 1) * 128], Mb[:, :], start=True, stop=True)
                    last.then_inc(mlstm_maxima_by_pe, 1)
                    pe.wait_ge(mlstm_floor_by_act, n * 2 + 1)
                    for k in range(4):
                        head = 8 + k
                        last = nc.tensor.matmul(PS[2][:, k * 128:(k + 1) * 128], SEL[:, head * 128:(head + 1) * 128], Ma[:, :], start=True, stop=True)
                    last.then_inc(mlstm_maxima_by_pe, 1)
                    pe.wait_ge(mlstm_masked_by_dve, n * 6 + 3)
                    for k in range(2):
                        last = nc.tensor.matmul(PS[4 + k][:, :], kTb[:, 0, :], HXb[:, 0 + 4 * k:0 + 4 * k + 4, :], start=True, stop=True)
                    last.then_inc(mlstm_scores_by_pe, 1)
                    pe.wait_ge(mlstm_floor_by_act, n * 2 + 2)
                    for k in range(4):
                        head = 8 + k
                        last = nc.tensor.matmul(PS[6][:, k * 128:(k + 1) * 128], SEL[:, head * 128:(head + 1) * 128], Mb[:, :], start=True, stop=True)
                    last.then_inc(mlstm_maxima_by_pe, 1)
                    pe.wait_ge(mlstm_expand_by_pool, n * 2 + 1)
                    pe.wait_ge(mlstm_masked_by_dve, n * 6 + 5)
                    for k in range(2):
                        last = nc.tensor.matmul(PS[2 + k][:, :], kTa[:, 1, :], HXa[:, 8 + 4 * k:8 + 4 * k + 4, :], start=True, stop=True)
                    last.then_inc(mlstm_scores_by_pe, 1)
                    pe.wait_ge(mlstm_expand_by_pool, n * 2 + 2)
                    pe.wait_ge(mlstm_masked_by_dve, n * 6 + 6)
                    for k in range(2):
                        last = nc.tensor.matmul(PS[6 + k][:, :], kTb[:, 1, :], HXb[:, 8 + 4 * k:8 + 4 * k + 4, :], start=True, stop=True)
                    last.then_inc(mlstm_scores_by_pe, 1)
                    for k in range(2):
                        last = nc.tensor.matmul(PS[0 + k][:, :], kTa[:, 0, :], HXa[:, 0 + 4 * k:0 + 4 * k + 4, :], start=True, stop=True)
                    last.then_inc(mlstm_scores_by_pe, 1)
                    pe.wait_ge(mlstm_weighted_by_dve, n * 2 + 1)
                    for head in range(16):
                        last = nc.tensor.matmul(PS[4][:, head * 17:head * 17 + 17], PWb[:, head, :], VXb[:, head, :], start=True, stop=True)
                    last.then_inc(mlstm_attended_by_pe, 1)
                    pe.wait_ge(mlstm_weighted_by_dve, n * 2 + 2)
                    for head in range(16):
                        last = nc.tensor.matmul(PS[0][:, head * 17:head * 17 + 17], PWa[:, head, :], VXa[:, head, :], start=True, stop=True)
                    last.then_inc(mlstm_attended_by_pe, 1)

            @block.vector
            def _(dve):
                dve.wait_ge(mlstm_setup_by_pe, 1)
                nc.vector.tensor_copy(LNB[:, :], PS[0][:, 0:256]).then_inc(mlstm_setup_by_dve, 1)
                dve.sem_inc(mlstm_values_by_dve, 2)
                dve.sem_inc(mlstm_residual_by_dve, 1)
                dve.wait_ge(mlstm_setup_by_pool, 2)
                dve.wait_ge(mlstm_setup_loads_sp, 112)
                dve.wait_ge(mlstm_setup_by_pe, 1)
                dve.wait_ge(mlstm_setup_by_dve, 1)
                with dve.Fori(0, 16) as i:
                    n = i
                    dve.wait_ge(mlstm_residual_by_dve, n * 1 + 1)
                    dve.sem_inc(mlstm_dve_passed, 1)
                    nc.vector.bn_stats(statsa[:, :], X[:, bass.ds((n * 2 + 0) * 256, 256)]).then_inc(mlstm_norm_by_dve, 1)
                    nc.vector.bn_stats(statsb[:, :], X[:, bass.ds((n * 2 + 1) * 256, 256)]).then_inc(mlstm_norm_by_dve, 1)
                    dve.wait_ge(mlstm_norm_by_dve, n * 6 + 1)
                    dve.sem_inc(mlstm_dve_passed, 1)
                    nc.vector.bn_aggr(mva[:, :], statsa[:, :]).then_inc(mlstm_norm_by_dve, 1)
                    dve.wait_ge(mlstm_norm_by_dve, n * 6 + 2)
                    dve.sem_inc(mlstm_dve_passed, 1)
                    nc.vector.bn_aggr(mvb[:, :], statsb[:, :]).then_inc(mlstm_norm_by_dve, 1)
                    dve.wait_ge(mlstm_norm_by_dve, n * 6 + 3)
                    nc.vector.tensor_scalar(varea[:, :], mva[:, 1:2], 1e-5, None, ALU.add).then_inc(mlstm_norm_by_dve, 1)
                    dve.wait_ge(mlstm_norm_by_dve, n * 6 + 4)
                    nc.vector.tensor_scalar(vareb[:, :], mvb[:, 1:2], 1e-5, None, ALU.add).then_inc(mlstm_norm_by_dve, 1)
                    dve.wait_ge(mlstm_context_b_dma, n * 16 + 16)
                    nc.vector.tensor_copy(VXb[:, :, 0:16], by_head(cxb[:, :])).then_inc(mlstm_values_by_dve, 1)
                    dve.wait_ge(mlstm_context_a_dma, n * 16 + 16)
                    nc.vector.tensor_copy(VXa[:, :, 0:16], by_head(cxa[:, :])).then_inc(mlstm_values_by_dve, 1)
                    dve.wait_ge(mlstm_rstd_by_pool, n * 2 + 1)
                    nc.vector.tensor_scalar(xna[:, :], X[:, bass.ds((n * 2 + 0) * 256, 256)], mva[:, 0:1], rstda[:, 0:1], ALU.subtract, ALU.mult).then_inc(mlstm_normed_by_dve, 1)
                    dve.wait_ge(mlstm_rstd_by_pool, n * 2 + 2)
                    nc.vector.tensor_scalar(xnb[:, :], X[:, bass.ds((n * 2 + 1) * 256, 256)], mvb[:, 0:1], rstdb[:, 0:1], ALU.subtract, ALU.mult).then_inc(mlstm_normed_by_dve, 1)
                    dve.wait_ge(mlstm_turned_by_act, n * 2 + 1)
                    nc.vector.tensor_tensor(HXa[:, 0:8, :], qTa[:, 0, :].unsqueeze(1).to_broadcast([128, 8, 128]),
                                           HM[:, :].unsqueeze(2).to_broadcast([128, 8, 128]), ALU.mult)
                    dve.wait_ge(mlstm_turned_by_act, n * 2 + 2)
                    nc.vector.tensor_tensor(HXb[:, 0:8, :], qTb[:, 0, :].unsqueeze(1).to_broadcast([128, 8, 128]),
                                           HM[:, :].unsqueeze(2).to_broadcast([128, 8, 128]), ALU.mult)
                    dve.wait_ge(mlstm_gates_by_pe, n * 2 + 1)
                    nc.vector.tensor_scalar(fa[:, :], PS[2][0:16, 128:256], BIF[:, 1:2], None, ALU.add).then_inc(mlstm_gates_by_dve, 1)
                    dve.wait_ge(mlstm_gates_by_pe, n * 2 + 2)
                    nc.vector.tensor_scalar(fb[:, :], PS[6][0:16, 128:256], BIF[:, 1:2], None, ALU.add).then_inc(mlstm_gates_by_dve, 1)
                    dve.wait_ge(mlstm_logf_by_act, n * 6 + 3)
                    nc.vector.scalar_tensor_tensor(lfa[:, :], fa[:, :], 0.0, f2a[:, :], ALU.min, ALU.subtract).then_inc(mlstm_scan_by_dve, 1)
                    dve.wait_ge(mlstm_scan_by_dve, n * 10 + 1)
                    nc.vector.tensor_tensor_scan(Fa[:, :], RST[:, 0:128], lfa[:, :], 0.0, ALU.mult, ALU.add).then_inc(mlstm_scan_by_dve, 1)
                    dve.wait_ge(mlstm_scan_by_dve, n * 10 + 2)
                    nc.vector.scalar_tensor_tensor(ua[:, :], PS[2][0:16, 0:128], BIF[:, 0:1], Fa[:, :], ALU.add, ALU.subtract).then_inc(mlstm_scan_by_dve, 1)
                    dve.wait_ge(mlstm_scan_by_dve, n * 10 + 3)
                    nc.vector.tensor_tensor_scan(Ma[:, :], RST[:, 128:256], ua[:, :], -1e30, ALU.add, ALU.max).then_inc(mlstm_scan_by_dve, 1)
                    dve.wait_ge(mlstm_scan_by_dve, n * 10 + 4)
                    nc.vector.tensor_tensor(FMa[:, :], Fa[:, :], Ma[:, :], ALU.add).then_inc(mlstm_scan_by_dve, 1)
                    dve.wait_ge(mlstm_maxima_by_pe, n * 8 + 1)
                    nc.vector.tensor_tensor(SCa[:, 0:4, :].rearrange("p k s -> p (k s)"), NMASK[:, :], PS[0][:, :], ALU.subtract)
                    dve.wait_ge(mlstm_logf_by_act, n * 6 + 6)
                    nc.vector.scalar_tensor_tensor(lfb[:, :], fb[:, :], 0.0, f2b[:, :], ALU.min, ALU.subtract).then_inc(mlstm_scan_by_dve, 1)
                    dve.wait_ge(mlstm_gturn_by_pe, n * 2 + 1)
                    nc.vector.tensor_copy(uTa[:, :], PS[2][:, 256:272]).then_inc(mlstm_gturn_by_dve, 1)
                    dve.wait_ge(mlstm_scan_by_dve, n * 10 + 6)
                    nc.vector.tensor_tensor_scan(Fb[:, :], RST[:, 0:128], lfb[:, :], 0.0, ALU.mult, ALU.add).then_inc(mlstm_scan_by_dve, 1)
                    dve.wait_ge(mlstm_scan_by_dve, n * 10 + 7)
                    nc.vector.scalar_tensor_tensor(ub[:, :], PS[6][0:16, 0:128], BIF[:, 0:1], Fb[:, :], ALU.add, ALU.subtract).then_inc(mlstm_scan_by_dve, 1)
                    dve.wait_ge(mlstm_scan_by_dve, n * 10 + 8)
                    nc.vector.tensor_tensor_scan(Mb[:, :], RST[:, 128:256], ub[:, :], -1e30, ALU.add, ALU.max).then_inc(mlstm_scan_by_dve, 1)
                    dve.wait_ge(mlstm_maxima_by_pe, n * 8 + 2)
                    nc.vector.tensor_tensor(SCa[:, 4:8, :].rearrange("p k s -> p (k s)"), NMASK[:, :], PS[1][:, :], ALU.subtract).then_inc(mlstm_masked_by_dve, 1)
                    dve.wait_ge(mlstm_scan_by_dve, n * 10 + 9)
                    nc.vector.tensor_tensor(FMb[:, :], Fb[:, :], Mb[:, :], ALU.add).then_inc(mlstm_scan_by_dve, 1)
                    dve.wait_ge(mlstm_maxima_by_pe, n * 8 + 3)
                    nc.vector.tensor_tensor(SCa[:, 12:16, :].rearrange("p k s -> p (k s)"), NMASK[:, :], PS[3][:, :], ALU.subtract).then_inc(mlstm_masked_by_dve, 1)
                    dve.wait_ge(mlstm_maxima_by_pe, n * 8 + 4)
                    nc.vector.tensor_tensor(SCb[:, 0:4, :].rearrange("p k s -> p (k s)"), NMASK[:, :], PS[4][:, :], ALU.subtract)
                    dve.wait_ge(mlstm_gturn_by_pe, n * 2 + 2)
                    nc.vector.tensor_copy(uTb[:, :], PS[6][:, 256:272]).then_inc(mlstm_gturn_by_dve, 1)
                    dve.wait_ge(mlstm_maxima_by_pe, n * 8 + 5)
                    nc.vector.tensor_tensor(SCb[:, 4:8, :].rearrange("p k s -> p (k s)"), NMASK[:, :], PS[5][:, :], ALU.subtract).then_inc(mlstm_masked_by_dve, 1)
                    dve.wait_ge(mlstm_maxima_by_pe, n * 8 + 6)
                    nc.vector.tensor_tensor(SCb[:, 12:16, :].rearrange("p k s -> p (k s)"), NMASK[:, :], PS[7][:, :], ALU.subtract).then_inc(mlstm_masked_by_dve, 1)
                    dve.wait_ge(mlstm_maxima_by_pe, n * 8 + 7)
                    nc.vector.tensor_tensor(SCa[:, 8:12, :].rearrange("p k s -> p (k s)"), NMASK[:, :], PS[2][:, :], ALU.subtract).then_inc(mlstm_masked_by_dve, 1)
                    dve.wait_ge(mlstm_scores_by_pe, n * 4 + 1)
                    dve.wait_ge(mlstm_exp_by_act, n * 4 + 1)
                    nc.vector.tensor_tensor(PWb[:, 0:4, :].rearrange("p k s -> p (k s)"), SCb[:, 0:4, :].rearrange("p k s -> p (k s)"), PS[4][:, :], ALU.mult)
                    dve.wait_ge(mlstm_maxima_by_pe, n * 8 + 8)
                    nc.vector.tensor_tensor(SCb[:, 8:12, :].rearrange("p k s -> p (k s)"), NMASK[:, :], PS[6][:, :], ALU.subtract).then_inc(mlstm_masked_by_dve, 1)
                    dve.wait_ge(mlstm_exp_by_act, n * 4 + 2)
                    nc.vector.tensor_tensor(PWb[:, 4:8, :].rearrange("p k s -> p (k s)"), SCb[:, 4:8, :].rearrange("p k s -> p (k s)"), PS[5][:, :], ALU.mult)
                    dve.wait_ge(mlstm_scores_by_pe, n * 4 + 2)
                    nc.vector.tensor_tensor(PWa[:, 12:16, :].rearrange("p k s -> p (k s)"), SCa[:, 12:16, :].rearrange("p k s -> p (k s)"), PS[3][:, :], ALU.mult)
                    dve.wait_ge(mlstm_scores_by_pe, n * 4 + 3)
                    nc.vector.tensor_tensor(PWb[:, 12:16, :].rearrange("p k s -> p (k s)"), SCb[:, 12:16, :].rearrange("p k s -> p (k s)"), PS[7][:, :], ALU.mult)
                    dve.wait_ge(mlstm_exp_by_act, n * 4 + 3)
                    nc.vector.tensor_tensor(PWb[:, 8:12, :].rearrange("p k s -> p (k s)"), SCb[:, 8:12, :].rearrange("p k s -> p (k s)"), PS[6][:, :], ALU.mult).then_inc(mlstm_weighted_by_dve, 1)
                    dve.wait_ge(mlstm_exp_by_act, n * 4 + 4)
                    nc.vector.tensor_tensor(PWa[:, 8:12, :].rearrange("p k s -> p (k s)"), SCa[:, 8:12, :].rearrange("p k s -> p (k s)"), PS[2][:, :], ALU.mult)
                    dve.wait_ge(mlstm_scores_by_pe, n * 4 + 4)
                    nc.vector.tensor_tensor(PWa[:, 4:8, :].rearrange("p k s -> p (k s)"), SCa[:, 4:8, :].rearrange("p k s -> p (k s)"), PS[1][:, :], ALU.mult)
                    nc.vector.tensor_tensor(PWa[:, 0:4, :].rearrange("p k s -> p (k s)"), SCa[:, 0:4, :].rearrange("p k s -> p (k s)"), PS[0][:, :], ALU.mult).then_inc(mlstm_weighted_by_dve, 1)
                    dve.wait_ge(mlstm_attended_by_pe, n * 2 + 1)
                    nc.vector.scalar_tensor_tensor(rnb[:, :], PS[4][:, 0:272].rearrange("p (h d) -> p h d", d=17)[:, :, 16], -1.0, eTb[:, :], ALU.mult, ALU.max).then_inc(mlstm_normalize_by_dve, 1)
                    dve.wait_ge(mlstm_normalize_by_dve, n * 10 + 1)
                    nc.vector.tensor_tensor(rnb[:, :], PS[4][:, 0:272].rearrange("p (h d) -> p h d", d=17)[:, :, 16], rnb[:, :], ALU.max).then_inc(mlstm_normalize_by_dve, 1)
                    dve.wait_ge(mlstm_normalize_by_dve, n * 10 + 2)
                    nc.vector.tensor_scalar(rnb[:, :], rnb[:, :], 1e-6, None, ALU.add).then_inc(mlstm_normalize_by_dve, 1)
                    dve.wait_ge(mlstm_normalize_by_dve, n * 10 + 3)
                    nc.vector.reciprocal(rdb[:, :], rnb[:, :]).then_inc(mlstm_normalize_by_dve, 1)
                    dve.wait_ge(mlstm_normalize_by_dve, n * 10 + 4)
                    nc.vector.tensor_tensor(by_head(hhb[:, :]), PS[4][:, 0:272].rearrange("p (h d) -> p h d", d=17)[:, :, 0:16], rdb[:, :].unsqueeze(2).to_broadcast([128, 16, 16]), ALU.mult).then_inc(mlstm_normalize_by_dve, 1)
                    dve.wait_ge(mlstm_normalize_by_dve, n * 10 + 5)
                    nc.vector.reduce_sum(mub[:, :], by_head(hhb[:, :]), AX.X).then_inc(mlstm_headnorm_by_dve, 1)
                    dve.wait_ge(mlstm_headnorm_by_dve, n * 11 + 1)
                    nc.vector.tensor_scalar(mub[:, :], mub[:, :], 1.0 / 16, None, ALU.mult).then_inc(mlstm_headnorm_by_dve, 1)
                    dve.wait_ge(mlstm_headnorm_by_dve, n * 11 + 2)
                    nc.vector.tensor_tensor(by_head(hcb[:, :]), by_head(hhb[:, :]), mub[:, :].unsqueeze(2).to_broadcast([128, 16, 16]), ALU.subtract).then_inc(mlstm_headnorm_by_dve, 1)
                    dve.wait_ge(mlstm_headsq_by_pool, n * 4 + 1)
                    nc.vector.reduce_sum(varb[:, :], by_head(hqb[:, :]), AX.X).then_inc(mlstm_headnorm_by_dve, 1)
                    dve.wait_ge(mlstm_headnorm_by_dve, n * 11 + 4)
                    nc.vector.tensor_scalar(varb[:, :], varb[:, :], 1.0 / 16, 1e-6, ALU.mult, ALU.add).then_inc(mlstm_headnorm_by_dve, 1)
                    dve.wait_ge(mlstm_attended_by_pe, n * 2 + 2)
                    nc.vector.scalar_tensor_tensor(rna[:, :], PS[0][:, 0:272].rearrange("p (h d) -> p h d", d=17)[:, :, 16], -1.0, eTa[:, :], ALU.mult, ALU.max).then_inc(mlstm_normalize_by_dve, 1)
                    dve.wait_ge(mlstm_normalize_by_dve, n * 10 + 6)
                    nc.vector.tensor_tensor(rna[:, :], PS[0][:, 0:272].rearrange("p (h d) -> p h d", d=17)[:, :, 16], rna[:, :], ALU.max).then_inc(mlstm_normalize_by_dve, 1)
                    dve.wait_ge(mlstm_normalize_by_dve, n * 10 + 7)
                    nc.vector.tensor_scalar(rna[:, :], rna[:, :], 1e-6, None, ALU.add).then_inc(mlstm_normalize_by_dve, 1)
                    dve.wait_ge(mlstm_normalize_by_dve, n * 10 + 8)
                    nc.vector.reciprocal(rda[:, :], rna[:, :]).then_inc(mlstm_normalize_by_dve, 1)
                    dve.wait_ge(mlstm_headsq_by_pool, n * 4 + 2)
                    nc.vector.tensor_tensor(by_head(hhb[:, :]), by_head(hcb[:, :]), rsb[:, :].unsqueeze(2).to_broadcast([128, 16, 16]), ALU.mult)
                    dve.wait_ge(mlstm_normalize_by_dve, n * 10 + 9)
                    nc.vector.tensor_tensor(by_head(hha[:, :]), PS[0][:, 0:272].rearrange("p (h d) -> p h d", d=17)[:, :, 0:16], rda[:, :].unsqueeze(2).to_broadcast([128, 16, 16]), ALU.mult).then_inc(mlstm_normalize_by_dve, 1)
                    dve.wait_ge(mlstm_normalize_by_dve, n * 10 + 10)
                    nc.vector.reduce_sum(mua[:, :], by_head(hha[:, :]), AX.X).then_inc(mlstm_headnorm_by_dve, 1)
                    dve.wait_ge(mlstm_headnorm_by_dve, n * 11 + 6)
                    nc.vector.tensor_scalar(mua[:, :], mua[:, :], 1.0 / 16, None, ALU.mult).then_inc(mlstm_headnorm_by_dve, 1)
                    dve.wait_ge(mlstm_headnorm_by_dve, n * 11 + 7)
                    nc.vector.tensor_tensor(by_head(hca[:, :]), by_head(hha[:, :]), mua[:, :].unsqueeze(2).to_broadcast([128, 16, 16]), ALU.subtract).then_inc(mlstm_headnorm_by_dve, 1)
                    nc.vector.tensor_tensor(X[:, bass.ds((n * 2 + 1) * 256, 256)], X[:, bass.ds((n * 2 + 1) * 256, 256)], hhb[:, :], ALU.add)
                    dve.wait_ge(mlstm_headsq_by_pool, n * 4 + 3)
                    nc.vector.reduce_sum(vara[:, :], by_head(hqa[:, :]), AX.X).then_inc(mlstm_headnorm_by_dve, 1)
                    dve.wait_ge(mlstm_headnorm_by_dve, n * 11 + 9)
                    nc.vector.tensor_scalar(vara[:, :], vara[:, :], 1.0 / 16, 1e-6, ALU.mult, ALU.add).then_inc(mlstm_headnorm_by_dve, 1)
                    dve.wait_ge(mlstm_headsq_by_pool, n * 4 + 4)
                    nc.vector.tensor_tensor(by_head(hha[:, :]), by_head(hca[:, :]), rsa[:, :].unsqueeze(2).to_broadcast([128, 16, 16]), ALU.mult).then_inc(mlstm_headnorm_by_dve, 1)
                    dve.wait_ge(mlstm_headnorm_by_dve, n * 11 + 11)
                    nc.vector.tensor_tensor(X[:, bass.ds((n * 2 + 0) * 256, 256)], X[:, bass.ds((n * 2 + 0) * 256, 256)], hha[:, :], ALU.add).then_inc(mlstm_residual_by_dve, 1)

            @block.scalar
            def _(act):
                act.wait_ge(mlstm_setup_by_pool, 2)
                act.wait_ge(mlstm_setup_loads_sp, 112)
                act.wait_ge(mlstm_setup_by_pe, 1)
                act.wait_ge(mlstm_setup_by_dve, 1)
                with act.Fori(0, 16) as i:
                    n = i
                    act.wait_ge(mlstm_turned_by_pe, n * 4 + 5)
                    nc.scalar.activation(kTb[:, :, :].rearrange("p c t -> p (c t)"), PS[5][:, 0:256], ACT.Copy)
                    act.wait_ge(mlstm_turned_by_pe, n * 4 + 6)
                    nc.scalar.activation(kTa[:, :, :].rearrange("p c t -> p (c t)"), PS[1][:, 0:256], ACT.Copy)
                    act.wait_ge(mlstm_turned_by_pe, n * 4 + 7)
                    nc.scalar.activation(qTa[:, :, :].rearrange("p c t -> p (c t)"), PS[0][:, 0:256], ACT.Copy).then_inc(mlstm_turned_by_act, 1)
                    act.wait_ge(mlstm_turned_by_pe, n * 4 + 8)
                    nc.scalar.activation(qTb[:, :, :].rearrange("p c t -> p (c t)"), PS[4][:, 0:256], ACT.Copy).then_inc(mlstm_turned_by_act, 1)
                    act.wait_ge(mlstm_gates_by_dve, n * 2 + 1)
                    nc.scalar.activation(f2a[:, :], fa[:, :], ACT.Abs).then_inc(mlstm_logf_by_act, 1)
                    act.wait_ge(mlstm_logf_by_act, n * 6 + 1)
                    nc.scalar.activation(f2a[:, :], f2a[:, :], ACT.Exp, scale=-1.0).then_inc(mlstm_logf_by_act, 1)
                    act.wait_ge(mlstm_logf_by_act, n * 6 + 2)
                    nc.scalar.activation(f2a[:, :], f2a[:, :], ACT.Ln, bias=1.0).then_inc(mlstm_logf_by_act, 1)
                    act.wait_ge(mlstm_gates_by_dve, n * 2 + 2)
                    nc.scalar.activation(f2b[:, :], fb[:, :], ACT.Abs).then_inc(mlstm_logf_by_act, 1)
                    act.wait_ge(mlstm_logf_by_act, n * 6 + 4)
                    nc.scalar.activation(f2b[:, :], f2b[:, :], ACT.Exp, scale=-1.0).then_inc(mlstm_logf_by_act, 1)
                    act.wait_ge(mlstm_logf_by_act, n * 6 + 5)
                    nc.scalar.activation(f2b[:, :], f2b[:, :], ACT.Ln, bias=1.0).then_inc(mlstm_logf_by_act, 1)
                    act.wait_ge(mlstm_gturn_by_dve, n * 2 + 1)
                    nc.scalar.activation(eTa[:, :], PS[2][:, 272:288], ACT.Exp, scale=-1.0).then_inc(mlstm_floor_by_act, 1)
                    for k in range(0, 4):
                        last = nc.scalar.activation(SCa[:, k, :], SCa[:, k, :], ACT.Exp, bias=uTa[:, k:k + 1])
                    act.wait_ge(mlstm_masked_by_dve, n * 6 + 1)
                    for k in range(4, 8):
                        last = nc.scalar.activation(SCa[:, k, :], SCa[:, k, :], ACT.Exp, bias=uTa[:, k:k + 1])
                    act.wait_ge(mlstm_masked_by_dve, n * 6 + 2)
                    for k in range(12, 16):
                        last = nc.scalar.activation(SCa[:, k, :], SCa[:, k, :], ACT.Exp, bias=uTa[:, k:k + 1])
                    act.wait_ge(mlstm_gturn_by_dve, n * 2 + 2)
                    nc.scalar.activation(eTb[:, :], PS[6][:, 272:288], ACT.Exp, scale=-1.0).then_inc(mlstm_floor_by_act, 1)
                    for k in range(0, 4):
                        last = nc.scalar.activation(SCb[:, k, :], SCb[:, k, :], ACT.Exp, bias=uTb[:, k:k + 1])
                    last.then_inc(mlstm_exp_by_act, 1)
                    act.wait_ge(mlstm_masked_by_dve, n * 6 + 4)
                    for k in range(12, 16):
                        last = nc.scalar.activation(SCb[:, k, :], SCb[:, k, :], ACT.Exp, bias=uTb[:, k:k + 1])
                    for k in range(4, 8):
                        last = nc.scalar.activation(SCb[:, k, :], SCb[:, k, :], ACT.Exp, bias=uTb[:, k:k + 1])
                    last.then_inc(mlstm_exp_by_act, 1)
                    act.wait_ge(mlstm_masked_by_dve, n * 6 + 6)
                    for k in range(8, 12):
                        last = nc.scalar.activation(SCb[:, k, :], SCb[:, k, :], ACT.Exp, bias=uTb[:, k:k + 1])
                    last.then_inc(mlstm_exp_by_act, 1)
                    for k in range(8, 12):
                        last = nc.scalar.activation(SCa[:, k, :], SCa[:, k, :], ACT.Exp, bias=uTa[:, k:k + 1])
                    last.then_inc(mlstm_exp_by_act, 1)

            @block.gpsimd
            def _(pool):
                nc.gpsimd.memset(NEGHALF[:, :], -0.5)
                nc.gpsimd.memset(onerow[:, :], 1.0).then_inc(mlstm_setup_by_pool, 1)
                nc.gpsimd.memset(VXa[:, :, :], 1.0)
                nc.gpsimd.memset(VXb[:, :, :], 1.0).then_inc(mlstm_setup_by_pool, 1)
                pool.wait_ge(mlstm_setup_by_pool, 2)
                pool.wait_ge(mlstm_setup_loads_sp, 112)
                pool.wait_ge(mlstm_setup_by_pe, 1)
                pool.wait_ge(mlstm_setup_by_dve, 1)
                with pool.Fori(0, 16) as i:
                    n = i
                    pool.wait_ge(mlstm_norm_by_dve, n * 6 + 5)
                    nc.gpsimd.tensor_tensor(rstda[:, :], varea[:, :], NEGHALF[:, 0:1], ALU.pow).then_inc(mlstm_rstd_by_pool, 1)
                    pool.wait_ge(mlstm_norm_by_dve, n * 6 + 6)
                    nc.gpsimd.tensor_tensor(rstdb[:, :], vareb[:, :], NEGHALF[:, 0:1], ALU.pow).then_inc(mlstm_rstd_by_pool, 1)
                    pool.wait_ge(mlstm_turned_by_act, n * 2 + 1)
                    nc.gpsimd.tensor_tensor(HXa[:, 8:16, :], qTa[:, 1, :].unsqueeze(1).to_broadcast([128, 8, 128]),
                                           HM[:, :].unsqueeze(2).to_broadcast([128, 8, 128]), ALU.mult).then_inc(mlstm_expand_by_pool, 1)
                    pool.wait_ge(mlstm_turned_by_act, n * 2 + 2)
                    nc.gpsimd.tensor_tensor(HXb[:, 8:16, :], qTb[:, 1, :].unsqueeze(1).to_broadcast([128, 8, 128]),
                                           HM[:, :].unsqueeze(2).to_broadcast([128, 8, 128]), ALU.mult).then_inc(mlstm_expand_by_pool, 1)
                    pool.wait_ge(mlstm_headnorm_by_dve, n * 11 + 3)
                    nc.gpsimd.tensor_tensor(hqb[:, :], hcb[:, :], hcb[:, :], ALU.mult).then_inc(mlstm_headsq_by_pool, 1)
                    nc.gpsimd.tensor_tensor(hcb[:, :], hcb[:, :], LNB[:, :], ALU.mult)
                    pool.wait_ge(mlstm_headnorm_by_dve, n * 11 + 5)
                    nc.gpsimd.tensor_tensor(rsb[:, :], varb[:, :], NEGHALF[:, :], ALU.pow).then_inc(mlstm_headsq_by_pool, 1)
                    pool.wait_ge(mlstm_headnorm_by_dve, n * 11 + 8)
                    nc.gpsimd.tensor_tensor(hqa[:, :], hca[:, :], hca[:, :], ALU.mult).then_inc(mlstm_headsq_by_pool, 1)
                    nc.gpsimd.tensor_tensor(hca[:, :], hca[:, :], LNB[:, :], ALU.mult)
                    pool.wait_ge(mlstm_headnorm_by_dve, n * 11 + 10)
                    nc.gpsimd.tensor_tensor(rsa[:, :], vara[:, :], NEGHALF[:, :], ALU.pow).then_inc(mlstm_headsq_by_pool, 1)

            @block.sync
            def _(sp):
                nc.sync.dma_start(HM[:, :], io["head_mask"]).then_inc(mlstm_setup_loads_sp, 16)
                nc.sync.dma_start(WIF[:, :, :], io["w_if"]).then_inc(mlstm_setup_loads_sp, 16)
                nc.sync.dma_start(BIF[:, :], io["b_if"]).then_inc(mlstm_setup_loads_sp, 16)
                nc.sync.dma_start(RST[:, :], io["resets"]).then_inc(mlstm_setup_loads_sp, 16)
                nc.sync.dma_start(SEL[:, :], io["select"]).then_inc(mlstm_setup_loads_sp, 16)
                nc.sync.dma_start(NMASK[:, :], io["neg_causal_t"]).then_inc(mlstm_setup_loads_sp, 16)
                nc.sync.dma_start(LNS[:, :], io["ln_scale"]).then_inc(mlstm_setup_loads_sp, 16)
                sp.wait_ge(mlstm_setup_by_pool, 2)
                sp.wait_ge(mlstm_setup_loads_sp, 112)
                sp.wait_ge(mlstm_setup_by_pe, 1)
                sp.wait_ge(mlstm_setup_by_dve, 1)
                with sp.Fori(0, 16) as i:
                    n = i
                    sp.wait_ge(mlstm_turned_by_pe, n * 4 + 1)
                    sp.sem_inc(mlstm_sp_passed, 1)
                    sp.wait_ge(mlstm_values_by_dve, n * 2 + 1)
                    sp.sem_inc(mlstm_sp_passed, 1)
                    nc.sync.dma_start(cxb[:, :], io["ctx"][bass.ds((n * 2 + 1) * 128, 128), :]).then_inc(mlstm_context_b_dma, 16)
                    sp.wait_ge(mlstm_turned_by_pe, n * 4 + 2)
                    sp.sem_inc(mlstm_sp_passed, 1)
                    sp.wait_ge(mlstm_values_by_dve, n * 2 + 2)
                    sp.sem_inc(mlstm_sp_passed, 1)
                    nc.sync.dma_start(cxa[:, :], io["ctx"][bass.ds((n * 2 + 0) * 128, 128), :]).then_inc(mlstm_context_a_dma, 16)

        nc.clear_and_free_semaphores(signals)
        nc.all_engine_barrier()

def ffn0a(nc, io, X, PS, IDENT, shared):
    ctx = ExitStack()
    with ctx:
        def sb(name, shape, dt=F32):
            return ctx.enter_context(nc.sbuf_tensor("ffn0a_" + name, shape, dt))

        signals = []

        def signal(name):
            signals.append(nc.alloc_semaphore(name))
            return signals[-1]

        H0T, CW0 = shared
        statsa = sb("statsa", [128, 6])
        mva = sb("mva", [128, 2])
        varea = sb("varea", [128, 1])
        rstda = sb("rstda", [128, 1])
        xna = sb("xna", [128, 256])
        qTa = sb("qTa", [128, 2, 128])
        HXa = sb("HXa", [128, 16, 128])
        kTa = sb("kTa", [128, 2, 128])
        VXa = sb("VXa", [128, 16, 17])
        SCa = sb("SCa", [128, 16, 128])
        PWa = sb("PWa", [128, 16, 128])
        ctx_a = sb("ctx_a", [128, 256])
        cTa = sb("cTa", [128, 2, 128])
        xTa = sb("xTa", [128, 2, 128])
        rda = sb("rda", [128, 16])
        mxa = sb("mxa", [128, 16])
        nmxa = sb("nmxa", [128, 16])
        tma = sb("tma", [128, 1])
        tna = sb("tna", [128, 1])
        psa = sb("psa", [128, 1])
        pra = sb("pra", [128, 1])
        sha = sb("sha", [128, 1])
        csa = sb("csa", [128, 1])
        cra = sb("cra", [128, 1])
        pea = sb("pea", [128, 8])
        m8a = sb("m8a", [128, 8])
        topa = sb("topa", [128, 8])
        c8a = sb("c8a", [128, 8])
        ppa = sb("ppa", [128, 14])
        pza = sb("pza", [128, 14])
        jka = sb("jka", [128, 256])
        msa = sb("msa", [128, 1])
        hna = sb("hna", [128, 256])
        t1a = sb("t1a", [128, 256])
        t2a = sb("t2a", [128, 256])
        k1a = sb("k1a", [128, 256])
        k2a = sb("k2a", [128, 256])
        x2a = sb("x2a", [128, 256])
        statsb = sb("statsb", [128, 6])
        mvb = sb("mvb", [128, 2])
        vareb = sb("vareb", [128, 1])
        rstdb = sb("rstdb", [128, 1])
        xnb = sb("xnb", [128, 256])
        qTb = sb("qTb", [128, 2, 128])
        HXb = sb("HXb", [128, 16, 128])
        kTb = sb("kTb", [128, 2, 128])
        VXb = sb("VXb", [128, 16, 17])
        SCb = sb("SCb", [128, 16, 128])
        PWb = sb("PWb", [128, 16, 128])
        ctx_b = sb("ctx_b", [128, 256])
        cTb = sb("cTb", [128, 2, 128])
        xTb = sb("xTb", [128, 2, 128])
        rdb = sb("rdb", [128, 16])
        mxb = sb("mxb", [128, 16])
        nmxb = sb("nmxb", [128, 16])
        tmb = sb("tmb", [128, 1])
        tnb = sb("tnb", [128, 1])
        psb = sb("psb", [128, 1])
        prb = sb("prb", [128, 1])
        shb = sb("shb", [128, 1])
        csb = sb("csb", [128, 1])
        crb = sb("crb", [128, 1])
        peb = sb("peb", [128, 8])
        m8b = sb("m8b", [128, 8])
        topb = sb("topb", [128, 8])
        c8b = sb("c8b", [128, 8])
        ppb = sb("ppb", [128, 14])
        pzb = sb("pzb", [128, 14])
        jkb = sb("jkb", [128, 256])
        msb = sb("msb", [128, 1])
        hnb = sb("hnb", [128, 256])
        t1b = sb("t1b", [128, 256])
        t2b = sb("t2b", [128, 256])
        k1b = sb("k1b", [128, 256])
        k2b = sb("k2b", [128, 256])
        x2b = sb("x2b", [128, 256])
        NEGHALF = sb("neghalf", [128, 16])
        HM = sb("hm", [128, 8])
        onerow = sb("onerow", [1, 128])
        WQ = sb("WQ", [128, 2, 256])
        WK = sb("WK", [128, 2, 256])
        WV = sb("WV", [128, 2, 256])
        WO = sb("WO", [128, 2, 256])
        WR = sb("WR", [128, 2, 9])
        BQKV = sb("BQKV", [1, 768])
        LNW = sb("LNW", [128, 4])
        COS = sb("COS", [128, 256])
        SIN = sb("SIN", [128, 256])
        NMASK = sb("NMASK", [128, 512])
        WQR = sb("wqr", [128, 2, 256])
        WKR = sb("wkr", [128, 2, 256])
        BR = sb("br", [1, 512])
        BQ = BQKV[0:1, 0:256]
        BK = BQKV[0:1, 256:512]
        BV = BQKV[0:1, 512:768]
        BQR = BR[0:1, 0:256]
        BKR = BR[0:1, 256:512]
        def by_head(t):
            return t.rearrange("p (h d) -> p h d", d=16)
        def halves(t, k):
            return t.rearrange("p (h two d) -> p h two d", two=2, d=8)[:, :, k, :]

        ffn0a_setup_loads_sp = signal("ffn0a_setup_loads_sp")
        ffn0a_setup_by_pool = signal("ffn0a_setup_by_pool")
        ffn0a_setup_by_dve = signal("ffn0a_setup_by_dve")
        ffn0a_norm_by_dve = signal("ffn0a_norm_by_dve")
        ffn0a_rstd_by_pool = signal("ffn0a_rstd_by_pool")
        ffn0a_normed_by_dve = signal("ffn0a_normed_by_dve")
        ffn0a_rms_by_act = signal("ffn0a_rms_by_act")
        ffn0a_turned_by_pe = signal("ffn0a_turned_by_pe")
        ffn0a_turned_by_act = signal("ffn0a_turned_by_act")
        ffn0a_projected_by_pe = signal("ffn0a_projected_by_pe")
        ffn0a_rope_by_dve = signal("ffn0a_rope_by_dve")
        ffn0a_rope_by_pool = signal("ffn0a_rope_by_pool")
        ffn0a_values_by_act = signal("ffn0a_values_by_act")
        ffn0a_scores_by_pe = signal("ffn0a_scores_by_pe")
        ffn0a_masked_by_dve = signal("ffn0a_masked_by_dve")
        ffn0a_max_by_dve = signal("ffn0a_max_by_dve")
        ffn0a_exp_by_act = signal("ffn0a_exp_by_act")
        ffn0a_pturn_by_pe = signal("ffn0a_pturn_by_pe")
        ffn0a_pturn_by_dve = signal("ffn0a_pturn_by_dve")
        ffn0a_pturn_by_act = signal("ffn0a_pturn_by_act")
        ffn0a_attended_by_pe = signal("ffn0a_attended_by_pe")
        ffn0a_normalize_by_dve = signal("ffn0a_normalize_by_dve")
        ffn0a_outproj_by_pe = signal("ffn0a_outproj_by_pe")
        ffn0a_residual_by_dve = signal("ffn0a_residual_by_dve")
        ffn0a_residual_by_pool = signal("ffn0a_residual_by_pool")
        ffn0a_router_by_pe = signal("ffn0a_router_by_pe")
        ffn0a_route_by_dve = signal("ffn0a_route_by_dve")
        ffn0a_kept_by_pool = signal("ffn0a_kept_by_pool")
        ffn0a_route_by_act = signal("ffn0a_route_by_act")
        ffn0a_pool_passed = signal("ffn0a_pool_passed")
        ffn0a_dve_passed = signal("ffn0a_dve_passed")
        with nc.Block() as block:

            @block.tensor
            def _(pe):
                pe.wait_ge(ffn0a_setup_loads_sp, 176)
                pe.wait_ge(ffn0a_setup_by_pool, 1)
                pe.wait_ge(ffn0a_setup_by_dve, 1)
                with pe.Fori(0, 16) as i:
                    n = i
                    pe.wait_ge(ffn0a_normed_by_dve, n * 6 + 3)
                    for c in range(2):
                        last = nc.tensor.transpose(PS[0][:, c * 128:(c + 1) * 128], hna[:, c * 128:(c + 1) * 128], IDENT[:, :])
                    last.then_inc(ffn0a_turned_by_pe, 1)
                    pe.wait_ge(ffn0a_turned_by_act, n * 6 + 1)
                    for e in range(2):
                        for c in range(2):
                            last = nc.tensor.matmul(PS[1][:, 0 + e * 128:0 + (e + 1) * 128], WK[:, c, e * 128:(e + 1) * 128], xTa[:, c, :], start=(c == 0), stop=False)
                        last = nc.tensor.matmul(PS[1][:, 0 + e * 128:0 + (e + 1) * 128], BK[0:1, e * 128:(e + 1) * 128], onerow[0:1, :], start=False, stop=True)
                    pe.wait_ge(ffn0a_normed_by_dve, n * 6 + 4)
                    for c in range(2):
                        last = nc.tensor.transpose(PS[4][:, c * 128:(c + 1) * 128], hnb[:, c * 128:(c + 1) * 128], IDENT[:, :])
                    last.then_inc(ffn0a_turned_by_pe, 1)
                    for e in range(2):
                        for c in range(2):
                            last = nc.tensor.matmul(PS[1][:, 256 + e * 128:256 + (e + 1) * 128], WKR[:, c, e * 128:(e + 1) * 128], xTa[:, c, :], start=(c == 0), stop=False)
                        last = nc.tensor.matmul(PS[1][:, 256 + e * 128:256 + (e + 1) * 128], BKR[0:1, e * 128:(e + 1) * 128], onerow[0:1, :], start=False, stop=True)
                    last.then_inc(ffn0a_projected_by_pe, 1)
                    pe.wait_ge(ffn0a_turned_by_act, n * 6 + 2)
                    for e in range(2):
                        for c in range(2):
                            last = nc.tensor.matmul(PS[5][:, 0 + e * 128:0 + (e + 1) * 128], WK[:, c, e * 128:(e + 1) * 128], xTb[:, c, :], start=(c == 0), stop=False)
                        last = nc.tensor.matmul(PS[5][:, 0 + e * 128:0 + (e + 1) * 128], BK[0:1, e * 128:(e + 1) * 128], onerow[0:1, :], start=False, stop=True)
                    for e in range(2):
                        for c in range(2):
                            last = nc.tensor.matmul(PS[0][:, 0 + e * 128:0 + (e + 1) * 128], WQ[:, c, e * 128:(e + 1) * 128], xTa[:, c, :], start=(c == 0), stop=False)
                        last = nc.tensor.matmul(PS[0][:, 0 + e * 128:0 + (e + 1) * 128], BQ[0:1, e * 128:(e + 1) * 128], onerow[0:1, :], start=False, stop=True)
                    for e in range(2):
                        for c in range(2):
                            last = nc.tensor.matmul(PS[5][:, 256 + e * 128:256 + (e + 1) * 128], WKR[:, c, e * 128:(e + 1) * 128], xTb[:, c, :], start=(c == 0), stop=False)
                        last = nc.tensor.matmul(PS[5][:, 256 + e * 128:256 + (e + 1) * 128], BKR[0:1, e * 128:(e + 1) * 128], onerow[0:1, :], start=False, stop=True)
                    last.then_inc(ffn0a_projected_by_pe, 1)
                    for e in range(2):
                        for c in range(2):
                            last = nc.tensor.matmul(PS[4][:, 0 + e * 128:0 + (e + 1) * 128], WQ[:, c, e * 128:(e + 1) * 128], xTb[:, c, :], start=(c == 0), stop=False)
                        last = nc.tensor.matmul(PS[4][:, 0 + e * 128:0 + (e + 1) * 128], BQ[0:1, e * 128:(e + 1) * 128], onerow[0:1, :], start=False, stop=True)
                    for e in range(2):
                        for c in range(2):
                            last = nc.tensor.matmul(PS[0][:, 256 + e * 128:256 + (e + 1) * 128], WQR[:, c, e * 128:(e + 1) * 128], xTa[:, c, :], start=(c == 0), stop=False)
                        last = nc.tensor.matmul(PS[0][:, 256 + e * 128:256 + (e + 1) * 128], BQR[0:1, e * 128:(e + 1) * 128], onerow[0:1, :], start=False, stop=True)
                    last.then_inc(ffn0a_projected_by_pe, 1)
                    for e in range(2):
                        for c in range(2):
                            last = nc.tensor.matmul(PS[4][:, 256 + e * 128:256 + (e + 1) * 128], WQR[:, c, e * 128:(e + 1) * 128], xTb[:, c, :], start=(c == 0), stop=False)
                        last = nc.tensor.matmul(PS[4][:, 256 + e * 128:256 + (e + 1) * 128], BQR[0:1, e * 128:(e + 1) * 128], onerow[0:1, :], start=False, stop=True)
                    last.then_inc(ffn0a_projected_by_pe, 1)
                    for c in range(2):
                        last = nc.tensor.matmul(PS[2][:, 0:256], xTa[:, c, :], WV[:, c, :], start=(c == 0), stop=False)
                    last = nc.tensor.matmul(PS[2][:, 0:256], onerow[0:1, :], BV[0:1, :], start=False, stop=True)
                    last.then_inc(ffn0a_projected_by_pe, 1)
                    for c in range(2):
                        last = nc.tensor.matmul(PS[6][:, 0:256], xTb[:, c, :], WV[:, c, :], start=(c == 0), stop=False)
                    last = nc.tensor.matmul(PS[6][:, 0:256], onerow[0:1, :], BV[0:1, :], start=False, stop=True)
                    last.then_inc(ffn0a_projected_by_pe, 1)
                    pe.wait_ge(ffn0a_rope_by_pool, n * 4 + 3)
                    for k in range(2):
                        last = nc.tensor.matmul(PS[0 + k][:, :], qTa[:, 0, :], HXa[:, 0 + 4 * k:0 + 4 * k + 4, :], start=True, stop=True)
                    last.then_inc(ffn0a_scores_by_pe, 1)
                    pe.wait_ge(ffn0a_values_by_act, n * 2 + 1)
                    for k in range(2):
                        last = nc.tensor.matmul(PS[2 + k][:, :], qTa[:, 1, :], HXa[:, 8 + 4 * k:8 + 4 * k + 4, :], start=True, stop=True)
                    last.then_inc(ffn0a_scores_by_pe, 1)
                    pe.wait_ge(ffn0a_rope_by_pool, n * 4 + 4)
                    for k in range(2):
                        last = nc.tensor.matmul(PS[4 + k][:, :], qTb[:, 0, :], HXb[:, 0 + 4 * k:0 + 4 * k + 4, :], start=True, stop=True)
                    last.then_inc(ffn0a_scores_by_pe, 1)
                    pe.wait_ge(ffn0a_values_by_act, n * 2 + 2)
                    for k in range(2):
                        last = nc.tensor.matmul(PS[6 + k][:, :], qTb[:, 1, :], HXb[:, 8 + 4 * k:8 + 4 * k + 4, :], start=True, stop=True)
                    last.then_inc(ffn0a_scores_by_pe, 1)
                    pe.wait_ge(ffn0a_exp_by_act, n * 2 + 1)
                    for k in range(4):
                        last = nc.tensor.transpose(PS[3][:, k * 128:(k + 1) * 128], SCa[:, 12 + k, :], IDENT[:, :])
                    last.then_inc(ffn0a_pturn_by_pe, 1)
                    for k in range(4):
                        last = nc.tensor.transpose(PS[0][:, k * 128:(k + 1) * 128], SCa[:, 0 + k, :], IDENT[:, :])
                    last.then_inc(ffn0a_pturn_by_pe, 1)
                    for k in range(4):
                        last = nc.tensor.transpose(PS[1][:, k * 128:(k + 1) * 128], SCa[:, 4 + k, :], IDENT[:, :])
                    last.then_inc(ffn0a_pturn_by_pe, 1)
                    for k in range(4):
                        last = nc.tensor.transpose(PS[2][:, k * 128:(k + 1) * 128], SCa[:, 8 + k, :], IDENT[:, :])
                    last.then_inc(ffn0a_pturn_by_pe, 1)
                    pe.wait_ge(ffn0a_exp_by_act, n * 2 + 2)
                    for k in range(4):
                        last = nc.tensor.transpose(PS[5][:, k * 128:(k + 1) * 128], SCb[:, 4 + k, :], IDENT[:, :])
                    last.then_inc(ffn0a_pturn_by_pe, 1)
                    for k in range(4):
                        last = nc.tensor.transpose(PS[4][:, k * 128:(k + 1) * 128], SCb[:, 0 + k, :], IDENT[:, :])
                    last.then_inc(ffn0a_pturn_by_pe, 1)
                    for k in range(4):
                        last = nc.tensor.transpose(PS[7][:, k * 128:(k + 1) * 128], SCb[:, 12 + k, :], IDENT[:, :])
                    last.then_inc(ffn0a_pturn_by_pe, 1)
                    for k in range(4):
                        last = nc.tensor.transpose(PS[6][:, k * 128:(k + 1) * 128], SCb[:, 8 + k, :], IDENT[:, :])
                    last.then_inc(ffn0a_pturn_by_pe, 1)
                    pe.wait_ge(ffn0a_pturn_by_dve, n * 2 + 1)
                    pe.wait_ge(ffn0a_pturn_by_act, n * 2 + 1)
                    for head in range(16):
                        last = nc.tensor.matmul(PS[0][:, head * 17:head * 17 + 17], PWa[:, head, :], VXa[:, head, :], start=True, stop=True)
                    last.then_inc(ffn0a_attended_by_pe, 1)
                    pe.wait_ge(ffn0a_pturn_by_dve, n * 2 + 2)
                    pe.wait_ge(ffn0a_pturn_by_act, n * 2 + 2)
                    for head in range(16):
                        last = nc.tensor.matmul(PS[4][:, head * 17:head * 17 + 17], PWb[:, head, :], VXb[:, head, :], start=True, stop=True)
                    last.then_inc(ffn0a_attended_by_pe, 1)
                    pe.wait_ge(ffn0a_normalize_by_dve, n * 4 + 2)
                    for c in range(2):
                        last = nc.tensor.transpose(PS[1][:, c * 128:(c + 1) * 128], ctx_a[:, c * 128:(c + 1) * 128], IDENT[:, :])
                    last.then_inc(ffn0a_turned_by_pe, 1)
                    pe.wait_ge(ffn0a_normalize_by_dve, n * 4 + 4)
                    for c in range(2):
                        last = nc.tensor.transpose(PS[5][:, c * 128:(c + 1) * 128], ctx_b[:, c * 128:(c + 1) * 128], IDENT[:, :])
                    last.then_inc(ffn0a_turned_by_pe, 1)
                    pe.wait_ge(ffn0a_turned_by_act, n * 6 + 3)
                    for c in range(2):
                        last = nc.tensor.matmul(PS[2][:, 0:256], cTa[:, c, :], WO[:, c, :], start=(c == 0), stop=(c == 1))
                    last.then_inc(ffn0a_outproj_by_pe, 1)
                    pe.wait_ge(ffn0a_turned_by_act, n * 6 + 4)
                    for c in range(2):
                        last = nc.tensor.matmul(PS[6][:, 0:256], cTb[:, c, :], WO[:, c, :], start=(c == 0), stop=(c == 1))
                    last.then_inc(ffn0a_outproj_by_pe, 1)
                    pe.wait_ge(ffn0a_normed_by_dve, n * 6 + 5)
                    for c in range(2):
                        last = nc.tensor.transpose(PS[0][:, c * 128:(c + 1) * 128], hna[:, c * 128:(c + 1) * 128], IDENT[:, :])
                    last.then_inc(ffn0a_turned_by_pe, 1)
                    pe.wait_ge(ffn0a_normed_by_dve, n * 6 + 6)
                    for c in range(2):
                        last = nc.tensor.transpose(PS[4][:, c * 128:(c + 1) * 128], hnb[:, c * 128:(c + 1) * 128], IDENT[:, :])
                    last.then_inc(ffn0a_turned_by_pe, 1)
                    pe.wait_ge(ffn0a_turned_by_act, n * 6 + 5)
                    for c in range(2):
                        last = nc.tensor.matmul(PS[3][:, 256:265], xTa[:, c, :], WR[:, c, :], start=(c == 0), stop=(c == 1))
                    last.then_inc(ffn0a_router_by_pe, 1)
                    pe.wait_ge(ffn0a_turned_by_act, n * 6 + 6)
                    for c in range(2):
                        last = nc.tensor.matmul(PS[7][:, 256:265], xTb[:, c, :], WR[:, c, :], start=(c == 0), stop=(c == 1))
                    last.then_inc(ffn0a_router_by_pe, 1)

            @block.vector
            def _(dve):
                dve.wait_ge(ffn0a_setup_loads_sp, 176)
                nc.vector.tensor_scalar(halves(WQR[:, :, :].rearrange("p c n -> p (c n)"), 0), halves(WQ[:, :, :].rearrange("p c n -> p (c n)"), 1), -1.0, None, ALU.mult)
                nc.vector.tensor_copy(halves(WQR[:, :, :].rearrange("p c n -> p (c n)"), 1), halves(WQ[:, :, :].rearrange("p c n -> p (c n)"), 0))
                nc.vector.tensor_scalar(halves(WKR[:, :, :].rearrange("p c n -> p (c n)"), 0), halves(WK[:, :, :].rearrange("p c n -> p (c n)"), 1), -1.0, None, ALU.mult)
                nc.vector.tensor_copy(halves(WKR[:, :, :].rearrange("p c n -> p (c n)"), 1), halves(WK[:, :, :].rearrange("p c n -> p (c n)"), 0))
                nc.vector.tensor_scalar(halves(BR[:, :], 0), halves(BQKV[0:1, 0:512], 1), -1.0, None, ALU.mult)
                nc.vector.tensor_copy(halves(BR[:, :], 1), halves(BQKV[0:1, 0:512], 0)).then_inc(ffn0a_setup_by_dve, 1)
                dve.wait_ge(ffn0a_setup_loads_sp, 176)
                dve.wait_ge(ffn0a_setup_by_pool, 1)
                dve.wait_ge(ffn0a_setup_by_dve, 1)
                with dve.Fori(0, 16) as i:
                    n = i
                    nc.vector.bn_stats(statsa[:, :], X[:, bass.ds((n * 2 + 0) * 256, 256)]).then_inc(ffn0a_norm_by_dve, 1)
                    dve.wait_ge(ffn0a_norm_by_dve, n * 10 + 1)
                    dve.sem_inc(ffn0a_dve_passed, 1)
                    nc.vector.bn_aggr(mva[:, :], statsa[:, :]).then_inc(ffn0a_norm_by_dve, 1)
                    dve.wait_ge(ffn0a_norm_by_dve, n * 10 + 2)
                    nc.vector.tensor_scalar(varea[:, :], mva[:, 1:2], 1e-5, None, ALU.add).then_inc(ffn0a_norm_by_dve, 1)
                    dve.wait_ge(ffn0a_residual_by_pool, n * 1 + 1)
                    dve.sem_inc(ffn0a_dve_passed, 1)
                    nc.vector.bn_stats(statsb[:, :], X[:, bass.ds((n * 2 + 1) * 256, 256)]).then_inc(ffn0a_norm_by_dve, 1)
                    dve.wait_ge(ffn0a_rstd_by_pool, n * 6 + 1)
                    nc.vector.tensor_scalar(xna[:, :], X[:, bass.ds((n * 2 + 0) * 256, 256)], mva[:, 0:1], rstda[:, 0:1], ALU.subtract, ALU.mult).then_inc(ffn0a_normed_by_dve, 1)
                    dve.wait_ge(ffn0a_norm_by_dve, n * 10 + 4)
                    dve.sem_inc(ffn0a_dve_passed, 1)
                    nc.vector.bn_aggr(mvb[:, :], statsb[:, :]).then_inc(ffn0a_norm_by_dve, 1)
                    dve.wait_ge(ffn0a_norm_by_dve, n * 10 + 5)
                    nc.vector.tensor_scalar(vareb[:, :], mvb[:, 1:2], 1e-5, None, ALU.add).then_inc(ffn0a_norm_by_dve, 1)
                    dve.wait_ge(ffn0a_rstd_by_pool, n * 6 + 2)
                    nc.vector.tensor_scalar(xnb[:, :], X[:, bass.ds((n * 2 + 1) * 256, 256)], mvb[:, 0:1], rstdb[:, 0:1], ALU.subtract, ALU.mult).then_inc(ffn0a_normed_by_dve, 1)
                    dve.wait_ge(ffn0a_rms_by_act, n * 4 + 1)
                    nc.vector.tensor_scalar(varea[:, :], msa[:, :], 1.0 / 256, 1e-6, ALU.mult, ALU.add).then_inc(ffn0a_norm_by_dve, 1)
                    dve.wait_ge(ffn0a_rstd_by_pool, n * 6 + 3)
                    nc.vector.tensor_scalar(hna[:, :], xna[:, :], rstda[:, 0:1], None, ALU.mult).then_inc(ffn0a_normed_by_dve, 1)
                    dve.wait_ge(ffn0a_rms_by_act, n * 4 + 2)
                    nc.vector.tensor_scalar(vareb[:, :], msb[:, :], 1.0 / 256, 1e-6, ALU.mult, ALU.add).then_inc(ffn0a_norm_by_dve, 1)
                    dve.wait_ge(ffn0a_rstd_by_pool, n * 6 + 4)
                    nc.vector.tensor_scalar(hnb[:, :], xnb[:, :], rstdb[:, 0:1], None, ALU.mult).then_inc(ffn0a_normed_by_dve, 1)
                    dve.wait_ge(ffn0a_projected_by_pe, n * 6 + 1)
                    nc.vector.tensor_tensor(k1a[:, :], PS[1][:, 0:256], COS[:, :], ALU.mult)
                    nc.vector.tensor_tensor(k2a[:, :], PS[1][:, 256:512], SIN[:, :], ALU.mult).then_inc(ffn0a_rope_by_dve, 1)
                    dve.wait_ge(ffn0a_rope_by_pool, n * 4 + 1)
                    nc.vector.tensor_tensor(HXa[:, 0:8, :], kTa[:, 0, :].unsqueeze(1).to_broadcast([128, 8, 128]),
                                           HM[:, :].unsqueeze(2).to_broadcast([128, 8, 128]), ALU.mult)
                    dve.wait_ge(ffn0a_projected_by_pe, n * 6 + 2)
                    nc.vector.tensor_tensor(k1b[:, :], PS[5][:, 0:256], COS[:, :], ALU.mult)
                    nc.vector.tensor_tensor(k2b[:, :], PS[5][:, 256:512], SIN[:, :], ALU.mult).then_inc(ffn0a_rope_by_dve, 1)
                    dve.wait_ge(ffn0a_rope_by_pool, n * 4 + 2)
                    nc.vector.tensor_tensor(HXb[:, 0:8, :], kTb[:, 0, :].unsqueeze(1).to_broadcast([128, 8, 128]),
                                           HM[:, :].unsqueeze(2).to_broadcast([128, 8, 128]), ALU.mult)
                    dve.wait_ge(ffn0a_projected_by_pe, n * 6 + 3)
                    nc.vector.tensor_tensor(t1a[:, :], PS[0][:, 0:256], COS[:, :], ALU.mult)
                    nc.vector.tensor_tensor(t2a[:, :], PS[0][:, 256:512], SIN[:, :], ALU.mult).then_inc(ffn0a_rope_by_dve, 1)
                    dve.wait_ge(ffn0a_projected_by_pe, n * 6 + 4)
                    nc.vector.tensor_tensor(t1b[:, :], PS[4][:, 0:256], COS[:, :], ALU.mult)
                    nc.vector.tensor_tensor(t2b[:, :], PS[4][:, 256:512], SIN[:, :], ALU.mult).then_inc(ffn0a_rope_by_dve, 1)
                    dve.wait_ge(ffn0a_scores_by_pe, n * 4 + 1)
                    nc.vector.tensor_tensor(SCa[:, 4:8, :].rearrange("p k s -> p (k s)"), PS[1][:, :], NMASK[:, :], ALU.add)
                    nc.vector.tensor_tensor(SCa[:, 0:4, :].rearrange("p k s -> p (k s)"), PS[0][:, :], NMASK[:, :], ALU.add)
                    dve.wait_ge(ffn0a_scores_by_pe, n * 4 + 2)
                    nc.vector.tensor_tensor(SCa[:, 12:16, :].rearrange("p k s -> p (k s)"), PS[3][:, :], NMASK[:, :], ALU.add)
                    nc.vector.tensor_tensor(SCa[:, 8:12, :].rearrange("p k s -> p (k s)"), PS[2][:, :], NMASK[:, :], ALU.add).then_inc(ffn0a_masked_by_dve, 1)
                    dve.wait_ge(ffn0a_masked_by_dve, n * 2 + 1)
                    nc.vector.reduce_max(mxa[:, :], SCa[:, :, :], AX.X).then_inc(ffn0a_max_by_dve, 1)
                    dve.wait_ge(ffn0a_scores_by_pe, n * 4 + 3)
                    nc.vector.tensor_tensor(SCb[:, 4:8, :].rearrange("p k s -> p (k s)"), PS[5][:, :], NMASK[:, :], ALU.add)
                    nc.vector.tensor_tensor(SCb[:, 0:4, :].rearrange("p k s -> p (k s)"), PS[4][:, :], NMASK[:, :], ALU.add)
                    dve.wait_ge(ffn0a_scores_by_pe, n * 4 + 4)
                    nc.vector.tensor_tensor(SCb[:, 12:16, :].rearrange("p k s -> p (k s)"), PS[7][:, :], NMASK[:, :], ALU.add)
                    nc.vector.tensor_tensor(SCb[:, 8:12, :].rearrange("p k s -> p (k s)"), PS[6][:, :], NMASK[:, :], ALU.add).then_inc(ffn0a_masked_by_dve, 1)
                    dve.wait_ge(ffn0a_max_by_dve, n * 4 + 1)
                    nc.vector.tensor_scalar(nmxa[:, :], mxa[:, :], -1.0, None, ALU.mult).then_inc(ffn0a_max_by_dve, 1)
                    dve.wait_ge(ffn0a_masked_by_dve, n * 2 + 2)
                    nc.vector.reduce_max(mxb[:, :], SCb[:, :, :], AX.X).then_inc(ffn0a_max_by_dve, 1)
                    dve.wait_ge(ffn0a_max_by_dve, n * 4 + 3)
                    nc.vector.tensor_scalar(nmxb[:, :], mxb[:, :], -1.0, None, ALU.mult).then_inc(ffn0a_max_by_dve, 1)
                    dve.wait_ge(ffn0a_pturn_by_pe, n * 8 + 1)
                    nc.vector.tensor_copy(PWa[:, 12:16, :].rearrange("p k s -> p (k s)"), PS[3][:, :])
                    dve.wait_ge(ffn0a_pturn_by_pe, n * 8 + 3)
                    nc.vector.tensor_copy(PWa[:, 4:8, :].rearrange("p k s -> p (k s)"), PS[1][:, :]).then_inc(ffn0a_pturn_by_dve, 1)
                    dve.wait_ge(ffn0a_pturn_by_pe, n * 8 + 5)
                    nc.vector.tensor_copy(PWb[:, 4:8, :].rearrange("p k s -> p (k s)"), PS[5][:, :])
                    dve.wait_ge(ffn0a_pturn_by_pe, n * 8 + 7)
                    nc.vector.tensor_copy(PWb[:, 12:16, :].rearrange("p k s -> p (k s)"), PS[7][:, :]).then_inc(ffn0a_pturn_by_dve, 1)
                    dve.wait_ge(ffn0a_attended_by_pe, n * 2 + 1)
                    nc.vector.reciprocal(rda[:, :], PS[0][:, 0:272].rearrange("p (h d) -> p h d", d=17)[:, :, 16]).then_inc(ffn0a_normalize_by_dve, 1)
                    dve.wait_ge(ffn0a_normalize_by_dve, n * 4 + 1)
                    nc.vector.tensor_tensor(by_head(ctx_a[:, :]), PS[0][:, 0:272].rearrange("p (h d) -> p h d", d=17)[:, :, 0:16], rda[:, :].unsqueeze(2).to_broadcast([128, 16, 16]), ALU.mult).then_inc(ffn0a_normalize_by_dve, 1)
                    dve.wait_ge(ffn0a_attended_by_pe, n * 2 + 2)
                    nc.vector.reciprocal(rdb[:, :], PS[4][:, 0:272].rearrange("p (h d) -> p h d", d=17)[:, :, 16]).then_inc(ffn0a_normalize_by_dve, 1)
                    dve.wait_ge(ffn0a_normalize_by_dve, n * 4 + 3)
                    nc.vector.tensor_tensor(by_head(ctx_b[:, :]), PS[4][:, 0:272].rearrange("p (h d) -> p h d", d=17)[:, :, 0:16], rdb[:, :].unsqueeze(2).to_broadcast([128, 16, 16]), ALU.mult).then_inc(ffn0a_normalize_by_dve, 1)
                    dve.wait_ge(ffn0a_outproj_by_pe, n * 2 + 1)
                    nc.vector.tensor_tensor(x2a[:, :], PS[2][:, 0:256], xna[:, :], ALU.add).then_inc(ffn0a_residual_by_dve, 1)
                    dve.wait_ge(ffn0a_outproj_by_pe, n * 2 + 2)
                    nc.vector.tensor_tensor(x2b[:, :], PS[6][:, 0:256], xnb[:, :], ALU.add).then_inc(ffn0a_residual_by_dve, 1)
                    dve.wait_ge(ffn0a_rms_by_act, n * 4 + 3)
                    nc.vector.tensor_scalar(varea[:, :], msa[:, :], 1.0 / 256, 1e-6, ALU.mult, ALU.add).then_inc(ffn0a_norm_by_dve, 1)
                    dve.wait_ge(ffn0a_rms_by_act, n * 4 + 4)
                    nc.vector.tensor_scalar(vareb[:, :], msb[:, :], 1.0 / 256, 1e-6, ALU.mult, ALU.add).then_inc(ffn0a_norm_by_dve, 1)
                    dve.wait_ge(ffn0a_rstd_by_pool, n * 6 + 5)
                    nc.vector.tensor_scalar(hna[:, :], x2a[:, :], rstda[:, 0:1], None, ALU.mult).then_inc(ffn0a_normed_by_dve, 1)
                    dve.wait_ge(ffn0a_rstd_by_pool, n * 6 + 6)
                    nc.vector.tensor_scalar(hnb[:, :], x2b[:, :], rstdb[:, 0:1], None, ALU.mult).then_inc(ffn0a_normed_by_dve, 1)
                    dve.wait_ge(ffn0a_router_by_pe, n * 2 + 1)
                    nc.vector.reduce_max(tma[:, :], PS[3][:, 256:264], AX.X).then_inc(ffn0a_route_by_dve, 1)
                    dve.wait_ge(ffn0a_route_by_dve, n * 14 + 1)
                    nc.vector.tensor_scalar(tna[:, :], tma[:, :], -1.0, None, ALU.mult).then_inc(ffn0a_route_by_dve, 1)
                    dve.wait_ge(ffn0a_router_by_pe, n * 2 + 2)
                    nc.vector.reduce_max(tmb[:, :], PS[7][:, 256:264], AX.X).then_inc(ffn0a_route_by_dve, 1)
                    dve.wait_ge(ffn0a_route_by_dve, n * 14 + 3)
                    nc.vector.tensor_scalar(tnb[:, :], tmb[:, :], -1.0, None, ALU.mult).then_inc(ffn0a_route_by_dve, 1)
                    dve.wait_ge(ffn0a_route_by_act, n * 4 + 1)
                    nc.vector.reciprocal(pra[:, :], psa[:, :]).then_inc(ffn0a_route_by_dve, 1)
                    dve.wait_ge(ffn0a_route_by_dve, n * 14 + 5)
                    nc.vector.tensor_scalar(ppa[:, 0:8], pea[:, :], pra[:, 0:1], None, ALU.mult).then_inc(ffn0a_route_by_dve, 1)
                    dve.wait_ge(ffn0a_route_by_dve, n * 14 + 6)
                    dve.sem_inc(ffn0a_dve_passed, 1)
                    nc.vector.max(m8a[:, :], ppa[:, 0:8])
                    dve.wait_ge(ffn0a_route_by_act, n * 4 + 2)
                    nc.vector.tensor_scalar(sha[:, :], sha[:, :], 1.0, None, ALU.add)
                    dve.wait_ge(ffn0a_route_by_act, n * 4 + 3)
                    nc.vector.reciprocal(prb[:, :], psb[:, :]).then_inc(ffn0a_route_by_dve, 1)
                    dve.wait_ge(ffn0a_route_by_dve, n * 14 + 7)
                    nc.vector.tensor_scalar(ppb[:, 0:8], peb[:, :], prb[:, 0:1], None, ALU.mult).then_inc(ffn0a_route_by_dve, 1)
                    nc.vector.tensor_copy(topa[:, 0:2], m8a[:, 0:2]).then_inc(ffn0a_route_by_dve, 1)
                    nc.vector.reciprocal(CW0[:, bass.ds((n * 2 + 0), 1), 8], sha[:, :])
                    dve.wait_ge(ffn0a_route_by_act, n * 4 + 4)
                    nc.vector.tensor_scalar(shb[:, :], shb[:, :], 1.0, None, ALU.add).then_inc(ffn0a_route_by_dve, 1)
                    dve.wait_ge(ffn0a_route_by_dve, n * 14 + 8)
                    dve.sem_inc(ffn0a_dve_passed, 1)
                    nc.vector.max(m8b[:, :], ppb[:, 0:8]).then_inc(ffn0a_route_by_dve, 1)
                    dve.wait_ge(ffn0a_route_by_dve, n * 14 + 9)
                    dve.sem_inc(ffn0a_dve_passed, 1)
                    nc.vector.match_replace(pza[:, :], topa[:, :], ppa[:, :], 0.0)
                    dve.wait_ge(ffn0a_route_by_dve, n * 14 + 10)
                    nc.vector.reciprocal(CW0[:, bass.ds((n * 2 + 1), 1), 8], shb[:, :]).then_inc(ffn0a_route_by_dve, 1)
                    dve.wait_ge(ffn0a_route_by_dve, n * 14 + 11)
                    nc.vector.tensor_copy(topb[:, 0:2], m8b[:, 0:2]).then_inc(ffn0a_route_by_dve, 1)
                    dve.wait_ge(ffn0a_route_by_dve, n * 14 + 12)
                    nc.vector.tensor_tensor(CW0[:, bass.ds((n * 2 + 0), 1), 0:8].rearrange("p i e -> p (i e)"), ppa[:, 0:8], pza[:, 0:8], ALU.subtract)
                    dve.wait_ge(ffn0a_route_by_dve, n * 14 + 13)
                    dve.sem_inc(ffn0a_dve_passed, 1)
                    nc.vector.match_replace(pzb[:, :], topb[:, :], ppb[:, :], 0.0).then_inc(ffn0a_route_by_dve, 1)
                    dve.wait_ge(ffn0a_route_by_dve, n * 14 + 14)
                    nc.vector.tensor_tensor(CW0[:, bass.ds((n * 2 + 1), 1), 0:8].rearrange("p i e -> p (i e)"), ppb[:, 0:8], pzb[:, 0:8], ALU.subtract)

            @block.scalar
            def _(act):
                act.wait_ge(ffn0a_setup_loads_sp, 176)
                act.wait_ge(ffn0a_setup_by_pool, 1)
                act.wait_ge(ffn0a_setup_by_dve, 1)
                with act.Fori(0, 16) as i:
                    n = i
                    act.wait_ge(ffn0a_normed_by_dve, n * 6 + 1)
                    nc.scalar.activation(jka[:, :], xna[:, :], ACT.Square, accum_out=msa[:, 0:1]).then_inc(ffn0a_rms_by_act, 1)
                    act.wait_ge(ffn0a_normed_by_dve, n * 6 + 2)
                    nc.scalar.activation(jkb[:, :], xnb[:, :], ACT.Square, accum_out=msb[:, 0:1]).then_inc(ffn0a_rms_by_act, 1)
                    act.wait_ge(ffn0a_turned_by_pe, n * 6 + 1)
                    for c in range(2):
                        last = nc.scalar.activation(xTa[:, c, :], PS[0][:, c * 128:(c + 1) * 128], ACT.Copy, scale=LNW[:, 0:2][:, c:c + 1])
                    last.then_inc(ffn0a_turned_by_act, 1)
                    act.wait_ge(ffn0a_turned_by_pe, n * 6 + 2)
                    for c in range(2):
                        last = nc.scalar.activation(xTb[:, c, :], PS[4][:, c * 128:(c + 1) * 128], ACT.Copy, scale=LNW[:, 0:2][:, c:c + 1])
                    last.then_inc(ffn0a_turned_by_act, 1)
                    act.wait_ge(ffn0a_projected_by_pe, n * 6 + 5)
                    nc.scalar.activation(VXa[:, :, 0:16], by_head(PS[2][:, 0:256]), ACT.Copy).then_inc(ffn0a_values_by_act, 1)
                    act.wait_ge(ffn0a_projected_by_pe, n * 6 + 6)
                    nc.scalar.activation(VXb[:, :, 0:16], by_head(PS[6][:, 0:256]), ACT.Copy).then_inc(ffn0a_values_by_act, 1)
                    act.wait_ge(ffn0a_max_by_dve, n * 4 + 2)
                    for k in range(16):
                        last = nc.scalar.activation(SCa[:, k, :], SCa[:, k, :], ACT.Exp, bias=nmxa[:, k:k + 1])
                    last.then_inc(ffn0a_exp_by_act, 1)
                    act.wait_ge(ffn0a_max_by_dve, n * 4 + 4)
                    for k in range(16):
                        last = nc.scalar.activation(SCb[:, k, :], SCb[:, k, :], ACT.Exp, bias=nmxb[:, k:k + 1])
                    last.then_inc(ffn0a_exp_by_act, 1)
                    act.wait_ge(ffn0a_pturn_by_pe, n * 8 + 2)
                    nc.scalar.activation(PWa[:, 0:4, :].rearrange("p k s -> p (k s)"), PS[0][:, :], ACT.Copy)
                    act.wait_ge(ffn0a_pturn_by_pe, n * 8 + 4)
                    nc.scalar.activation(PWa[:, 8:12, :].rearrange("p k s -> p (k s)"), PS[2][:, :], ACT.Copy).then_inc(ffn0a_pturn_by_act, 1)
                    act.wait_ge(ffn0a_pturn_by_pe, n * 8 + 6)
                    nc.scalar.activation(PWb[:, 0:4, :].rearrange("p k s -> p (k s)"), PS[4][:, :], ACT.Copy)
                    act.wait_ge(ffn0a_pturn_by_pe, n * 8 + 8)
                    nc.scalar.activation(PWb[:, 8:12, :].rearrange("p k s -> p (k s)"), PS[6][:, :], ACT.Copy).then_inc(ffn0a_pturn_by_act, 1)
                    act.wait_ge(ffn0a_turned_by_pe, n * 6 + 3)
                    nc.scalar.activation(cTa[:, :, :].rearrange("p c t -> p (c t)"), PS[1][:, 0:256], ACT.Copy).then_inc(ffn0a_turned_by_act, 1)
                    act.wait_ge(ffn0a_turned_by_pe, n * 6 + 4)
                    nc.scalar.activation(cTb[:, :, :].rearrange("p c t -> p (c t)"), PS[5][:, 0:256], ACT.Copy).then_inc(ffn0a_turned_by_act, 1)
                    act.wait_ge(ffn0a_residual_by_dve, n * 2 + 1)
                    nc.scalar.activation(jka[:, :], x2a[:, :], ACT.Square, accum_out=msa[:, 0:1]).then_inc(ffn0a_rms_by_act, 1)
                    act.wait_ge(ffn0a_residual_by_dve, n * 2 + 2)
                    nc.scalar.activation(jkb[:, :], x2b[:, :], ACT.Square, accum_out=msb[:, 0:1]).then_inc(ffn0a_rms_by_act, 1)
                    act.wait_ge(ffn0a_turned_by_pe, n * 6 + 5)
                    for c in range(2):
                        last = nc.scalar.activation(xTa[:, c, :], PS[0][:, c * 128:(c + 1) * 128], ACT.Copy, scale=LNW[:, 2:4][:, c:c + 1])
                    last.then_inc(ffn0a_turned_by_act, 1)
                    act.wait_ge(ffn0a_turned_by_pe, n * 6 + 6)
                    for c in range(2):
                        last = nc.scalar.activation(xTb[:, c, :], PS[4][:, c * 128:(c + 1) * 128], ACT.Copy, scale=LNW[:, 2:4][:, c:c + 1])
                    last.then_inc(ffn0a_turned_by_act, 1)
                    act.wait_ge(ffn0a_route_by_dve, n * 14 + 2)
                    nc.scalar.activation(pea[:, :], PS[3][:, 256:264], ACT.Exp, bias=tna[:, 0:1], accum_out=psa[:, 0:1]).then_inc(ffn0a_route_by_act, 1)
                    nc.scalar.activation(sha[:, :], PS[3][:, 264:265], ACT.Exp, scale=-1.0).then_inc(ffn0a_route_by_act, 1)
                    act.wait_ge(ffn0a_route_by_dve, n * 14 + 4)
                    nc.scalar.activation(peb[:, :], PS[7][:, 256:264], ACT.Exp, bias=tnb[:, 0:1], accum_out=psb[:, 0:1]).then_inc(ffn0a_route_by_act, 1)
                    nc.scalar.activation(shb[:, :], PS[7][:, 264:265], ACT.Exp, scale=-1.0).then_inc(ffn0a_route_by_act, 1)

            @block.gpsimd
            def _(pool):
                nc.gpsimd.memset(NEGHALF[:, :], -0.5)
                nc.gpsimd.memset(onerow[:, :], 1.0)
                nc.gpsimd.memset(VXa[:, :, :], 1.0)
                nc.gpsimd.memset(VXb[:, :, :], 1.0)
                nc.gpsimd.memset(topa[:, :], -1.0)
                nc.gpsimd.memset(ppa[:, :], -1.0)
                nc.gpsimd.memset(topb[:, :], -1.0)
                nc.gpsimd.memset(ppb[:, :], -1.0).then_inc(ffn0a_setup_by_pool, 1)
                pool.sem_inc(ffn0a_residual_by_pool, 1)
                pool.wait_ge(ffn0a_setup_loads_sp, 176)
                pool.wait_ge(ffn0a_setup_by_pool, 1)
                pool.wait_ge(ffn0a_setup_by_dve, 1)
                with pool.Fori(0, 16) as i:
                    n = i
                    pool.wait_ge(ffn0a_norm_by_dve, n * 10 + 3)
                    nc.gpsimd.tensor_tensor(rstda[:, :], varea[:, :], NEGHALF[:, 0:1], ALU.pow).then_inc(ffn0a_rstd_by_pool, 1)
                    pool.wait_ge(ffn0a_norm_by_dve, n * 10 + 6)
                    nc.gpsimd.tensor_tensor(rstdb[:, :], vareb[:, :], NEGHALF[:, 0:1], ALU.pow).then_inc(ffn0a_rstd_by_pool, 1)
                    pool.wait_ge(ffn0a_norm_by_dve, n * 10 + 7)
                    nc.gpsimd.tensor_tensor(rstda[:, :], varea[:, :], NEGHALF[:, 0:1], ALU.pow).then_inc(ffn0a_rstd_by_pool, 1)
                    pool.wait_ge(ffn0a_norm_by_dve, n * 10 + 8)
                    nc.gpsimd.tensor_tensor(rstdb[:, :], vareb[:, :], NEGHALF[:, 0:1], ALU.pow).then_inc(ffn0a_rstd_by_pool, 1)
                    pool.wait_ge(ffn0a_rope_by_dve, n * 4 + 1)
                    nc.gpsimd.tensor_tensor(kTa[:, :, :].rearrange("p c t -> p (c t)"), k1a[:, :], k2a[:, :], ALU.add).then_inc(ffn0a_rope_by_pool, 1)
                    pool.wait_ge(ffn0a_rope_by_pool, n * 4 + 1)
                    nc.gpsimd.tensor_tensor(HXa[:, 8:16, :], kTa[:, 1, :].unsqueeze(1).to_broadcast([128, 8, 128]),
                                           HM[:, :].unsqueeze(2).to_broadcast([128, 8, 128]), ALU.mult)
                    pool.wait_ge(ffn0a_rope_by_dve, n * 4 + 2)
                    nc.gpsimd.tensor_tensor(kTb[:, :, :].rearrange("p c t -> p (c t)"), k1b[:, :], k2b[:, :], ALU.add).then_inc(ffn0a_rope_by_pool, 1)
                    pool.wait_ge(ffn0a_rope_by_pool, n * 4 + 2)
                    nc.gpsimd.tensor_tensor(HXb[:, 8:16, :], kTb[:, 1, :].unsqueeze(1).to_broadcast([128, 8, 128]),
                                           HM[:, :].unsqueeze(2).to_broadcast([128, 8, 128]), ALU.mult)
                    pool.wait_ge(ffn0a_rope_by_dve, n * 4 + 3)
                    nc.gpsimd.tensor_tensor(qTa[:, :, :].rearrange("p c t -> p (c t)"), t1a[:, :], t2a[:, :], ALU.add).then_inc(ffn0a_rope_by_pool, 1)
                    pool.wait_ge(ffn0a_rope_by_dve, n * 4 + 4)
                    nc.gpsimd.tensor_tensor(qTb[:, :, :].rearrange("p c t -> p (c t)"), t1b[:, :], t2b[:, :], ALU.add).then_inc(ffn0a_rope_by_pool, 1)
                    pool.wait_ge(ffn0a_residual_by_dve, n * 2 + 1)
                    nc.gpsimd.tensor_tensor(X[:, bass.ds((n * 2 + 0) * 256, 256)], X[:, bass.ds((n * 2 + 0) * 256, 256)], x2a[:, :], ALU.add)
                    pool.wait_ge(ffn0a_norm_by_dve, n * 10 + 9)
                    nc.gpsimd.tensor_tensor(rstda[:, :], varea[:, :], NEGHALF[:, 0:1], ALU.pow).then_inc(ffn0a_rstd_by_pool, 1)
                    pool.wait_ge(ffn0a_norm_by_dve, n * 10 + 10)
                    nc.gpsimd.tensor_tensor(rstdb[:, :], vareb[:, :], NEGHALF[:, 0:1], ALU.pow).then_inc(ffn0a_rstd_by_pool, 1)
                    nc.gpsimd.tensor_tensor(X[:, bass.ds((n * 2 + 1) * 256, 256)], X[:, bass.ds((n * 2 + 1) * 256, 256)], x2b[:, :], ALU.add).then_inc(ffn0a_residual_by_pool, 1)
                    pool.wait_ge(ffn0a_turned_by_act, n * 6 + 5)
                    pool.sem_inc(ffn0a_pool_passed, 1)
                    nc.gpsimd.tensor_copy(H0T[:, :, bass.ds((n * 2 + 0) * 128, 128)], xTa[:, :, :]).then_inc(ffn0a_kept_by_pool, 1)
                    pool.wait_ge(ffn0a_turned_by_act, n * 6 + 6)
                    pool.wait_ge(ffn0a_kept_by_pool, n * 1 + 1)
                    pool.sem_inc(ffn0a_pool_passed, 1)
                    nc.gpsimd.tensor_copy(H0T[:, :, bass.ds((n * 2 + 1) * 128, 128)], xTb[:, :, :])

            @block.sync
            def _(sp):
                nc.sync.dma_start(HM[:, :], io["head_mask"]).then_inc(ffn0a_setup_loads_sp, 16)
                nc.sync.dma_start(WQ[:, :, :], io["f0_wq"]).then_inc(ffn0a_setup_loads_sp, 16)
                nc.sync.dma_start(WK[:, :, :], io["f0_wk"]).then_inc(ffn0a_setup_loads_sp, 16)
                nc.sync.dma_start(WV[:, :, :], io["f0_wv"]).then_inc(ffn0a_setup_loads_sp, 16)
                nc.sync.dma_start(WO[:, :, :], io["f0_wo"]).then_inc(ffn0a_setup_loads_sp, 16)
                nc.sync.dma_start(WR[:, :, :], io["f0_router"]).then_inc(ffn0a_setup_loads_sp, 16)
                nc.sync.dma_start(BQKV[:, :], io["f0_bqkv"]).then_inc(ffn0a_setup_loads_sp, 16)
                nc.sync.dma_start(LNW[:, :], io["f0_ln"]).then_inc(ffn0a_setup_loads_sp, 16)
                nc.sync.dma_start(COS[:, :], io["cos"]).then_inc(ffn0a_setup_loads_sp, 16)
                nc.sync.dma_start(SIN[:, :], io["sin"]).then_inc(ffn0a_setup_loads_sp, 16)
                nc.sync.dma_start(NMASK[:, :], io["neg_causal"]).then_inc(ffn0a_setup_loads_sp, 16)

        nc.clear_and_free_semaphores(signals)
        nc.all_engine_barrier()

def ffn0b(nc, io, X, PS, IDENT, shared):
    ctx = ExitStack()
    with ctx:
        def sb(name, shape, dt=F32):
            return ctx.enter_context(nc.sbuf_tensor("ffn0b_" + name, shape, dt))

        signals = []

        def signal(name):
            signals.append(nc.alloc_semaphore(name))
            return signals[-1]

        H0T, CW0 = shared
        CWf = CW0[:, :, :].rearrange("p i e -> p (i e)")
        sl = sb("sl", [128, 3, 512])
        act_ = sb("act", [128, 12, 512])
        WG = sb("WG", [128, 2, 2304])
        WU = sb("WU", [128, 2, 2304])
        WD = sb("WD", [128, 18, 256])

        ffn0b_setup_loads_sp = signal("ffn0b_setup_loads_sp")
        ffn0b_hidden_by_pe = signal("ffn0b_hidden_by_pe")
        ffn0b_silu_by_act = signal("ffn0b_silu_by_act")
        ffn0b_hidden_by_dve = signal("ffn0b_hidden_by_dve")
        ffn0b_down_by_pe = signal("ffn0b_down_by_pe")
        ffn0b_combine_by_dve = signal("ffn0b_combine_by_dve")
        with nc.Block() as block:

            @block.tensor
            def _(pe):
                pe.wait_ge(ffn0b_setup_loads_sp, 48)
                with pe.Fori(0, 8) as g:
                    n = g
                    for w, bank in ((WG, PS[0]), (WU, PS[2])):
                        for c in range(2):
                            last = nc.tensor.matmul(bank[0:128, :], w[:, c, 0:128], H0T[:, c, bass.ds(g * 512, 512)], start=(c == 0), stop=(c == 1))
                    last.then_inc(ffn0b_hidden_by_pe, 1)
                    for w, bank in ((WG, PS[1]), (WU, PS[3])):
                        for c in range(2):
                            last = nc.tensor.matmul(bank[0:128, :], w[:, c, 128:256], H0T[:, c, bass.ds(g * 512, 512)], start=(c == 0), stop=(c == 1))
                    last.then_inc(ffn0b_hidden_by_pe, 1)
                    pe.wait_ge(ffn0b_hidden_by_dve, n * 16 + 1)
                    for w, bank in ((WG, PS[0]), (WU, PS[2])):
                        for c in range(2):
                            last = nc.tensor.matmul(bank[0:112, :], w[:, c, 256:368], H0T[:, c, bass.ds(g * 512, 512)], start=(c == 0), stop=(c == 1))
                    last.then_inc(ffn0b_hidden_by_pe, 1)
                    pe.wait_ge(ffn0b_hidden_by_dve, n * 16 + 2)
                    for w, bank in ((WG, PS[1]), (WU, PS[3])):
                        for c in range(2):
                            last = nc.tensor.matmul(bank[0:128, :], w[:, c, 384:512], H0T[:, c, bass.ds(g * 512, 512)], start=(c == 0), stop=(c == 1))
                    last.then_inc(ffn0b_hidden_by_pe, 1)
                    pe.wait_ge(ffn0b_hidden_by_dve, n * 16 + 3)
                    for w, bank in ((WG, PS[0]), (WU, PS[2])):
                        for c in range(2):
                            last = nc.tensor.matmul(bank[0:128, :], w[:, c, 512:640], H0T[:, c, bass.ds(g * 512, 512)], start=(c == 0), stop=(c == 1))
                    last.then_inc(ffn0b_hidden_by_pe, 1)
                    pe.wait_ge(ffn0b_hidden_by_dve, n * 16 + 4)
                    for w, bank in ((WG, PS[1]), (WU, PS[3])):
                        for c in range(2):
                            last = nc.tensor.matmul(bank[0:112, :], w[:, c, 640:752], H0T[:, c, bass.ds(g * 512, 512)], start=(c == 0), stop=(c == 1))
                    last.then_inc(ffn0b_hidden_by_pe, 1)
                    pe.wait_ge(ffn0b_hidden_by_dve, n * 16 + 5)
                    for w, bank in ((WG, PS[0]), (WU, PS[2])):
                        for c in range(2):
                            last = nc.tensor.matmul(bank[0:128, :], w[:, c, 768:896], H0T[:, c, bass.ds(g * 512, 512)], start=(c == 0), stop=(c == 1))
                    last.then_inc(ffn0b_hidden_by_pe, 1)
                    pe.wait_ge(ffn0b_hidden_by_dve, n * 16 + 6)
                    for w, bank in ((WG, PS[1]), (WU, PS[3])):
                        for c in range(2):
                            last = nc.tensor.matmul(bank[0:128, :], w[:, c, 896:1024], H0T[:, c, bass.ds(g * 512, 512)], start=(c == 0), stop=(c == 1))
                    last.then_inc(ffn0b_hidden_by_pe, 1)
                    for j in range(4):
                        for k, (slot, chunk, lo, hi) in enumerate([(0, 0, 0, 128), (2, 2, 0, 48)]):
                            last = nc.tensor.matmul(PS[4 + j // 2][:, (j % 2) * 256:(j % 2) * 256 + 256], act_[lo:hi, slot, j * 128:(j + 1) * 128], WD[lo:hi, chunk, :], start=(k == 0), stop=(k == 1))
                    last.then_inc(ffn0b_down_by_pe, 1)
                    for j in range(4):
                        for k, (slot, chunk, lo, hi) in enumerate([(1, 1, 0, 128), (2, 2, 64, 112)]):
                            last = nc.tensor.matmul(PS[6 + j // 2][:, (j % 2) * 256:(j % 2) * 256 + 256], act_[lo:hi, slot, j * 128:(j + 1) * 128], WD[lo:hi, chunk, :], start=(k == 0), stop=(k == 1))
                    last.then_inc(ffn0b_down_by_pe, 1)
                    pe.wait_ge(ffn0b_hidden_by_dve, n * 16 + 7)
                    for w, bank in ((WG, PS[0]), (WU, PS[2])):
                        for c in range(2):
                            last = nc.tensor.matmul(bank[0:112, :], w[:, c, 1024:1136], H0T[:, c, bass.ds(g * 512, 512)], start=(c == 0), stop=(c == 1))
                    last.then_inc(ffn0b_hidden_by_pe, 1)
                    pe.wait_ge(ffn0b_hidden_by_dve, n * 16 + 8)
                    for w, bank in ((WG, PS[1]), (WU, PS[3])):
                        for c in range(2):
                            last = nc.tensor.matmul(bank[0:128, :], w[:, c, 1152:1280], H0T[:, c, bass.ds(g * 512, 512)], start=(c == 0), stop=(c == 1))
                    last.then_inc(ffn0b_hidden_by_pe, 1)
                    for j in range(4):
                        for k, (slot, chunk, lo, hi) in enumerate([(3, 3, 0, 128), (5, 5, 0, 48)]):
                            last = nc.tensor.matmul(PS[4 + j // 2][:, (j % 2) * 256:(j % 2) * 256 + 256], act_[lo:hi, slot, j * 128:(j + 1) * 128], WD[lo:hi, chunk, :], start=(k == 0), stop=(k == 1))
                    last.then_inc(ffn0b_down_by_pe, 1)
                    pe.wait_ge(ffn0b_hidden_by_dve, n * 16 + 9)
                    for w, bank in ((WG, PS[0]), (WU, PS[2])):
                        for c in range(2):
                            last = nc.tensor.matmul(bank[0:128, :], w[:, c, 1280:1408], H0T[:, c, bass.ds(g * 512, 512)], start=(c == 0), stop=(c == 1))
                    last.then_inc(ffn0b_hidden_by_pe, 1)
                    pe.wait_ge(ffn0b_hidden_by_dve, n * 16 + 10)
                    for w, bank in ((WG, PS[1]), (WU, PS[3])):
                        for c in range(2):
                            last = nc.tensor.matmul(bank[0:112, :], w[:, c, 1408:1520], H0T[:, c, bass.ds(g * 512, 512)], start=(c == 0), stop=(c == 1))
                    last.then_inc(ffn0b_hidden_by_pe, 1)
                    for j in range(4):
                        for k, (slot, chunk, lo, hi) in enumerate([(4, 4, 0, 128), (5, 5, 64, 112)]):
                            last = nc.tensor.matmul(PS[6 + j // 2][:, (j % 2) * 256:(j % 2) * 256 + 256], act_[lo:hi, slot, j * 128:(j + 1) * 128], WD[lo:hi, chunk, :], start=(k == 0), stop=(k == 1))
                    last.then_inc(ffn0b_down_by_pe, 1)
                    pe.wait_ge(ffn0b_combine_by_dve, n * 7 + 3)
                    for j in range(4):
                        for k, (slot, chunk, lo, hi) in enumerate([(0, 6, 0, 128), (2, 8, 0, 48)]):
                            last = nc.tensor.matmul(PS[4 + j // 2][:, (j % 2) * 256:(j % 2) * 256 + 256], act_[lo:hi, slot, j * 128:(j + 1) * 128], WD[lo:hi, chunk, :], start=(k == 0), stop=(k == 1))
                    last.then_inc(ffn0b_down_by_pe, 1)
                    pe.wait_ge(ffn0b_hidden_by_dve, n * 16 + 11)
                    for w, bank in ((WG, PS[0]), (WU, PS[2])):
                        for c in range(2):
                            last = nc.tensor.matmul(bank[0:128, :], w[:, c, 1536:1664], H0T[:, c, bass.ds(g * 512, 512)], start=(c == 0), stop=(c == 1))
                    last.then_inc(ffn0b_hidden_by_pe, 1)
                    pe.wait_ge(ffn0b_hidden_by_dve, n * 16 + 12)
                    for w, bank in ((WG, PS[1]), (WU, PS[3])):
                        for c in range(2):
                            last = nc.tensor.matmul(bank[0:128, :], w[:, c, 1664:1792], H0T[:, c, bass.ds(g * 512, 512)], start=(c == 0), stop=(c == 1))
                    last.then_inc(ffn0b_hidden_by_pe, 1)
                    pe.wait_ge(ffn0b_hidden_by_dve, n * 16 + 13)
                    for w, bank in ((WG, PS[0]), (WU, PS[2])):
                        for c in range(2):
                            last = nc.tensor.matmul(bank[0:128, :], w[:, c, 1792:1920], H0T[:, c, bass.ds(g * 512, 512)], start=(c == 0), stop=(c == 1))
                    last.then_inc(ffn0b_hidden_by_pe, 1)
                    pe.wait_ge(ffn0b_hidden_by_dve, n * 16 + 14)
                    for w, bank in ((WG, PS[1]), (WU, PS[3])):
                        for c in range(2):
                            last = nc.tensor.matmul(bank[0:128, :], w[:, c, 1920:2048], H0T[:, c, bass.ds(g * 512, 512)], start=(c == 0), stop=(c == 1))
                    last.then_inc(ffn0b_hidden_by_pe, 1)
                    pe.wait_ge(ffn0b_hidden_by_dve, n * 16 + 15)
                    for w, bank in ((WG, PS[0]), (WU, PS[2])):
                        for c in range(2):
                            last = nc.tensor.matmul(bank[0:128, :], w[:, c, 2048:2176], H0T[:, c, bass.ds(g * 512, 512)], start=(c == 0), stop=(c == 1))
                    last.then_inc(ffn0b_hidden_by_pe, 1)
                    pe.wait_ge(ffn0b_hidden_by_dve, n * 16 + 16)
                    for w, bank in ((WG, PS[1]), (WU, PS[3])):
                        for c in range(2):
                            last = nc.tensor.matmul(bank[0:128, :], w[:, c, 2176:2304], H0T[:, c, bass.ds(g * 512, 512)], start=(c == 0), stop=(c == 1))
                    last.then_inc(ffn0b_hidden_by_pe, 1)
                    for j in range(4):
                        for k, (slot, chunk, lo, hi) in enumerate([(1, 7, 0, 128), (2, 8, 64, 112)]):
                            last = nc.tensor.matmul(PS[6 + j // 2][:, (j % 2) * 256:(j % 2) * 256 + 256], act_[lo:hi, slot, j * 128:(j + 1) * 128], WD[lo:hi, chunk, :], start=(k == 0), stop=(k == 1))
                    last.then_inc(ffn0b_down_by_pe, 1)
                    for j in range(4):
                        for k, (slot, chunk, lo, hi) in enumerate([(3, 9, 0, 128), (5, 11, 0, 48)]):
                            last = nc.tensor.matmul(PS[4 + j // 2][:, (j % 2) * 256:(j % 2) * 256 + 256], act_[lo:hi, slot, j * 128:(j + 1) * 128], WD[lo:hi, chunk, :], start=(k == 0), stop=(k == 1))
                    last.then_inc(ffn0b_down_by_pe, 1)
                    pe.wait_ge(ffn0b_combine_by_dve, n * 7 + 5)
                    for j in range(4):
                        for k, (slot, chunk, lo, hi) in enumerate([(4, 10, 0, 128), (5, 11, 64, 112)]):
                            last = nc.tensor.matmul(PS[6 + j // 2][:, (j % 2) * 256:(j % 2) * 256 + 256], act_[lo:hi, slot, j * 128:(j + 1) * 128], WD[lo:hi, chunk, :], start=(k == 0), stop=(k == 1))
                    last.then_inc(ffn0b_down_by_pe, 1)
                    pe.wait_ge(ffn0b_combine_by_dve, n * 7 + 6)
                    for j in range(4):
                        for k, (slot, chunk, lo, hi) in enumerate([(6, 12, 0, 128), (7, 13, 0, 128), (8, 14, 0, 128), (9, 15, 0, 128), (10, 16, 0, 128), (11, 17, 0, 128)]):
                            last = nc.tensor.matmul(PS[4 + j // 2][:, (j % 2) * 256:(j % 2) * 256 + 256], act_[lo:hi, slot, j * 128:(j + 1) * 128], WD[lo:hi, chunk, :], start=(k == 0), stop=(k == 5))
                    last.then_inc(ffn0b_down_by_pe, 1)

            @block.vector
            def _(dve):
                dve.wait_ge(ffn0b_setup_loads_sp, 48)
                with dve.Fori(0, 8) as g:
                    n = g
                    dve.wait_ge(ffn0b_silu_by_act, n * 18 + 1)
                    nc.vector.tensor_tensor(act_[0:128, 0, :], sl[0:128, 0, :], PS[2][0:128, :], ALU.mult).then_inc(ffn0b_hidden_by_dve, 1)
                    dve.wait_ge(ffn0b_silu_by_act, n * 18 + 2)
                    nc.vector.tensor_tensor(act_[0:128, 1, :], sl[0:128, 1, :], PS[3][0:128, :], ALU.mult).then_inc(ffn0b_hidden_by_dve, 1)
                    dve.wait_ge(ffn0b_silu_by_act, n * 18 + 3)
                    nc.vector.tensor_tensor(act_[0:112, 2, :], sl[0:112, 2, :], PS[2][0:112, :], ALU.mult).then_inc(ffn0b_hidden_by_dve, 1)
                    dve.wait_ge(ffn0b_silu_by_act, n * 18 + 4)
                    nc.vector.tensor_tensor(act_[0:128, 3, :], sl[0:128, 0, :], PS[3][0:128, :], ALU.mult).then_inc(ffn0b_hidden_by_dve, 1)
                    dve.wait_ge(ffn0b_silu_by_act, n * 18 + 5)
                    nc.vector.tensor_tensor(act_[0:128, 4, :], sl[0:128, 1, :], PS[2][0:128, :], ALU.mult).then_inc(ffn0b_hidden_by_dve, 1)
                    dve.wait_ge(ffn0b_silu_by_act, n * 18 + 6)
                    nc.vector.tensor_tensor(act_[0:112, 5, :], sl[0:112, 2, :], PS[3][0:112, :], ALU.mult).then_inc(ffn0b_hidden_by_dve, 1)
                    dve.wait_ge(ffn0b_silu_by_act, n * 18 + 7)
                    dve.wait_ge(ffn0b_down_by_pe, n * 9 + 1)
                    nc.vector.tensor_tensor(act_[0:128, 0, :], sl[0:128, 0, :], PS[2][0:128, :], ALU.mult).then_inc(ffn0b_hidden_by_dve, 1)
                    for j in range(4):
                        xs = X[:, bass.ds(g * 1024 + j * 256, 256)]
                        last = nc.vector.scalar_tensor_tensor(xs, PS[4 + j // 2][:, (j % 2) * 256:(j % 2) * 256 + 256], CWf[:, bass.ds(g * 36 + 0 + j * 9, 1)], xs, ALU.mult, ALU.add)
                    last.then_inc(ffn0b_combine_by_dve, 1)
                    dve.wait_ge(ffn0b_silu_by_act, n * 18 + 8)
                    dve.wait_ge(ffn0b_down_by_pe, n * 9 + 2)
                    nc.vector.tensor_tensor(act_[0:128, 1, :], sl[0:128, 1, :], PS[3][0:128, :], ALU.mult).then_inc(ffn0b_hidden_by_dve, 1)
                    dve.wait_ge(ffn0b_combine_by_dve, n * 7 + 1)
                    for j in range(4):
                        xs = X[:, bass.ds(g * 1024 + j * 256, 256)]
                        last = nc.vector.scalar_tensor_tensor(xs, PS[6 + j // 2][:, (j % 2) * 256:(j % 2) * 256 + 256], CWf[:, bass.ds(g * 36 + 1 + j * 9, 1)], xs, ALU.mult, ALU.add)
                    last.then_inc(ffn0b_combine_by_dve, 1)
                    dve.wait_ge(ffn0b_silu_by_act, n * 18 + 9)
                    nc.vector.tensor_tensor(act_[0:112, 2, :], sl[0:112, 2, :], PS[2][0:112, :], ALU.mult).then_inc(ffn0b_hidden_by_dve, 1)
                    dve.wait_ge(ffn0b_down_by_pe, n * 9 + 3)
                    dve.wait_ge(ffn0b_silu_by_act, n * 18 + 10)
                    nc.vector.tensor_tensor(act_[0:128, 3, :], sl[0:128, 0, :], PS[3][0:128, :], ALU.mult).then_inc(ffn0b_hidden_by_dve, 1)
                    dve.wait_ge(ffn0b_combine_by_dve, n * 7 + 2)
                    for j in range(4):
                        xs = X[:, bass.ds(g * 1024 + j * 256, 256)]
                        last = nc.vector.scalar_tensor_tensor(xs, PS[4 + j // 2][:, (j % 2) * 256:(j % 2) * 256 + 256], CWf[:, bass.ds(g * 36 + 2 + j * 9, 1)], xs, ALU.mult, ALU.add)
                    last.then_inc(ffn0b_combine_by_dve, 1)
                    dve.wait_ge(ffn0b_silu_by_act, n * 18 + 11)
                    dve.wait_ge(ffn0b_down_by_pe, n * 9 + 4)
                    nc.vector.tensor_tensor(act_[0:128, 4, :], sl[0:128, 1, :], PS[2][0:128, :], ALU.mult).then_inc(ffn0b_hidden_by_dve, 1)
                    dve.wait_ge(ffn0b_silu_by_act, n * 18 + 12)
                    nc.vector.tensor_tensor(act_[0:112, 5, :], sl[0:112, 2, :], PS[3][0:112, :], ALU.mult).then_inc(ffn0b_hidden_by_dve, 1)
                    dve.wait_ge(ffn0b_combine_by_dve, n * 7 + 3)
                    for j in range(4):
                        xs = X[:, bass.ds(g * 1024 + j * 256, 256)]
                        last = nc.vector.scalar_tensor_tensor(xs, PS[6 + j // 2][:, (j % 2) * 256:(j % 2) * 256 + 256], CWf[:, bass.ds(g * 36 + 3 + j * 9, 1)], xs, ALU.mult, ALU.add)
                    last.then_inc(ffn0b_combine_by_dve, 1)
                    dve.wait_ge(ffn0b_down_by_pe, n * 9 + 5)
                    dve.wait_ge(ffn0b_combine_by_dve, n * 7 + 4)
                    for j in range(4):
                        xs = X[:, bass.ds(g * 1024 + j * 256, 256)]
                        last = nc.vector.scalar_tensor_tensor(xs, PS[4 + j // 2][:, (j % 2) * 256:(j % 2) * 256 + 256], CWf[:, bass.ds(g * 36 + 4 + j * 9, 1)], xs, ALU.mult, ALU.add)
                    dve.wait_ge(ffn0b_silu_by_act, n * 18 + 13)
                    nc.vector.tensor_tensor(act_[0:128, 6, :], sl[0:128, 0, :], PS[2][0:128, :], ALU.mult).then_inc(ffn0b_hidden_by_dve, 1)
                    dve.wait_ge(ffn0b_silu_by_act, n * 18 + 14)
                    nc.vector.tensor_tensor(act_[0:128, 7, :], sl[0:128, 1, :], PS[3][0:128, :], ALU.mult).then_inc(ffn0b_hidden_by_dve, 1)
                    dve.wait_ge(ffn0b_silu_by_act, n * 18 + 15)
                    nc.vector.tensor_tensor(act_[0:128, 8, :], sl[0:128, 2, :], PS[2][0:128, :], ALU.mult).then_inc(ffn0b_hidden_by_dve, 1)
                    dve.wait_ge(ffn0b_silu_by_act, n * 18 + 16)
                    nc.vector.tensor_tensor(act_[0:128, 9, :], sl[0:128, 0, :], PS[3][0:128, :], ALU.mult).then_inc(ffn0b_hidden_by_dve, 1)
                    dve.wait_ge(ffn0b_silu_by_act, n * 18 + 17)
                    nc.vector.tensor_tensor(act_[0:128, 10, :], sl[0:128, 1, :], PS[2][0:128, :], ALU.mult)
                    dve.wait_ge(ffn0b_silu_by_act, n * 18 + 18)
                    nc.vector.tensor_tensor(act_[0:128, 11, :], sl[0:128, 2, :], PS[3][0:128, :], ALU.mult)
                    dve.wait_ge(ffn0b_down_by_pe, n * 9 + 6)
                    for j in range(4):
                        xs = X[:, bass.ds(g * 1024 + j * 256, 256)]
                        last = nc.vector.scalar_tensor_tensor(xs, PS[6 + j // 2][:, (j % 2) * 256:(j % 2) * 256 + 256], CWf[:, bass.ds(g * 36 + 5 + j * 9, 1)], xs, ALU.mult, ALU.add)
                    last.then_inc(ffn0b_combine_by_dve, 1)
                    dve.wait_ge(ffn0b_down_by_pe, n * 9 + 7)
                    dve.wait_ge(ffn0b_combine_by_dve, n * 7 + 5)
                    for j in range(4):
                        xs = X[:, bass.ds(g * 1024 + j * 256, 256)]
                        last = nc.vector.scalar_tensor_tensor(xs, PS[4 + j // 2][:, (j % 2) * 256:(j % 2) * 256 + 256], CWf[:, bass.ds(g * 36 + 6 + j * 9, 1)], xs, ALU.mult, ALU.add)
                    last.then_inc(ffn0b_combine_by_dve, 1)
                    dve.wait_ge(ffn0b_down_by_pe, n * 9 + 8)
                    dve.wait_ge(ffn0b_combine_by_dve, n * 7 + 6)
                    for j in range(4):
                        xs = X[:, bass.ds(g * 1024 + j * 256, 256)]
                        last = nc.vector.scalar_tensor_tensor(xs, PS[6 + j // 2][:, (j % 2) * 256:(j % 2) * 256 + 256], CWf[:, bass.ds(g * 36 + 7 + j * 9, 1)], xs, ALU.mult, ALU.add)
                    last.then_inc(ffn0b_combine_by_dve, 1)
                    dve.wait_ge(ffn0b_down_by_pe, n * 9 + 9)
                    dve.wait_ge(ffn0b_combine_by_dve, n * 7 + 7)
                    for j in range(4):
                        xs = X[:, bass.ds(g * 1024 + j * 256, 256)]
                        last = nc.vector.scalar_tensor_tensor(xs, PS[4 + j // 2][:, (j % 2) * 256:(j % 2) * 256 + 256], CWf[:, bass.ds(g * 36 + 8 + j * 9, 1)], xs, ALU.mult, ALU.add)

            @block.scalar
            def _(act):
                act.wait_ge(ffn0b_setup_loads_sp, 48)
                with act.Fori(0, 8) as g:
                    n = g
                    act.wait_ge(ffn0b_hidden_by_pe, n * 18 + 1)
                    nc.scalar.activation(sl[0:128, 0, :], PS[0][0:128, :], ACT.Silu).then_inc(ffn0b_silu_by_act, 1)
                    act.wait_ge(ffn0b_hidden_by_pe, n * 18 + 2)
                    nc.scalar.activation(sl[0:128, 1, :], PS[1][0:128, :], ACT.Silu).then_inc(ffn0b_silu_by_act, 1)
                    act.wait_ge(ffn0b_hidden_by_pe, n * 18 + 3)
                    nc.scalar.activation(sl[0:112, 2, :], PS[0][0:112, :], ACT.Silu).then_inc(ffn0b_silu_by_act, 1)
                    act.wait_ge(ffn0b_hidden_by_pe, n * 18 + 4)
                    nc.scalar.activation(sl[0:128, 0, :], PS[1][0:128, :], ACT.Silu).then_inc(ffn0b_silu_by_act, 1)
                    act.wait_ge(ffn0b_hidden_by_pe, n * 18 + 5)
                    nc.scalar.activation(sl[0:128, 1, :], PS[0][0:128, :], ACT.Silu).then_inc(ffn0b_silu_by_act, 1)
                    act.wait_ge(ffn0b_hidden_by_pe, n * 18 + 6)
                    nc.scalar.activation(sl[0:112, 2, :], PS[1][0:112, :], ACT.Silu).then_inc(ffn0b_silu_by_act, 1)
                    act.wait_ge(ffn0b_hidden_by_pe, n * 18 + 7)
                    nc.scalar.activation(sl[0:128, 0, :], PS[0][0:128, :], ACT.Silu).then_inc(ffn0b_silu_by_act, 1)
                    act.wait_ge(ffn0b_hidden_by_pe, n * 18 + 8)
                    nc.scalar.activation(sl[0:128, 1, :], PS[1][0:128, :], ACT.Silu).then_inc(ffn0b_silu_by_act, 1)
                    act.wait_ge(ffn0b_hidden_by_pe, n * 18 + 9)
                    nc.scalar.activation(sl[0:112, 2, :], PS[0][0:112, :], ACT.Silu).then_inc(ffn0b_silu_by_act, 1)
                    act.wait_ge(ffn0b_hidden_by_pe, n * 18 + 10)
                    nc.scalar.activation(sl[0:128, 0, :], PS[1][0:128, :], ACT.Silu).then_inc(ffn0b_silu_by_act, 1)
                    act.wait_ge(ffn0b_hidden_by_pe, n * 18 + 11)
                    nc.scalar.activation(sl[0:128, 1, :], PS[0][0:128, :], ACT.Silu).then_inc(ffn0b_silu_by_act, 1)
                    act.wait_ge(ffn0b_hidden_by_pe, n * 18 + 12)
                    nc.scalar.activation(sl[0:112, 2, :], PS[1][0:112, :], ACT.Silu).then_inc(ffn0b_silu_by_act, 1)
                    act.wait_ge(ffn0b_hidden_by_pe, n * 18 + 13)
                    nc.scalar.activation(sl[0:128, 0, :], PS[0][0:128, :], ACT.Silu).then_inc(ffn0b_silu_by_act, 1)
                    act.wait_ge(ffn0b_hidden_by_pe, n * 18 + 14)
                    nc.scalar.activation(sl[0:128, 1, :], PS[1][0:128, :], ACT.Silu).then_inc(ffn0b_silu_by_act, 1)
                    act.wait_ge(ffn0b_hidden_by_pe, n * 18 + 15)
                    nc.scalar.activation(sl[0:128, 2, :], PS[0][0:128, :], ACT.Silu).then_inc(ffn0b_silu_by_act, 1)
                    act.wait_ge(ffn0b_hidden_by_pe, n * 18 + 16)
                    nc.scalar.activation(sl[0:128, 0, :], PS[1][0:128, :], ACT.Silu).then_inc(ffn0b_silu_by_act, 1)
                    act.wait_ge(ffn0b_hidden_by_pe, n * 18 + 17)
                    nc.scalar.activation(sl[0:128, 1, :], PS[0][0:128, :], ACT.Silu).then_inc(ffn0b_silu_by_act, 1)
                    act.wait_ge(ffn0b_hidden_by_pe, n * 18 + 18)
                    nc.scalar.activation(sl[0:128, 2, :], PS[1][0:128, :], ACT.Silu).then_inc(ffn0b_silu_by_act, 1)

            @block.gpsimd
            def _(pool):
                pass

            @block.sync
            def _(sp):
                nc.sync.dma_start(WG[:, :, :], io["e0_gate"]).then_inc(ffn0b_setup_loads_sp, 16)
                nc.sync.dma_start(WU[:, :, :], io["e0_up"]).then_inc(ffn0b_setup_loads_sp, 16)
                nc.sync.dma_start(WD[:, :, :], io["e0_down"]).then_inc(ffn0b_setup_loads_sp, 16)

        nc.clear_and_free_semaphores(signals)
        nc.all_engine_barrier()

def infini(nc, io, X, PS, IDENT, shared):
    ctx = ExitStack()
    with ctx:
        def sb(name, shape, dt=F32):
            return ctx.enter_context(nc.sbuf_tensor("infini_" + name, shape, dt))

        signals = []

        def signal(name):
            signals.append(nc.alloc_semaphore(name))
            return signals[-1]

        statsa = sb("statsa", [128, 6])
        mva = sb("mva", [128, 2])
        varea = sb("varea", [128, 1])
        rstda = sb("rstda", [128, 1])
        xna = sb("xna", [128, 256])
        qTa = sb("qTa", [128, 2, 128])
        HXa = sb("HXa", [128, 16, 128])
        kTa = sb("kTa", [128, 2, 128])
        VXa = sb("VXa", [128, 16, 17])
        SCa = sb("SCa", [128, 16, 128])
        PWa = sb("PWa", [128, 16, 128])
        ctx_a = sb("ctx_a", [128, 256])
        cTa = sb("cTa", [128, 2, 128])
        xTa = sb("xTa", [128, 2, 128])
        rda = sb("rda", [128, 16])
        mxa = sb("mxa", [128, 16])
        nmxa = sb("nmxa", [128, 16])
        sTa = sb("sTa", [128, 2, 128])
        ena = sb("ena", [128, 256])
        moa = sb("moa", [128, 256])
        rawa = sb("rawa", [128, 4])
        ema = sb("ema", [128, 4])
        cfa = sb("cfa", [128, 4])
        rca = sb("rca", [128, 4])
        m1a = sb("m1a", [128, 1])
        n1a = sb("n1a", [128, 1])
        s1a = sb("s1a", [128, 1])
        r1a = sb("r1a", [128, 1])
        statsb = sb("statsb", [128, 6])
        mvb = sb("mvb", [128, 2])
        vareb = sb("vareb", [128, 1])
        rstdb = sb("rstdb", [128, 1])
        xnb = sb("xnb", [128, 256])
        qTb = sb("qTb", [128, 2, 128])
        HXb = sb("HXb", [128, 16, 128])
        kTb = sb("kTb", [128, 2, 128])
        VXb = sb("VXb", [128, 16, 17])
        SCb = sb("SCb", [128, 16, 128])
        PWb = sb("PWb", [128, 16, 128])
        ctx_b = sb("ctx_b", [128, 256])
        cTb = sb("cTb", [128, 2, 128])
        xTb = sb("xTb", [128, 2, 128])
        rdb = sb("rdb", [128, 16])
        mxb = sb("mxb", [128, 16])
        nmxb = sb("nmxb", [128, 16])
        sTb = sb("sTb", [128, 2, 128])
        enb = sb("enb", [128, 256])
        mob = sb("mob", [128, 256])
        rawb = sb("rawb", [128, 4])
        emb = sb("emb", [128, 4])
        cfb = sb("cfb", [128, 4])
        rcb = sb("rcb", [128, 4])
        m1b = sb("m1b", [128, 1])
        n1b = sb("n1b", [128, 1])
        s1b = sb("s1b", [128, 1])
        r1b = sb("r1b", [128, 1])
        NEGHALF = sb("neghalf", [128, 16])
        HM = sb("hm", [128, 8])
        onerow = sb("onerow", [1, 128])
        WQ = sb("WQ", [128, 2, 256])
        WK = sb("WK", [128, 2, 256])
        WV = sb("WV", [128, 2, 256])
        WO = sb("WO", [128, 2, 256])
        MEM = sb("MEM", [128, 2, 1024])
        MN = sb("MN", [128, 2, 4])
        GT = sb("GT", [128, 1])
        BM = sb("BM", [128, 128])
        NMASK = sb("NMASK", [128, 512])
        GS = sb("gs", [128, 1])
        GL = sb("gl", [128, 1])
        def by_head(t):
            return t.rearrange("p (h d) -> p h d", d=16)

        infini_setup_loads_sp = signal("infini_setup_loads_sp")
        infini_setup_by_pool = signal("infini_setup_by_pool")
        infini_setup_by_act = signal("infini_setup_by_act")
        infini_setup_by_dve = signal("infini_setup_by_dve")
        infini_norm_by_dve = signal("infini_norm_by_dve")
        infini_rstd_by_pool = signal("infini_rstd_by_pool")
        infini_normed_by_dve = signal("infini_normed_by_dve")
        infini_turned_by_pe = signal("infini_turned_by_pe")
        infini_turned_by_act = signal("infini_turned_by_act")
        infini_projected_by_pe = signal("infini_projected_by_pe")
        infini_keys_by_act = signal("infini_keys_by_act")
        infini_queries_by_act = signal("infini_queries_by_act")
        infini_expand_by_pool = signal("infini_expand_by_pool")
        infini_sigma_by_dve = signal("infini_sigma_by_dve")
        infini_sigma_by_act = signal("infini_sigma_by_act")
        infini_memory_by_pe = signal("infini_memory_by_pe")
        infini_memnorm_by_dve = signal("infini_memnorm_by_dve")
        infini_memsoft_by_dve = signal("infini_memsoft_by_dve")
        infini_relevance_by_pe = signal("infini_relevance_by_pe")
        infini_memsoft_by_act = signal("infini_memsoft_by_act")
        infini_mixmem_by_dve = signal("infini_mixmem_by_dve")
        infini_scores_by_pe = signal("infini_scores_by_pe")
        infini_masked_by_dve = signal("infini_masked_by_dve")
        infini_max_by_dve = signal("infini_max_by_dve")
        infini_exp_by_act = signal("infini_exp_by_act")
        infini_pturn_by_pe = signal("infini_pturn_by_pe")
        infini_pturn_by_dve = signal("infini_pturn_by_dve")
        infini_pturn_by_act = signal("infini_pturn_by_act")
        infini_attended_by_pe = signal("infini_attended_by_pe")
        infini_normalize_by_dve = signal("infini_normalize_by_dve")
        infini_mixed_by_pool = signal("infini_mixed_by_pool")
        infini_outproj_by_pe = signal("infini_outproj_by_pe")
        infini_residual_by_dve = signal("infini_residual_by_dve")
        infini_dve_passed = signal("infini_dve_passed")
        with nc.Block() as block:

            @block.tensor
            def _(pe):
                pe.wait_ge(infini_setup_loads_sp, 160)
                pe.wait_ge(infini_setup_by_pool, 1)
                pe.wait_ge(infini_setup_by_act, 1)
                pe.wait_ge(infini_setup_by_dve, 3)
                with pe.Fori(0, 16) as i:
                    n = i
                    pe.wait_ge(infini_normed_by_dve, n * 2 + 1)
                    for c in range(2):
                        last = nc.tensor.transpose(PS[4][:, c * 128:(c + 1) * 128], xnb[:, c * 128:(c + 1) * 128], IDENT[:, :])
                    last.then_inc(infini_turned_by_pe, 1)
                    pe.wait_ge(infini_normed_by_dve, n * 2 + 2)
                    for c in range(2):
                        last = nc.tensor.transpose(PS[0][:, c * 128:(c + 1) * 128], xna[:, c * 128:(c + 1) * 128], IDENT[:, :])
                    last.then_inc(infini_turned_by_pe, 1)
                    pe.wait_ge(infini_turned_by_act, n * 4 + 1)
                    for e in range(2):
                        for c in range(2):
                            last = nc.tensor.matmul(PS[4][:, 0 + e * 128:0 + (e + 1) * 128], WQ[:, c, e * 128:(e + 1) * 128], xTb[:, c, :], start=(c == 0), stop=(c == 1))
                    pe.wait_ge(infini_turned_by_act, n * 4 + 2)
                    for e in range(2):
                        for c in range(2):
                            last = nc.tensor.matmul(PS[0][:, 0 + e * 128:0 + (e + 1) * 128], WQ[:, c, e * 128:(e + 1) * 128], xTa[:, c, :], start=(c == 0), stop=(c == 1))
                    for e in range(2):
                        for c in range(2):
                            last = nc.tensor.matmul(PS[4][:, 256 + e * 128:256 + (e + 1) * 128], WK[:, c, e * 128:(e + 1) * 128], xTb[:, c, :], start=(c == 0), stop=(c == 1))
                    last.then_inc(infini_projected_by_pe, 1)
                    for e in range(2):
                        for c in range(2):
                            last = nc.tensor.matmul(PS[0][:, 256 + e * 128:256 + (e + 1) * 128], WK[:, c, e * 128:(e + 1) * 128], xTa[:, c, :], start=(c == 0), stop=(c == 1))
                    last.then_inc(infini_projected_by_pe, 1)
                    for c in range(2):
                        last = nc.tensor.matmul(PS[5][:, 0:256], xTb[:, c, :], WV[:, c, :], start=(c == 0), stop=(c == 1))
                    last.then_inc(infini_projected_by_pe, 1)
                    for c in range(2):
                        last = nc.tensor.matmul(PS[1][:, 0:256], xTa[:, c, :], WV[:, c, :], start=(c == 0), stop=(c == 1))
                    last.then_inc(infini_projected_by_pe, 1)
                    pe.wait_ge(infini_sigma_by_dve, n * 4 + 3)
                    for c in range(2):
                        last = nc.tensor.matmul(PS[5][:, 256:260], sTb[:, c, :], MN[:, c, :], start=(c == 0), stop=(c == 1))
                    last.then_inc(infini_memory_by_pe, 1)
                    for k in range(2):
                        for c in range(2):
                            last = nc.tensor.matmul(PS[6 + k][:, :], sTb[:, c, :], MEM[:, c, k * 512:(k + 1) * 512], start=(c == 0), stop=(c == 1))
                    pe.wait_ge(infini_sigma_by_dve, n * 4 + 4)
                    for c in range(2):
                        last = nc.tensor.matmul(PS[1][:, 256:260], sTa[:, c, :], MN[:, c, :], start=(c == 0), stop=(c == 1))
                    last.then_inc(infini_memory_by_pe, 1)
                    pe.wait_ge(infini_memnorm_by_dve, n * 2 + 1)
                    last = nc.tensor.matmul(PS[5][:, 264:268], BM[:, :], rawb[:, :], start=True, stop=True)
                    last.then_inc(infini_relevance_by_pe, 1)
                    for k in range(2):
                        for c in range(2):
                            last = nc.tensor.matmul(PS[2 + k][:, :], sTa[:, c, :], MEM[:, c, k * 512:(k + 1) * 512], start=(c == 0), stop=(c == 1))
                    pe.wait_ge(infini_memnorm_by_dve, n * 2 + 2)
                    last = nc.tensor.matmul(PS[1][:, 264:268], BM[:, :], rawa[:, :], start=True, stop=True)
                    last.then_inc(infini_relevance_by_pe, 1)
                    pe.wait_ge(infini_expand_by_pool, n * 2 + 1)
                    pe.wait_ge(infini_mixmem_by_dve, n * 8 + 4)
                    for k in range(2):
                        last = nc.tensor.matmul(PS[6 + k][:, :], qTb[:, 1, :], HXb[:, 8 + 4 * k:8 + 4 * k + 4, :], start=True, stop=True)
                    last.then_inc(infini_scores_by_pe, 1)
                    for k in range(2):
                        last = nc.tensor.matmul(PS[4 + k][:, :], qTb[:, 0, :], HXb[:, 0 + 4 * k:0 + 4 * k + 4, :], start=True, stop=True)
                    last.then_inc(infini_scores_by_pe, 1)
                    pe.wait_ge(infini_expand_by_pool, n * 2 + 2)
                    pe.wait_ge(infini_mixmem_by_dve, n * 8 + 8)
                    for k in range(2):
                        last = nc.tensor.matmul(PS[2 + k][:, :], qTa[:, 1, :], HXa[:, 8 + 4 * k:8 + 4 * k + 4, :], start=True, stop=True)
                    last.then_inc(infini_scores_by_pe, 1)
                    for k in range(2):
                        last = nc.tensor.matmul(PS[0 + k][:, :], qTa[:, 0, :], HXa[:, 0 + 4 * k:0 + 4 * k + 4, :], start=True, stop=True)
                    last.then_inc(infini_scores_by_pe, 1)
                    pe.wait_ge(infini_exp_by_act, n * 6 + 1)
                    for k in range(4):
                        last = nc.tensor.transpose(PS[7][:, k * 128:(k + 1) * 128], SCb[:, 12 + k, :], IDENT[:, :])
                    last.then_inc(infini_pturn_by_pe, 1)
                    pe.wait_ge(infini_exp_by_act, n * 6 + 2)
                    for k in range(4):
                        last = nc.tensor.transpose(PS[6][:, k * 128:(k + 1) * 128], SCb[:, 8 + k, :], IDENT[:, :])
                    last.then_inc(infini_pturn_by_pe, 1)
                    pe.wait_ge(infini_exp_by_act, n * 6 + 3)
                    for k in range(4):
                        last = nc.tensor.transpose(PS[4][:, k * 128:(k + 1) * 128], SCb[:, 0 + k, :], IDENT[:, :])
                    last.then_inc(infini_pturn_by_pe, 1)
                    for k in range(4):
                        last = nc.tensor.transpose(PS[5][:, k * 128:(k + 1) * 128], SCb[:, 4 + k, :], IDENT[:, :])
                    last.then_inc(infini_pturn_by_pe, 1)
                    pe.wait_ge(infini_exp_by_act, n * 6 + 4)
                    for k in range(4):
                        last = nc.tensor.transpose(PS[3][:, k * 128:(k + 1) * 128], SCa[:, 12 + k, :], IDENT[:, :])
                    last.then_inc(infini_pturn_by_pe, 1)
                    pe.wait_ge(infini_exp_by_act, n * 6 + 5)
                    for k in range(4):
                        last = nc.tensor.transpose(PS[1][:, k * 128:(k + 1) * 128], SCa[:, 4 + k, :], IDENT[:, :])
                    last.then_inc(infini_pturn_by_pe, 1)
                    for k in range(4):
                        last = nc.tensor.transpose(PS[2][:, k * 128:(k + 1) * 128], SCa[:, 8 + k, :], IDENT[:, :])
                    last.then_inc(infini_pturn_by_pe, 1)
                    pe.wait_ge(infini_exp_by_act, n * 6 + 6)
                    for k in range(4):
                        last = nc.tensor.transpose(PS[0][:, k * 128:(k + 1) * 128], SCa[:, 0 + k, :], IDENT[:, :])
                    last.then_inc(infini_pturn_by_pe, 1)
                    pe.wait_ge(infini_pturn_by_dve, n * 2 + 1)
                    pe.wait_ge(infini_pturn_by_act, n * 2 + 1)
                    for head in range(16):
                        last = nc.tensor.matmul(PS[4][:, head * 17:head * 17 + 17], PWb[:, head, :], VXb[:, head, :], start=True, stop=True)
                    last.then_inc(infini_attended_by_pe, 1)
                    pe.wait_ge(infini_pturn_by_dve, n * 2 + 2)
                    pe.wait_ge(infini_pturn_by_act, n * 2 + 2)
                    for head in range(16):
                        last = nc.tensor.matmul(PS[0][:, head * 17:head * 17 + 17], PWa[:, head, :], VXa[:, head, :], start=True, stop=True)
                    last.then_inc(infini_attended_by_pe, 1)
                    pe.wait_ge(infini_mixed_by_pool, n * 2 + 1)
                    for c in range(2):
                        last = nc.tensor.transpose(PS[5][:, c * 128:(c + 1) * 128], ctx_b[:, c * 128:(c + 1) * 128], IDENT[:, :])
                    last.then_inc(infini_turned_by_pe, 1)
                    pe.wait_ge(infini_turned_by_act, n * 4 + 3)
                    for c in range(2):
                        last = nc.tensor.matmul(PS[6][:, 0:256], cTb[:, c, :], WO[:, c, :], start=(c == 0), stop=(c == 1))
                    last.then_inc(infini_outproj_by_pe, 1)
                    pe.wait_ge(infini_mixed_by_pool, n * 2 + 2)
                    for c in range(2):
                        last = nc.tensor.transpose(PS[1][:, c * 128:(c + 1) * 128], ctx_a[:, c * 128:(c + 1) * 128], IDENT[:, :])
                    last.then_inc(infini_turned_by_pe, 1)
                    pe.wait_ge(infini_turned_by_act, n * 4 + 4)
                    for c in range(2):
                        last = nc.tensor.matmul(PS[2][:, 0:256], cTa[:, c, :], WO[:, c, :], start=(c == 0), stop=(c == 1))
                    last.then_inc(infini_outproj_by_pe, 1)

            @block.vector
            def _(dve):
                dve.wait_ge(infini_setup_by_act, 1)
                nc.vector.tensor_scalar(GL[:, :], GS[:, :], 1.0, None, ALU.add).then_inc(infini_setup_by_dve, 1)
                dve.wait_ge(infini_setup_by_dve, 1)
                nc.vector.reciprocal(GS[:, :], GL[:, :]).then_inc(infini_setup_by_dve, 1)
                dve.wait_ge(infini_setup_by_dve, 2)
                nc.vector.tensor_scalar(GL[:, :], GS[:, :], -1.0, 1.0, ALU.mult, ALU.add).then_inc(infini_setup_by_dve, 1)
                dve.sem_inc(infini_residual_by_dve, 2)
                dve.wait_ge(infini_setup_loads_sp, 160)
                dve.wait_ge(infini_setup_by_pool, 1)
                dve.wait_ge(infini_setup_by_act, 1)
                dve.wait_ge(infini_setup_by_dve, 3)
                with dve.Fori(0, 16) as i:
                    n = i
                    dve.wait_ge(infini_residual_by_dve, n * 2 + 1)
                    dve.sem_inc(infini_dve_passed, 1)
                    nc.vector.bn_stats(statsb[:, :], X[:, bass.ds((n * 2 + 1) * 256, 256)]).then_inc(infini_norm_by_dve, 1)
                    dve.wait_ge(infini_residual_by_dve, n * 2 + 2)
                    dve.sem_inc(infini_dve_passed, 1)
                    nc.vector.bn_stats(statsa[:, :], X[:, bass.ds((n * 2 + 0) * 256, 256)]).then_inc(infini_norm_by_dve, 1)
                    dve.wait_ge(infini_norm_by_dve, n * 6 + 1)
                    dve.sem_inc(infini_dve_passed, 1)
                    nc.vector.bn_aggr(mvb[:, :], statsb[:, :]).then_inc(infini_norm_by_dve, 1)
                    dve.wait_ge(infini_norm_by_dve, n * 6 + 2)
                    dve.sem_inc(infini_dve_passed, 1)
                    nc.vector.bn_aggr(mva[:, :], statsa[:, :]).then_inc(infini_norm_by_dve, 1)
                    dve.wait_ge(infini_norm_by_dve, n * 6 + 3)
                    nc.vector.tensor_scalar(vareb[:, :], mvb[:, 1:2], 1e-5, None, ALU.add).then_inc(infini_norm_by_dve, 1)
                    dve.wait_ge(infini_norm_by_dve, n * 6 + 4)
                    nc.vector.tensor_scalar(varea[:, :], mva[:, 1:2], 1e-5, None, ALU.add).then_inc(infini_norm_by_dve, 1)
                    dve.wait_ge(infini_rstd_by_pool, n * 2 + 1)
                    nc.vector.tensor_scalar(xnb[:, :], X[:, bass.ds((n * 2 + 1) * 256, 256)], mvb[:, 0:1], rstdb[:, 0:1], ALU.subtract, ALU.mult).then_inc(infini_normed_by_dve, 1)
                    dve.wait_ge(infini_rstd_by_pool, n * 2 + 2)
                    nc.vector.tensor_scalar(xna[:, :], X[:, bass.ds((n * 2 + 0) * 256, 256)], mva[:, 0:1], rstda[:, 0:1], ALU.subtract, ALU.mult).then_inc(infini_normed_by_dve, 1)
                    dve.wait_ge(infini_keys_by_act, n * 2 + 1)
                    nc.vector.tensor_tensor(HXb[:, 0:8, :], kTb[:, 0, :].unsqueeze(1).to_broadcast([128, 8, 128]),
                                           HM[:, :].unsqueeze(2).to_broadcast([128, 8, 128]), ALU.mult)
                    dve.wait_ge(infini_queries_by_act, n * 2 + 1)
                    nc.vector.tensor_scalar(enb[:, :], PS[4][:, 0:256], 0.0, None, ALU.min).then_inc(infini_sigma_by_dve, 1)
                    dve.wait_ge(infini_keys_by_act, n * 2 + 2)
                    nc.vector.tensor_tensor(HXa[:, 0:8, :], kTa[:, 0, :].unsqueeze(1).to_broadcast([128, 8, 128]),
                                           HM[:, :].unsqueeze(2).to_broadcast([128, 8, 128]), ALU.mult)
                    dve.wait_ge(infini_queries_by_act, n * 2 + 2)
                    nc.vector.tensor_scalar(ena[:, :], PS[0][:, 0:256], 0.0, None, ALU.min).then_inc(infini_sigma_by_dve, 1)
                    dve.wait_ge(infini_sigma_by_act, n * 2 + 1)
                    nc.vector.scalar_tensor_tensor(sTb[:, :, :].rearrange("p c t -> p (c t)"), PS[4][:, 0:256], 0.0, enb[:, :], ALU.max, ALU.add).then_inc(infini_sigma_by_dve, 1)
                    dve.wait_ge(infini_sigma_by_act, n * 2 + 2)
                    nc.vector.scalar_tensor_tensor(sTa[:, :, :].rearrange("p c t -> p (c t)"), PS[0][:, 0:256], 0.0, ena[:, :], ALU.max, ALU.add).then_inc(infini_sigma_by_dve, 1)
                    dve.wait_ge(infini_memory_by_pe, n * 2 + 1)
                    nc.vector.tensor_copy(rawb[:, :], PS[5][:, 256:260]).then_inc(infini_memnorm_by_dve, 1)
                    dve.wait_ge(infini_memnorm_by_dve, n * 2 + 1)
                    nc.vector.tensor_scalar(rcb[:, :], rawb[:, :], 1e-6, None, ALU.max).then_inc(infini_memsoft_by_dve, 1)
                    dve.wait_ge(infini_memsoft_by_dve, n * 12 + 1)
                    nc.vector.reciprocal(cfb[:, :], rcb[:, :])
                    dve.wait_ge(infini_memory_by_pe, n * 2 + 2)
                    nc.vector.tensor_copy(rawa[:, :], PS[1][:, 256:260]).then_inc(infini_memnorm_by_dve, 1)
                    dve.wait_ge(infini_memnorm_by_dve, n * 2 + 2)
                    nc.vector.tensor_scalar(rca[:, :], rawa[:, :], 1e-6, None, ALU.max).then_inc(infini_memsoft_by_dve, 1)
                    dve.wait_ge(infini_relevance_by_pe, n * 2 + 1)
                    nc.vector.reduce_max(m1b[:, :], PS[5][:, 264:268], AX.X).then_inc(infini_memsoft_by_dve, 1)
                    dve.wait_ge(infini_memsoft_by_dve, n * 12 + 2)
                    nc.vector.reciprocal(cfa[:, :], rca[:, :])
                    dve.wait_ge(infini_memsoft_by_dve, n * 12 + 3)
                    nc.vector.tensor_scalar(n1b[:, :], m1b[:, :], -1.0, None, ALU.mult).then_inc(infini_memsoft_by_dve, 1)
                    dve.wait_ge(infini_memsoft_by_act, n * 2 + 1)
                    nc.vector.reciprocal(r1b[:, :], s1b[:, :]).then_inc(infini_memsoft_by_dve, 1)
                    dve.wait_ge(infini_memsoft_by_dve, n * 12 + 5)
                    nc.vector.tensor_scalar(emb[:, :], emb[:, :], r1b[:, 0:1], GS[:, 0:1], ALU.mult, ALU.mult).then_inc(infini_memsoft_by_dve, 1)
                    dve.wait_ge(infini_memsoft_by_dve, n * 12 + 6)
                    nc.vector.tensor_tensor(cfb[:, :], cfb[:, :], emb[:, :], ALU.mult).then_inc(infini_memsoft_by_dve, 1)
                    dve.wait_ge(infini_memsoft_by_dve, n * 12 + 7)
                    nc.vector.tensor_scalar(mob[:, :], PS[6][:, 0:256], cfb[:, 0:1], None, ALU.mult).then_inc(infini_mixmem_by_dve, 1)
                    dve.wait_ge(infini_mixmem_by_dve, n * 8 + 1)
                    nc.vector.scalar_tensor_tensor(mob[:, :], PS[6][:, 256:512], cfb[:, 1:2], mob[:, :], ALU.mult, ALU.add).then_inc(infini_mixmem_by_dve, 1)
                    dve.wait_ge(infini_mixmem_by_dve, n * 8 + 2)
                    nc.vector.scalar_tensor_tensor(mob[:, :], PS[7][:, 0:256], cfb[:, 2:3], mob[:, :], ALU.mult, ALU.add).then_inc(infini_mixmem_by_dve, 1)
                    dve.wait_ge(infini_mixmem_by_dve, n * 8 + 3)
                    nc.vector.scalar_tensor_tensor(mob[:, :], PS[7][:, 256:512], cfb[:, 3:4], mob[:, :], ALU.mult, ALU.add).then_inc(infini_mixmem_by_dve, 1)
                    dve.wait_ge(infini_relevance_by_pe, n * 2 + 2)
                    nc.vector.reduce_max(m1a[:, :], PS[1][:, 264:268], AX.X).then_inc(infini_memsoft_by_dve, 1)
                    dve.wait_ge(infini_memsoft_by_dve, n * 12 + 8)
                    nc.vector.tensor_scalar(n1a[:, :], m1a[:, :], -1.0, None, ALU.mult).then_inc(infini_memsoft_by_dve, 1)
                    dve.wait_ge(infini_memsoft_by_act, n * 2 + 2)
                    nc.vector.reciprocal(r1a[:, :], s1a[:, :]).then_inc(infini_memsoft_by_dve, 1)
                    dve.wait_ge(infini_memsoft_by_dve, n * 12 + 10)
                    nc.vector.tensor_scalar(ema[:, :], ema[:, :], r1a[:, 0:1], GS[:, 0:1], ALU.mult, ALU.mult).then_inc(infini_memsoft_by_dve, 1)
                    dve.wait_ge(infini_memsoft_by_dve, n * 12 + 11)
                    nc.vector.tensor_tensor(cfa[:, :], cfa[:, :], ema[:, :], ALU.mult).then_inc(infini_memsoft_by_dve, 1)
                    dve.wait_ge(infini_memsoft_by_dve, n * 12 + 12)
                    nc.vector.tensor_scalar(moa[:, :], PS[2][:, 0:256], cfa[:, 0:1], None, ALU.mult).then_inc(infini_mixmem_by_dve, 1)
                    dve.wait_ge(infini_mixmem_by_dve, n * 8 + 5)
                    nc.vector.scalar_tensor_tensor(moa[:, :], PS[2][:, 256:512], cfa[:, 1:2], moa[:, :], ALU.mult, ALU.add).then_inc(infini_mixmem_by_dve, 1)
                    dve.wait_ge(infini_scores_by_pe, n * 4 + 1)
                    nc.vector.tensor_tensor(SCb[:, 12:16, :].rearrange("p k s -> p (k s)"), PS[7][:, :], NMASK[:, :], ALU.add)
                    dve.wait_ge(infini_mixmem_by_dve, n * 8 + 6)
                    nc.vector.scalar_tensor_tensor(moa[:, :], PS[3][:, 0:256], cfa[:, 2:3], moa[:, :], ALU.mult, ALU.add).then_inc(infini_mixmem_by_dve, 1)
                    dve.wait_ge(infini_mixmem_by_dve, n * 8 + 7)
                    nc.vector.scalar_tensor_tensor(moa[:, :], PS[3][:, 256:512], cfa[:, 3:4], moa[:, :], ALU.mult, ALU.add).then_inc(infini_mixmem_by_dve, 1)
                    nc.vector.tensor_tensor(SCb[:, 8:12, :].rearrange("p k s -> p (k s)"), PS[6][:, :], NMASK[:, :], ALU.add).then_inc(infini_masked_by_dve, 1)
                    nc.vector.reduce_max(mxb[:, 12:16], SCb[:, 12:16, :], AX.X)
                    dve.wait_ge(infini_masked_by_dve, n * 7 + 1)
                    nc.vector.reduce_max(mxb[:, 8:12], SCb[:, 8:12, :], AX.X)
                    dve.wait_ge(infini_scores_by_pe, n * 4 + 2)
                    nc.vector.tensor_tensor(SCb[:, 4:8, :].rearrange("p k s -> p (k s)"), PS[5][:, :], NMASK[:, :], ALU.add).then_inc(infini_masked_by_dve, 1)
                    nc.vector.tensor_tensor(SCb[:, 0:4, :].rearrange("p k s -> p (k s)"), PS[4][:, :], NMASK[:, :], ALU.add).then_inc(infini_masked_by_dve, 1)
                    dve.wait_ge(infini_masked_by_dve, n * 7 + 2)
                    nc.vector.reduce_max(mxb[:, 4:8], SCb[:, 4:8, :], AX.X).then_inc(infini_max_by_dve, 1)
                    dve.wait_ge(infini_masked_by_dve, n * 7 + 3)
                    nc.vector.reduce_max(mxb[:, 0:4], SCb[:, 0:4, :], AX.X)
                    nc.vector.tensor_scalar(nmxb[:, 12:16], mxb[:, 12:16], -1.0, None, ALU.mult).then_inc(infini_max_by_dve, 1)
                    nc.vector.tensor_scalar(nmxb[:, 8:12], mxb[:, 8:12], -1.0, None, ALU.mult).then_inc(infini_max_by_dve, 1)
                    dve.wait_ge(infini_max_by_dve, n * 13 + 1)
                    nc.vector.tensor_scalar(nmxb[:, 4:8], mxb[:, 4:8], -1.0, None, ALU.mult).then_inc(infini_max_by_dve, 1)
                    dve.wait_ge(infini_scores_by_pe, n * 4 + 3)
                    nc.vector.tensor_tensor(SCa[:, 12:16, :].rearrange("p k s -> p (k s)"), PS[3][:, :], NMASK[:, :], ALU.add).then_inc(infini_masked_by_dve, 1)
                    nc.vector.tensor_tensor(SCa[:, 8:12, :].rearrange("p k s -> p (k s)"), PS[2][:, :], NMASK[:, :], ALU.add).then_inc(infini_masked_by_dve, 1)
                    dve.wait_ge(infini_masked_by_dve, n * 7 + 4)
                    nc.vector.reduce_max(mxa[:, 12:16], SCa[:, 12:16, :], AX.X).then_inc(infini_max_by_dve, 1)
                    nc.vector.tensor_scalar(nmxb[:, 0:4], mxb[:, 0:4], -1.0, None, ALU.mult).then_inc(infini_max_by_dve, 1)
                    dve.wait_ge(infini_masked_by_dve, n * 7 + 5)
                    nc.vector.reduce_max(mxa[:, 8:12], SCa[:, 8:12, :], AX.X).then_inc(infini_max_by_dve, 1)
                    dve.wait_ge(infini_max_by_dve, n * 13 + 5)
                    nc.vector.tensor_scalar(nmxa[:, 12:16], mxa[:, 12:16], -1.0, None, ALU.mult).then_inc(infini_max_by_dve, 1)
                    dve.wait_ge(infini_max_by_dve, n * 13 + 7)
                    nc.vector.tensor_scalar(nmxa[:, 8:12], mxa[:, 8:12], -1.0, None, ALU.mult).then_inc(infini_max_by_dve, 1)
                    dve.wait_ge(infini_scores_by_pe, n * 4 + 4)
                    nc.vector.tensor_tensor(SCa[:, 4:8, :].rearrange("p k s -> p (k s)"), PS[1][:, :], NMASK[:, :], ALU.add).then_inc(infini_masked_by_dve, 1)
                    nc.vector.tensor_tensor(SCa[:, 0:4, :].rearrange("p k s -> p (k s)"), PS[0][:, :], NMASK[:, :], ALU.add).then_inc(infini_masked_by_dve, 1)
                    dve.wait_ge(infini_masked_by_dve, n * 7 + 6)
                    nc.vector.reduce_max(mxa[:, 4:8], SCa[:, 4:8, :], AX.X).then_inc(infini_max_by_dve, 1)
                    dve.wait_ge(infini_masked_by_dve, n * 7 + 7)
                    nc.vector.reduce_max(mxa[:, 0:4], SCa[:, 0:4, :], AX.X).then_inc(infini_max_by_dve, 1)
                    dve.wait_ge(infini_max_by_dve, n * 13 + 10)
                    nc.vector.tensor_scalar(nmxa[:, 4:8], mxa[:, 4:8], -1.0, None, ALU.mult).then_inc(infini_max_by_dve, 1)
                    dve.wait_ge(infini_max_by_dve, n * 13 + 11)
                    nc.vector.tensor_scalar(nmxa[:, 0:4], mxa[:, 0:4], -1.0, None, ALU.mult).then_inc(infini_max_by_dve, 1)
                    dve.wait_ge(infini_pturn_by_pe, n * 8 + 1)
                    nc.vector.tensor_copy(PWb[:, 12:16, :].rearrange("p k s -> p (k s)"), PS[7][:, :])
                    dve.wait_ge(infini_pturn_by_pe, n * 8 + 4)
                    nc.vector.tensor_copy(PWb[:, 4:8, :].rearrange("p k s -> p (k s)"), PS[5][:, :]).then_inc(infini_pturn_by_dve, 1)
                    dve.wait_ge(infini_pturn_by_pe, n * 8 + 5)
                    nc.vector.tensor_copy(PWa[:, 12:16, :].rearrange("p k s -> p (k s)"), PS[3][:, :])
                    dve.wait_ge(infini_pturn_by_pe, n * 8 + 6)
                    nc.vector.tensor_copy(PWa[:, 4:8, :].rearrange("p k s -> p (k s)"), PS[1][:, :]).then_inc(infini_pturn_by_dve, 1)
                    dve.wait_ge(infini_attended_by_pe, n * 2 + 1)
                    nc.vector.reciprocal(rdb[:, :], PS[4][:, 0:272].rearrange("p (h d) -> p h d", d=17)[:, :, 16]).then_inc(infini_normalize_by_dve, 1)
                    dve.wait_ge(infini_normalize_by_dve, n * 6 + 1)
                    nc.vector.tensor_scalar(rdb[:, :], rdb[:, :], GL[:, 0:1], None, ALU.mult).then_inc(infini_normalize_by_dve, 1)
                    dve.wait_ge(infini_normalize_by_dve, n * 6 + 2)
                    nc.vector.tensor_tensor(by_head(ctx_b[:, :]), PS[4][:, 0:272].rearrange("p (h d) -> p h d", d=17)[:, :, 0:16], rdb[:, :].unsqueeze(2).to_broadcast([128, 16, 16]), ALU.mult).then_inc(infini_normalize_by_dve, 1)
                    dve.wait_ge(infini_attended_by_pe, n * 2 + 2)
                    nc.vector.reciprocal(rda[:, :], PS[0][:, 0:272].rearrange("p (h d) -> p h d", d=17)[:, :, 16]).then_inc(infini_normalize_by_dve, 1)
                    dve.wait_ge(infini_normalize_by_dve, n * 6 + 4)
                    nc.vector.tensor_scalar(rda[:, :], rda[:, :], GL[:, 0:1], None, ALU.mult).then_inc(infini_normalize_by_dve, 1)
                    dve.wait_ge(infini_normalize_by_dve, n * 6 + 5)
                    nc.vector.tensor_tensor(by_head(ctx_a[:, :]), PS[0][:, 0:272].rearrange("p (h d) -> p h d", d=17)[:, :, 0:16], rda[:, :].unsqueeze(2).to_broadcast([128, 16, 16]), ALU.mult).then_inc(infini_normalize_by_dve, 1)
                    dve.wait_ge(infini_outproj_by_pe, n * 2 + 1)
                    nc.vector.tensor_tensor(X[:, bass.ds((n * 2 + 1) * 256, 256)], PS[6][:, 0:256], X[:, bass.ds((n * 2 + 1) * 256, 256)], ALU.add).then_inc(infini_residual_by_dve, 1)
                    dve.wait_ge(infini_outproj_by_pe, n * 2 + 2)
                    nc.vector.tensor_tensor(X[:, bass.ds((n * 2 + 0) * 256, 256)], PS[2][:, 0:256], X[:, bass.ds((n * 2 + 0) * 256, 256)], ALU.add).then_inc(infini_residual_by_dve, 1)

            @block.scalar
            def _(act):
                act.wait_ge(infini_setup_loads_sp, 160)
                nc.scalar.activation(GS[:, :], GT[:, :], ACT.Exp, scale=-1.0).then_inc(infini_setup_by_act, 1)
                act.wait_ge(infini_setup_loads_sp, 160)
                act.wait_ge(infini_setup_by_pool, 1)
                act.wait_ge(infini_setup_by_act, 1)
                act.wait_ge(infini_setup_by_dve, 3)
                with act.Fori(0, 16) as i:
                    n = i
                    act.wait_ge(infini_turned_by_pe, n * 4 + 1)
                    nc.scalar.activation(xTb[:, :, :].rearrange("p c t -> p (c t)"), PS[4][:, 0:256], ACT.Copy).then_inc(infini_turned_by_act, 1)
                    act.wait_ge(infini_turned_by_pe, n * 4 + 2)
                    nc.scalar.activation(xTa[:, :, :].rearrange("p c t -> p (c t)"), PS[0][:, 0:256], ACT.Copy).then_inc(infini_turned_by_act, 1)
                    act.wait_ge(infini_projected_by_pe, n * 4 + 1)
                    nc.scalar.activation(kTb[:, :, :].rearrange("p c t -> p (c t)"), PS[4][:, 256:512], ACT.Copy).then_inc(infini_keys_by_act, 1)
                    nc.scalar.activation(qTb[:, :, :].rearrange("p c t -> p (c t)"), PS[4][:, 0:256], ACT.Copy).then_inc(infini_queries_by_act, 1)
                    act.wait_ge(infini_projected_by_pe, n * 4 + 2)
                    nc.scalar.activation(kTa[:, :, :].rearrange("p c t -> p (c t)"), PS[0][:, 256:512], ACT.Copy).then_inc(infini_keys_by_act, 1)
                    nc.scalar.activation(qTa[:, :, :].rearrange("p c t -> p (c t)"), PS[0][:, 0:256], ACT.Copy).then_inc(infini_queries_by_act, 1)
                    act.wait_ge(infini_projected_by_pe, n * 4 + 3)
                    nc.scalar.activation(VXb[:, :, 0:16], by_head(PS[5][:, 0:256]), ACT.Copy)
                    act.wait_ge(infini_projected_by_pe, n * 4 + 4)
                    nc.scalar.activation(VXa[:, :, 0:16], by_head(PS[1][:, 0:256]), ACT.Copy)
                    act.wait_ge(infini_sigma_by_dve, n * 4 + 1)
                    nc.scalar.activation(enb[:, :], enb[:, :], ACT.Exp).then_inc(infini_sigma_by_act, 1)
                    act.wait_ge(infini_sigma_by_dve, n * 4 + 2)
                    nc.scalar.activation(ena[:, :], ena[:, :], ACT.Exp).then_inc(infini_sigma_by_act, 1)
                    act.wait_ge(infini_memsoft_by_dve, n * 12 + 4)
                    nc.scalar.activation(emb[:, :], PS[5][:, 264:268], ACT.Exp, bias=n1b[:, 0:1], accum_out=s1b[:, 0:1]).then_inc(infini_memsoft_by_act, 1)
                    act.wait_ge(infini_memsoft_by_dve, n * 12 + 9)
                    nc.scalar.activation(ema[:, :], PS[1][:, 264:268], ACT.Exp, bias=n1a[:, 0:1], accum_out=s1a[:, 0:1]).then_inc(infini_memsoft_by_act, 1)
                    act.wait_ge(infini_max_by_dve, n * 13 + 2)
                    for k in range(12, 16):
                        last = nc.scalar.activation(SCb[:, k, :], SCb[:, k, :], ACT.Exp, bias=nmxb[:, k:k + 1])
                    last.then_inc(infini_exp_by_act, 1)
                    act.wait_ge(infini_max_by_dve, n * 13 + 3)
                    for k in range(8, 12):
                        last = nc.scalar.activation(SCb[:, k, :], SCb[:, k, :], ACT.Exp, bias=nmxb[:, k:k + 1])
                    last.then_inc(infini_exp_by_act, 1)
                    act.wait_ge(infini_max_by_dve, n * 13 + 4)
                    for k in range(4, 8):
                        last = nc.scalar.activation(SCb[:, k, :], SCb[:, k, :], ACT.Exp, bias=nmxb[:, k:k + 1])
                    act.wait_ge(infini_max_by_dve, n * 13 + 6)
                    for k in range(0, 4):
                        last = nc.scalar.activation(SCb[:, k, :], SCb[:, k, :], ACT.Exp, bias=nmxb[:, k:k + 1])
                    last.then_inc(infini_exp_by_act, 1)
                    act.wait_ge(infini_max_by_dve, n * 13 + 8)
                    for k in range(12, 16):
                        last = nc.scalar.activation(SCa[:, k, :], SCa[:, k, :], ACT.Exp, bias=nmxa[:, k:k + 1])
                    last.then_inc(infini_exp_by_act, 1)
                    act.wait_ge(infini_max_by_dve, n * 13 + 9)
                    for k in range(8, 12):
                        last = nc.scalar.activation(SCa[:, k, :], SCa[:, k, :], ACT.Exp, bias=nmxa[:, k:k + 1])
                    act.wait_ge(infini_max_by_dve, n * 13 + 12)
                    for k in range(4, 8):
                        last = nc.scalar.activation(SCa[:, k, :], SCa[:, k, :], ACT.Exp, bias=nmxa[:, k:k + 1])
                    last.then_inc(infini_exp_by_act, 1)
                    act.wait_ge(infini_max_by_dve, n * 13 + 13)
                    for k in range(0, 4):
                        last = nc.scalar.activation(SCa[:, k, :], SCa[:, k, :], ACT.Exp, bias=nmxa[:, k:k + 1])
                    last.then_inc(infini_exp_by_act, 1)
                    act.wait_ge(infini_pturn_by_pe, n * 8 + 2)
                    nc.scalar.activation(PWb[:, 8:12, :].rearrange("p k s -> p (k s)"), PS[6][:, :], ACT.Copy)
                    act.wait_ge(infini_pturn_by_pe, n * 8 + 3)
                    nc.scalar.activation(PWb[:, 0:4, :].rearrange("p k s -> p (k s)"), PS[4][:, :], ACT.Copy).then_inc(infini_pturn_by_act, 1)
                    act.wait_ge(infini_pturn_by_pe, n * 8 + 7)
                    nc.scalar.activation(PWa[:, 8:12, :].rearrange("p k s -> p (k s)"), PS[2][:, :], ACT.Copy)
                    act.wait_ge(infini_pturn_by_pe, n * 8 + 8)
                    nc.scalar.activation(PWa[:, 0:4, :].rearrange("p k s -> p (k s)"), PS[0][:, :], ACT.Copy).then_inc(infini_pturn_by_act, 1)
                    act.wait_ge(infini_turned_by_pe, n * 4 + 3)
                    nc.scalar.activation(cTb[:, :, :].rearrange("p c t -> p (c t)"), PS[5][:, 0:256], ACT.Copy).then_inc(infini_turned_by_act, 1)
                    act.wait_ge(infini_turned_by_pe, n * 4 + 4)
                    nc.scalar.activation(cTa[:, :, :].rearrange("p c t -> p (c t)"), PS[1][:, 0:256], ACT.Copy).then_inc(infini_turned_by_act, 1)

            @block.gpsimd
            def _(pool):
                nc.gpsimd.memset(NEGHALF[:, :], -0.5)
                nc.gpsimd.memset(onerow[:, :], 1.0)
                nc.gpsimd.memset(VXa[:, :, :], 1.0)
                nc.gpsimd.memset(VXb[:, :, :], 1.0).then_inc(infini_setup_by_pool, 1)
                pool.wait_ge(infini_setup_loads_sp, 160)
                pool.wait_ge(infini_setup_by_pool, 1)
                pool.wait_ge(infini_setup_by_act, 1)
                pool.wait_ge(infini_setup_by_dve, 3)
                with pool.Fori(0, 16) as i:
                    n = i
                    pool.wait_ge(infini_norm_by_dve, n * 6 + 5)
                    nc.gpsimd.tensor_tensor(rstdb[:, :], vareb[:, :], NEGHALF[:, 0:1], ALU.pow).then_inc(infini_rstd_by_pool, 1)
                    pool.wait_ge(infini_norm_by_dve, n * 6 + 6)
                    nc.gpsimd.tensor_tensor(rstda[:, :], varea[:, :], NEGHALF[:, 0:1], ALU.pow).then_inc(infini_rstd_by_pool, 1)
                    pool.wait_ge(infini_keys_by_act, n * 2 + 1)
                    nc.gpsimd.tensor_tensor(HXb[:, 8:16, :], kTb[:, 1, :].unsqueeze(1).to_broadcast([128, 8, 128]),
                                           HM[:, :].unsqueeze(2).to_broadcast([128, 8, 128]), ALU.mult).then_inc(infini_expand_by_pool, 1)
                    pool.wait_ge(infini_keys_by_act, n * 2 + 2)
                    nc.gpsimd.tensor_tensor(HXa[:, 8:16, :], kTa[:, 1, :].unsqueeze(1).to_broadcast([128, 8, 128]),
                                           HM[:, :].unsqueeze(2).to_broadcast([128, 8, 128]), ALU.mult).then_inc(infini_expand_by_pool, 1)
                    pool.wait_ge(infini_normalize_by_dve, n * 6 + 3)
                    nc.gpsimd.tensor_tensor(ctx_b[:, :], ctx_b[:, :], mob[:, :], ALU.add).then_inc(infini_mixed_by_pool, 1)
                    pool.wait_ge(infini_normalize_by_dve, n * 6 + 6)
                    nc.gpsimd.tensor_tensor(ctx_a[:, :], ctx_a[:, :], moa[:, :], ALU.add).then_inc(infini_mixed_by_pool, 1)

            @block.sync
            def _(sp):
                nc.sync.dma_start(HM[:, :], io["head_mask"]).then_inc(infini_setup_loads_sp, 16)
                nc.sync.dma_start(WQ[:, :, :], io["l1_wq"]).then_inc(infini_setup_loads_sp, 16)
                nc.sync.dma_start(WK[:, :, :], io["l1_wk"]).then_inc(infini_setup_loads_sp, 16)
                nc.sync.dma_start(WV[:, :, :], io["l1_wv"]).then_inc(infini_setup_loads_sp, 16)
                nc.sync.dma_start(WO[:, :, :], io["l1_wo"]).then_inc(infini_setup_loads_sp, 16)
                nc.sync.dma_start(MEM[:, :, :], io["memories"]).then_inc(infini_setup_loads_sp, 16)
                nc.sync.dma_start(MN[:, :, :], io["memory_norms"]).then_inc(infini_setup_loads_sp, 16)
                nc.sync.dma_start(GT[:, :], io["gate"]).then_inc(infini_setup_loads_sp, 16)
                nc.sync.dma_start(BM[:, :], io["block_mean"]).then_inc(infini_setup_loads_sp, 16)
                nc.sync.dma_start(NMASK[:, :], io["neg_causal"]).then_inc(infini_setup_loads_sp, 16)

        nc.clear_and_free_semaphores(signals)
        nc.all_engine_barrier()

def cross(nc, io, X, PS, IDENT, shared):
    ctx = ExitStack()
    with ctx:
        def sb(name, shape, dt=F32):
            return ctx.enter_context(nc.sbuf_tensor("cross_" + name, shape, dt))

        signals = []

        def signal(name):
            signals.append(nc.alloc_semaphore(name))
            return signals[-1]

        H1T, CW1 = shared
        statsa = sb("statsa", [128, 6])
        mva = sb("mva", [128, 2])
        varea = sb("varea", [128, 1])
        rstda = sb("rstda", [128, 1])
        xna = sb("xna", [128, 256])
        qTa = sb("qTa", [128, 2, 128])
        HXa = sb("HXa", [128, 16, 128])
        kTa = sb("kTa", [128, 2, 128])
        VXa = sb("VXa", [128, 16, 17])
        SCa = sb("SCa", [128, 16, 128])
        PWa = sb("PWa", [128, 16, 128])
        ctx_a = sb("ctx_a", [128, 256])
        cTa = sb("cTa", [128, 2, 128])
        xTa = sb("xTa", [128, 2, 128])
        rda = sb("rda", [128, 16])
        mxa = sb("mxa", [128, 16])
        nmxa = sb("nmxa", [128, 16])
        tma = sb("tma", [128, 1])
        tna = sb("tna", [128, 1])
        psa = sb("psa", [128, 1])
        pra = sb("pra", [128, 1])
        sha = sb("sha", [128, 1])
        csa = sb("csa", [128, 1])
        cra = sb("cra", [128, 1])
        pea = sb("pea", [128, 8])
        m8a = sb("m8a", [128, 8])
        topa = sb("topa", [128, 8])
        c8a = sb("c8a", [128, 8])
        ppa = sb("ppa", [128, 14])
        pza = sb("pza", [128, 14])
        cxa = sb("cxa", [128, 256])
        mba = sb("mba", [128, 128])
        statsb = sb("statsb", [128, 6])
        mvb = sb("mvb", [128, 2])
        vareb = sb("vareb", [128, 1])
        rstdb = sb("rstdb", [128, 1])
        xnb = sb("xnb", [128, 256])
        qTb = sb("qTb", [128, 2, 128])
        HXb = sb("HXb", [128, 16, 128])
        kTb = sb("kTb", [128, 2, 128])
        VXb = sb("VXb", [128, 16, 17])
        SCb = sb("SCb", [128, 16, 128])
        PWb = sb("PWb", [128, 16, 128])
        ctx_b = sb("ctx_b", [128, 256])
        cTb = sb("cTb", [128, 2, 128])
        xTb = sb("xTb", [128, 2, 128])
        rdb = sb("rdb", [128, 16])
        mxb = sb("mxb", [128, 16])
        nmxb = sb("nmxb", [128, 16])
        tmb = sb("tmb", [128, 1])
        tnb = sb("tnb", [128, 1])
        psb = sb("psb", [128, 1])
        prb = sb("prb", [128, 1])
        shb = sb("shb", [128, 1])
        csb = sb("csb", [128, 1])
        crb = sb("crb", [128, 1])
        peb = sb("peb", [128, 8])
        m8b = sb("m8b", [128, 8])
        topb = sb("topb", [128, 8])
        c8b = sb("c8b", [128, 8])
        ppb = sb("ppb", [128, 14])
        pzb = sb("pzb", [128, 14])
        cxb = sb("cxb", [128, 256])
        mbb = sb("mbb", [128, 128])
        NEGHALF = sb("neghalf", [128, 16])
        HM = sb("hm", [128, 8])
        onerow = sb("onerow", [1, 128])
        WQ = sb("WQ", [128, 2, 256])
        WKV = sb("WKV", [128, 2, 128])
        WO = sb("WO", [128, 2, 256])
        WR = sb("WR", [128, 2, 8])
        ALI = sb("ALI", [128, 2048])
        WKR = sb("wkr", [128, 2, 256])
        MK8 = sb("mk8", [1, 4096], mybir.dt.uint8)
        MK = sb("mk", [1, 4096])
        def by_head(t):
            return t.rearrange("p (h d) -> p h d", d=16)

        cross_setup_loads_sp = signal("cross_setup_loads_sp")
        cross_setup_by_dve = signal("cross_setup_by_dve")
        cross_setup_by_pool = signal("cross_setup_by_pool")
        cross_norm_by_dve = signal("cross_norm_by_dve")
        cross_context_a_dma = signal("cross_context_a_dma")
        cross_turned_by_pe = signal("cross_turned_by_pe")
        cross_context_b_dma = signal("cross_context_b_dma")
        cross_turned_by_act = signal("cross_turned_by_act")
        cross_rstd_by_pool = signal("cross_rstd_by_pool")
        cross_normed_by_dve = signal("cross_normed_by_dve")
        cross_projected_by_pe = signal("cross_projected_by_pe")
        cross_keys_by_act = signal("cross_keys_by_act")
        cross_expand_by_pool = signal("cross_expand_by_pool")
        cross_expand_by_dve = signal("cross_expand_by_dve")
        cross_maskrow_by_pe = signal("cross_maskrow_by_pe")
        cross_values_by_dve = signal("cross_values_by_dve")
        cross_queries_by_act = signal("cross_queries_by_act")
        cross_scores_by_pe = signal("cross_scores_by_pe")
        cross_biased_by_dve = signal("cross_biased_by_dve")
        cross_masked_by_pool = signal("cross_masked_by_pool")
        cross_masked_by_dve = signal("cross_masked_by_dve")
        cross_max_by_dve = signal("cross_max_by_dve")
        cross_exp_by_act = signal("cross_exp_by_act")
        cross_pturn_by_pe = signal("cross_pturn_by_pe")
        cross_pturn_by_act = signal("cross_pturn_by_act")
        cross_pturn_by_dve = signal("cross_pturn_by_dve")
        cross_attended_by_pe = signal("cross_attended_by_pe")
        cross_normalize_by_dve = signal("cross_normalize_by_dve")
        cross_outproj_by_pe = signal("cross_outproj_by_pe")
        cross_residual_by_dve = signal("cross_residual_by_dve")
        cross_router_by_pe = signal("cross_router_by_pe")
        cross_kept_by_pool = signal("cross_kept_by_pool")
        cross_route_by_dve = signal("cross_route_by_dve")
        cross_route_by_act = signal("cross_route_by_act")
        cross_sp_passed = signal("cross_sp_passed")
        cross_pool_passed = signal("cross_pool_passed")
        cross_dve_passed = signal("cross_dve_passed")
        with nc.Block() as block:

            @block.tensor
            def _(pe):
                pe.sem_inc(cross_turned_by_pe, 8)
                pe.wait_ge(cross_setup_loads_sp, 112)
                pe.wait_ge(cross_setup_by_dve, 1)
                pe.wait_ge(cross_setup_by_pool, 1)
                with pe.Fori(0, 16) as i:
                    n = i
                    pe.wait_ge(cross_context_a_dma, n * 16 + 16)
                    for c in range(2):
                        last = nc.tensor.transpose(PS[1][:, c * 128:(c + 1) * 128], cxa[:, c * 128:(c + 1) * 128], IDENT[:, :])
                    last.then_inc(cross_turned_by_pe, 1)
                    pe.wait_ge(cross_context_b_dma, n * 16 + 16)
                    for c in range(2):
                        last = nc.tensor.transpose(PS[5][:, c * 128:(c + 1) * 128], cxb[:, c * 128:(c + 1) * 128], IDENT[:, :])
                    last.then_inc(cross_turned_by_pe, 1)
                    pe.wait_ge(cross_turned_by_act, n * 8 + 1)
                    for e in range(2):
                        for c in range(2):
                            last = nc.tensor.matmul(PS[1][:, 0 + e * 128:0 + (e + 1) * 128], WKR[:, c, e * 128:(e + 1) * 128], cTa[:, c, :], start=(c == 0), stop=(c == 1))
                    last.then_inc(cross_projected_by_pe, 1)
                    pe.wait_ge(cross_turned_by_act, n * 8 + 2)
                    for e in range(2):
                        for c in range(2):
                            last = nc.tensor.matmul(PS[5][:, 0 + e * 128:0 + (e + 1) * 128], WKR[:, c, e * 128:(e + 1) * 128], cTb[:, c, :], start=(c == 0), stop=(c == 1))
                    last.then_inc(cross_projected_by_pe, 1)
                    pe.wait_ge(cross_normed_by_dve, n * 4 + 1)
                    for c in range(2):
                        last = nc.tensor.transpose(PS[0][:, c * 128:(c + 1) * 128], xna[:, c * 128:(c + 1) * 128], IDENT[:, :])
                    last.then_inc(cross_turned_by_pe, 1)
                    for c in range(2):
                        last = nc.tensor.matmul(PS[2][:, 0:64], cTa[:, c, :], WKV[:, c, 64:128], start=(c == 0), stop=(c == 1))
                    pe.wait_ge(cross_normed_by_dve, n * 4 + 2)
                    for c in range(2):
                        last = nc.tensor.transpose(PS[4][:, c * 128:(c + 1) * 128], xnb[:, c * 128:(c + 1) * 128], IDENT[:, :])
                    last.then_inc(cross_turned_by_pe, 1)
                    for c in range(2):
                        last = nc.tensor.matmul(PS[6][:, 0:64], cTb[:, c, :], WKV[:, c, 64:128], start=(c == 0), stop=(c == 1))
                    last = nc.tensor.matmul(PS[2][:, 128:256], onerow[0:1, :], MK[0:1, bass.ds((n * 2 + 0) * 128, 128)], start=True, stop=True)
                    last.then_inc(cross_maskrow_by_pe, 1)
                    pe.wait_ge(cross_turned_by_act, n * 8 + 3)
                    for e in range(2):
                        for c in range(2):
                            last = nc.tensor.matmul(PS[0][:, 0 + e * 128:0 + (e + 1) * 128], WQ[:, c, e * 128:(e + 1) * 128], xTa[:, c, :], start=(c == 0), stop=(c == 1))
                    last.then_inc(cross_projected_by_pe, 1)
                    last = nc.tensor.matmul(PS[6][:, 128:256], onerow[0:1, :], MK[0:1, bass.ds((n * 2 + 1) * 128, 128)], start=True, stop=True)
                    last.then_inc(cross_maskrow_by_pe, 1)
                    pe.wait_ge(cross_turned_by_act, n * 8 + 4)
                    for e in range(2):
                        for c in range(2):
                            last = nc.tensor.matmul(PS[4][:, 0 + e * 128:0 + (e + 1) * 128], WQ[:, c, e * 128:(e + 1) * 128], xTb[:, c, :], start=(c == 0), stop=(c == 1))
                    last.then_inc(cross_projected_by_pe, 1)
                    pe.wait_ge(cross_expand_by_dve, n * 1 + 1)
                    pe.wait_ge(cross_queries_by_act, n * 2 + 1)
                    for k in range(2):
                        last = nc.tensor.matmul(PS[0 + k][:, :], qTa[:, 0, :], HXa[:, 0 + 4 * k:0 + 4 * k + 4, :], start=True, stop=True)
                    last.then_inc(cross_scores_by_pe, 1)
                    pe.wait_ge(cross_expand_by_pool, n * 2 + 1)
                    pe.wait_ge(cross_values_by_dve, n * 2 + 1)
                    for k in range(2):
                        last = nc.tensor.matmul(PS[2 + k][:, :], qTa[:, 1, :], HXa[:, 8 + 4 * k:8 + 4 * k + 4, :], start=True, stop=True)
                    last.then_inc(cross_scores_by_pe, 1)
                    pe.wait_ge(cross_queries_by_act, n * 2 + 2)
                    for k in range(2):
                        last = nc.tensor.matmul(PS[4 + k][:, :], qTb[:, 0, :], HXb[:, 0 + 4 * k:0 + 4 * k + 4, :], start=True, stop=True)
                    last.then_inc(cross_scores_by_pe, 1)
                    pe.wait_ge(cross_expand_by_pool, n * 2 + 2)
                    pe.wait_ge(cross_values_by_dve, n * 2 + 2)
                    for k in range(2):
                        last = nc.tensor.matmul(PS[6 + k][:, :], qTb[:, 1, :], HXb[:, 8 + 4 * k:8 + 4 * k + 4, :], start=True, stop=True)
                    last.then_inc(cross_scores_by_pe, 1)
                    pe.wait_ge(cross_exp_by_act, n * 2 + 1)
                    for k in range(4):
                        last = nc.tensor.transpose(PS[0][:, k * 128:(k + 1) * 128], SCa[:, 0 + k, :], IDENT[:, :])
                    last.then_inc(cross_pturn_by_pe, 1)
                    for k in range(4):
                        last = nc.tensor.transpose(PS[1][:, k * 128:(k + 1) * 128], SCa[:, 4 + k, :], IDENT[:, :])
                    last.then_inc(cross_pturn_by_pe, 1)
                    for k in range(4):
                        last = nc.tensor.transpose(PS[2][:, k * 128:(k + 1) * 128], SCa[:, 8 + k, :], IDENT[:, :])
                    last.then_inc(cross_pturn_by_pe, 1)
                    for k in range(4):
                        last = nc.tensor.transpose(PS[3][:, k * 128:(k + 1) * 128], SCa[:, 12 + k, :], IDENT[:, :])
                    last.then_inc(cross_pturn_by_pe, 1)
                    pe.wait_ge(cross_exp_by_act, n * 2 + 2)
                    for k in range(4):
                        last = nc.tensor.transpose(PS[4][:, k * 128:(k + 1) * 128], SCb[:, 0 + k, :], IDENT[:, :])
                    last.then_inc(cross_pturn_by_pe, 1)
                    for k in range(4):
                        last = nc.tensor.transpose(PS[5][:, k * 128:(k + 1) * 128], SCb[:, 4 + k, :], IDENT[:, :])
                    last.then_inc(cross_pturn_by_pe, 1)
                    for k in range(4):
                        last = nc.tensor.transpose(PS[6][:, k * 128:(k + 1) * 128], SCb[:, 8 + k, :], IDENT[:, :])
                    last.then_inc(cross_pturn_by_pe, 1)
                    for k in range(4):
                        last = nc.tensor.transpose(PS[7][:, k * 128:(k + 1) * 128], SCb[:, 12 + k, :], IDENT[:, :])
                    last.then_inc(cross_pturn_by_pe, 1)
                    pe.wait_ge(cross_pturn_by_act, n * 2 + 1)
                    pe.wait_ge(cross_pturn_by_dve, n * 2 + 1)
                    for head in range(16):
                        last = nc.tensor.matmul(PS[0][:, head * 17:head * 17 + 17], PWa[:, head, :], VXa[:, head, :], start=True, stop=True)
                    last.then_inc(cross_attended_by_pe, 1)
                    pe.wait_ge(cross_pturn_by_act, n * 2 + 2)
                    pe.wait_ge(cross_pturn_by_dve, n * 2 + 2)
                    for head in range(16):
                        last = nc.tensor.matmul(PS[4][:, head * 17:head * 17 + 17], PWb[:, head, :], VXb[:, head, :], start=True, stop=True)
                    last.then_inc(cross_attended_by_pe, 1)
                    pe.wait_ge(cross_normalize_by_dve, n * 4 + 2)
                    for c in range(2):
                        last = nc.tensor.transpose(PS[1][:, c * 128:(c + 1) * 128], ctx_a[:, c * 128:(c + 1) * 128], IDENT[:, :])
                    last.then_inc(cross_turned_by_pe, 1)
                    pe.wait_ge(cross_normalize_by_dve, n * 4 + 4)
                    for c in range(2):
                        last = nc.tensor.transpose(PS[5][:, c * 128:(c + 1) * 128], ctx_b[:, c * 128:(c + 1) * 128], IDENT[:, :])
                    last.then_inc(cross_turned_by_pe, 1)
                    pe.wait_ge(cross_turned_by_act, n * 8 + 5)
                    for c in range(2):
                        last = nc.tensor.matmul(PS[2][:, 0:256], cTa[:, c, :], WO[:, c, :], start=(c == 0), stop=(c == 1))
                    last.then_inc(cross_outproj_by_pe, 1)
                    pe.wait_ge(cross_turned_by_act, n * 8 + 6)
                    for c in range(2):
                        last = nc.tensor.matmul(PS[6][:, 0:256], cTb[:, c, :], WO[:, c, :], start=(c == 0), stop=(c == 1))
                    last.then_inc(cross_outproj_by_pe, 1)
                    pe.wait_ge(cross_normed_by_dve, n * 4 + 3)
                    for c in range(2):
                        last = nc.tensor.transpose(PS[0][:, c * 128:(c + 1) * 128], xna[:, c * 128:(c + 1) * 128], IDENT[:, :])
                    last.then_inc(cross_turned_by_pe, 1)
                    pe.wait_ge(cross_normed_by_dve, n * 4 + 4)
                    for c in range(2):
                        last = nc.tensor.transpose(PS[4][:, c * 128:(c + 1) * 128], xnb[:, c * 128:(c + 1) * 128], IDENT[:, :])
                    last.then_inc(cross_turned_by_pe, 1)
                    pe.wait_ge(cross_turned_by_act, n * 8 + 7)
                    for c in range(2):
                        last = nc.tensor.matmul(PS[3][:, 256:264], xTa[:, c, :], WR[:, c, :], start=(c == 0), stop=(c == 1))
                    last.then_inc(cross_router_by_pe, 1)
                    pe.wait_ge(cross_turned_by_act, n * 8 + 8)
                    for c in range(2):
                        last = nc.tensor.matmul(PS[7][:, 256:264], xTb[:, c, :], WR[:, c, :], start=(c == 0), stop=(c == 1))
                    last.then_inc(cross_router_by_pe, 1)

            @block.vector
            def _(dve):
                dve.wait_ge(cross_setup_loads_sp, 112)
                for c in range(2):
                    for k in range(4):
                        last = nc.vector.tensor_copy(WKR[:, c, :].rearrange("p (g k d) -> p g k d", g=4, k=4)[:, :, k, :], WKV[:, c, 0:64].rearrange("p (g d) -> p g d", g=4))
                dve.wait_ge(cross_setup_loads_sp, 112)
                nc.vector.tensor_scalar(MK[:, :], MK8[:, :], 1.0, 1e30, ALU.subtract, ALU.mult).then_inc(cross_setup_by_dve, 1)
                dve.wait_ge(cross_setup_loads_sp, 112)
                dve.wait_ge(cross_setup_by_dve, 1)
                dve.wait_ge(cross_setup_by_pool, 1)
                with dve.Fori(0, 16) as i:
                    n = i
                    nc.vector.bn_stats(statsa[:, :], X[:, bass.ds((n * 2 + 0) * 256, 256)]).then_inc(cross_norm_by_dve, 1)
                    nc.vector.bn_stats(statsb[:, :], X[:, bass.ds((n * 2 + 1) * 256, 256)]).then_inc(cross_norm_by_dve, 1)
                    dve.wait_ge(cross_norm_by_dve, n * 12 + 1)
                    dve.sem_inc(cross_dve_passed, 1)
                    nc.vector.bn_aggr(mva[:, :], statsa[:, :]).then_inc(cross_norm_by_dve, 1)
                    dve.wait_ge(cross_norm_by_dve, n * 12 + 2)
                    dve.sem_inc(cross_dve_passed, 1)
                    nc.vector.bn_aggr(mvb[:, :], statsb[:, :]).then_inc(cross_norm_by_dve, 1)
                    dve.wait_ge(cross_norm_by_dve, n * 12 + 3)
                    nc.vector.tensor_scalar(varea[:, :], mva[:, 1:2], 1e-5, None, ALU.add).then_inc(cross_norm_by_dve, 1)
                    dve.wait_ge(cross_norm_by_dve, n * 12 + 4)
                    nc.vector.tensor_scalar(vareb[:, :], mvb[:, 1:2], 1e-5, None, ALU.add).then_inc(cross_norm_by_dve, 1)
                    dve.wait_ge(cross_rstd_by_pool, n * 4 + 1)
                    nc.vector.tensor_scalar(xna[:, :], X[:, bass.ds((n * 2 + 0) * 256, 256)], mva[:, 0:1], rstda[:, 0:1], ALU.subtract, ALU.mult).then_inc(cross_normed_by_dve, 1)
                    dve.wait_ge(cross_rstd_by_pool, n * 4 + 2)
                    nc.vector.tensor_scalar(xnb[:, :], X[:, bass.ds((n * 2 + 1) * 256, 256)], mvb[:, 0:1], rstdb[:, 0:1], ALU.subtract, ALU.mult).then_inc(cross_normed_by_dve, 1)
                    dve.wait_ge(cross_keys_by_act, n * 2 + 1)
                    nc.vector.tensor_tensor(HXa[:, 0:8, :], kTa[:, 0, :].unsqueeze(1).to_broadcast([128, 8, 128]),
                                           HM[:, :].unsqueeze(2).to_broadcast([128, 8, 128]), ALU.mult).then_inc(cross_expand_by_dve, 1)
                    dve.wait_ge(cross_keys_by_act, n * 2 + 2)
                    nc.vector.tensor_tensor(HXb[:, 0:8, :], kTb[:, 0, :].unsqueeze(1).to_broadcast([128, 8, 128]),
                                           HM[:, :].unsqueeze(2).to_broadcast([128, 8, 128]), ALU.mult)
                    dve.wait_ge(cross_maskrow_by_pe, n * 2 + 1)
                    for k in range(4):
                        last = nc.vector.tensor_copy(VXa[:, :, 0:16].rearrange("p (g k) d -> p g k d", k=4)[:, :, k, :], PS[2][:, 0:64].rearrange("p (g d) -> p g d", g=4))
                    nc.vector.tensor_copy(mba[:, :], PS[2][:, 128:256]).then_inc(cross_values_by_dve, 1)
                    dve.wait_ge(cross_maskrow_by_pe, n * 2 + 2)
                    for k in range(4):
                        last = nc.vector.tensor_copy(VXb[:, :, 0:16].rearrange("p (g k) d -> p g k d", k=4)[:, :, k, :], PS[6][:, 0:64].rearrange("p (g d) -> p g d", g=4))
                    nc.vector.tensor_copy(mbb[:, :], PS[6][:, 128:256]).then_inc(cross_values_by_dve, 1)
                    dve.wait_ge(cross_scores_by_pe, n * 4 + 1)
                    nc.vector.tensor_tensor(SCa[:, 0:4, :].rearrange("p k s -> p (k s)"), PS[0][:, :], ALI[:, 0:512], ALU.add).then_inc(cross_biased_by_dve, 1)
                    nc.vector.tensor_tensor(SCa[:, 4:8, :].rearrange("p k s -> p (k s)"), PS[1][:, :], ALI[:, 512:1024], ALU.add).then_inc(cross_biased_by_dve, 1)
                    dve.wait_ge(cross_scores_by_pe, n * 4 + 2)
                    nc.vector.tensor_tensor(SCa[:, 8:12, :].rearrange("p k s -> p (k s)"), PS[2][:, :], ALI[:, 1024:1536], ALU.add).then_inc(cross_biased_by_dve, 1)
                    nc.vector.tensor_tensor(SCa[:, 12:16, :].rearrange("p k s -> p (k s)"), PS[3][:, :], ALI[:, 1536:2048], ALU.add).then_inc(cross_biased_by_dve, 1)
                    dve.wait_ge(cross_biased_by_dve, n * 8 + 3)
                    nc.vector.tensor_tensor(SCa[:, 8:12, :], SCa[:, 8:12, :], mba[:, :].unsqueeze(1).to_broadcast([128, 4, 128]), ALU.add)
                    dve.wait_ge(cross_biased_by_dve, n * 8 + 4)
                    nc.vector.tensor_tensor(SCa[:, 12:16, :], SCa[:, 12:16, :], mba[:, :].unsqueeze(1).to_broadcast([128, 4, 128]), ALU.add).then_inc(cross_masked_by_dve, 1)
                    dve.wait_ge(cross_masked_by_pool, n * 2 + 1)
                    dve.wait_ge(cross_masked_by_dve, n * 2 + 1)
                    nc.vector.reduce_max(mxa[:, :], SCa[:, :, :], AX.X).then_inc(cross_max_by_dve, 1)
                    dve.wait_ge(cross_scores_by_pe, n * 4 + 3)
                    nc.vector.tensor_tensor(SCb[:, 0:4, :].rearrange("p k s -> p (k s)"), PS[4][:, :], ALI[:, 0:512], ALU.add).then_inc(cross_biased_by_dve, 1)
                    nc.vector.tensor_tensor(SCb[:, 4:8, :].rearrange("p k s -> p (k s)"), PS[5][:, :], ALI[:, 512:1024], ALU.add).then_inc(cross_biased_by_dve, 1)
                    dve.wait_ge(cross_max_by_dve, n * 4 + 1)
                    nc.vector.tensor_scalar(nmxa[:, :], mxa[:, :], -1.0, None, ALU.mult).then_inc(cross_max_by_dve, 1)
                    dve.wait_ge(cross_scores_by_pe, n * 4 + 4)
                    nc.vector.tensor_tensor(SCb[:, 8:12, :].rearrange("p k s -> p (k s)"), PS[6][:, :], ALI[:, 1024:1536], ALU.add).then_inc(cross_biased_by_dve, 1)
                    nc.vector.tensor_tensor(SCb[:, 12:16, :].rearrange("p k s -> p (k s)"), PS[7][:, :], ALI[:, 1536:2048], ALU.add).then_inc(cross_biased_by_dve, 1)
                    dve.wait_ge(cross_biased_by_dve, n * 8 + 7)
                    nc.vector.tensor_tensor(SCb[:, 8:12, :], SCb[:, 8:12, :], mbb[:, :].unsqueeze(1).to_broadcast([128, 4, 128]), ALU.add)
                    dve.wait_ge(cross_biased_by_dve, n * 8 + 8)
                    nc.vector.tensor_tensor(SCb[:, 12:16, :], SCb[:, 12:16, :], mbb[:, :].unsqueeze(1).to_broadcast([128, 4, 128]), ALU.add).then_inc(cross_masked_by_dve, 1)
                    dve.wait_ge(cross_masked_by_pool, n * 2 + 2)
                    dve.wait_ge(cross_masked_by_dve, n * 2 + 2)
                    nc.vector.reduce_max(mxb[:, :], SCb[:, :, :], AX.X).then_inc(cross_max_by_dve, 1)
                    dve.wait_ge(cross_max_by_dve, n * 4 + 3)
                    nc.vector.tensor_scalar(nmxb[:, :], mxb[:, :], -1.0, None, ALU.mult).then_inc(cross_max_by_dve, 1)
                    dve.wait_ge(cross_pturn_by_pe, n * 8 + 2)
                    nc.vector.tensor_copy(PWa[:, 4:8, :].rearrange("p k s -> p (k s)"), PS[1][:, :])
                    dve.wait_ge(cross_pturn_by_pe, n * 8 + 4)
                    nc.vector.tensor_copy(PWa[:, 12:16, :].rearrange("p k s -> p (k s)"), PS[3][:, :]).then_inc(cross_pturn_by_dve, 1)
                    dve.wait_ge(cross_pturn_by_pe, n * 8 + 6)
                    nc.vector.tensor_copy(PWb[:, 4:8, :].rearrange("p k s -> p (k s)"), PS[5][:, :])
                    dve.wait_ge(cross_pturn_by_pe, n * 8 + 8)
                    nc.vector.tensor_copy(PWb[:, 12:16, :].rearrange("p k s -> p (k s)"), PS[7][:, :]).then_inc(cross_pturn_by_dve, 1)
                    dve.wait_ge(cross_attended_by_pe, n * 2 + 1)
                    nc.vector.reciprocal(rda[:, :], PS[0][:, 0:272].rearrange("p (h d) -> p h d", d=17)[:, :, 16]).then_inc(cross_normalize_by_dve, 1)
                    dve.wait_ge(cross_normalize_by_dve, n * 4 + 1)
                    nc.vector.tensor_tensor(by_head(ctx_a[:, :]), PS[0][:, 0:272].rearrange("p (h d) -> p h d", d=17)[:, :, 0:16], rda[:, :].unsqueeze(2).to_broadcast([128, 16, 16]), ALU.mult).then_inc(cross_normalize_by_dve, 1)
                    dve.wait_ge(cross_attended_by_pe, n * 2 + 2)
                    nc.vector.reciprocal(rdb[:, :], PS[4][:, 0:272].rearrange("p (h d) -> p h d", d=17)[:, :, 16]).then_inc(cross_normalize_by_dve, 1)
                    dve.wait_ge(cross_normalize_by_dve, n * 4 + 3)
                    nc.vector.tensor_tensor(by_head(ctx_b[:, :]), PS[4][:, 0:272].rearrange("p (h d) -> p h d", d=17)[:, :, 0:16], rdb[:, :].unsqueeze(2).to_broadcast([128, 16, 16]), ALU.mult).then_inc(cross_normalize_by_dve, 1)
                    dve.wait_ge(cross_outproj_by_pe, n * 2 + 1)
                    nc.vector.tensor_tensor(X[:, bass.ds((n * 2 + 0) * 256, 256)], PS[2][:, 0:256], X[:, bass.ds((n * 2 + 0) * 256, 256)], ALU.add).then_inc(cross_residual_by_dve, 1)
                    dve.wait_ge(cross_residual_by_dve, n * 2 + 1)
                    dve.sem_inc(cross_dve_passed, 1)
                    nc.vector.bn_stats(statsa[:, :], X[:, bass.ds((n * 2 + 0) * 256, 256)]).then_inc(cross_norm_by_dve, 1)
                    dve.wait_ge(cross_outproj_by_pe, n * 2 + 2)
                    nc.vector.tensor_tensor(X[:, bass.ds((n * 2 + 1) * 256, 256)], PS[6][:, 0:256], X[:, bass.ds((n * 2 + 1) * 256, 256)], ALU.add).then_inc(cross_residual_by_dve, 1)
                    dve.wait_ge(cross_norm_by_dve, n * 12 + 7)
                    dve.sem_inc(cross_dve_passed, 1)
                    nc.vector.bn_aggr(mva[:, :], statsa[:, :]).then_inc(cross_norm_by_dve, 1)
                    dve.wait_ge(cross_residual_by_dve, n * 2 + 2)
                    dve.sem_inc(cross_dve_passed, 1)
                    nc.vector.bn_stats(statsb[:, :], X[:, bass.ds((n * 2 + 1) * 256, 256)]).then_inc(cross_norm_by_dve, 1)
                    dve.wait_ge(cross_norm_by_dve, n * 12 + 8)
                    nc.vector.tensor_scalar(varea[:, :], mva[:, 1:2], 1e-5, None, ALU.add).then_inc(cross_norm_by_dve, 1)
                    dve.wait_ge(cross_norm_by_dve, n * 12 + 9)
                    dve.sem_inc(cross_dve_passed, 1)
                    nc.vector.bn_aggr(mvb[:, :], statsb[:, :]).then_inc(cross_norm_by_dve, 1)
                    dve.wait_ge(cross_norm_by_dve, n * 12 + 11)
                    nc.vector.tensor_scalar(vareb[:, :], mvb[:, 1:2], 1e-5, None, ALU.add).then_inc(cross_norm_by_dve, 1)
                    dve.wait_ge(cross_rstd_by_pool, n * 4 + 3)
                    nc.vector.tensor_scalar(xna[:, :], X[:, bass.ds((n * 2 + 0) * 256, 256)], mva[:, 0:1], rstda[:, 0:1], ALU.subtract, ALU.mult).then_inc(cross_normed_by_dve, 1)
                    dve.wait_ge(cross_rstd_by_pool, n * 4 + 4)
                    nc.vector.tensor_scalar(xnb[:, :], X[:, bass.ds((n * 2 + 1) * 256, 256)], mvb[:, 0:1], rstdb[:, 0:1], ALU.subtract, ALU.mult).then_inc(cross_normed_by_dve, 1)
                    dve.wait_ge(cross_router_by_pe, n * 2 + 1)
                    nc.vector.reduce_max(tma[:, :], PS[3][:, 256:264], AX.X).then_inc(cross_route_by_dve, 1)
                    dve.wait_ge(cross_route_by_dve, n * 17 + 1)
                    nc.vector.tensor_scalar(tna[:, :], tma[:, :], -1.0, None, ALU.mult).then_inc(cross_route_by_dve, 1)
                    dve.wait_ge(cross_router_by_pe, n * 2 + 2)
                    nc.vector.reduce_max(tmb[:, :], PS[7][:, 256:264], AX.X).then_inc(cross_route_by_dve, 1)
                    dve.wait_ge(cross_route_by_dve, n * 17 + 3)
                    nc.vector.tensor_scalar(tnb[:, :], tmb[:, :], -1.0, None, ALU.mult).then_inc(cross_route_by_dve, 1)
                    dve.wait_ge(cross_route_by_act, n * 2 + 1)
                    nc.vector.reciprocal(pra[:, :], psa[:, :]).then_inc(cross_route_by_dve, 1)
                    dve.wait_ge(cross_route_by_dve, n * 17 + 5)
                    nc.vector.tensor_scalar(ppa[:, 0:8], pea[:, :], pra[:, 0:1], None, ALU.mult).then_inc(cross_route_by_dve, 1)
                    dve.wait_ge(cross_route_by_act, n * 2 + 2)
                    nc.vector.reciprocal(prb[:, :], psb[:, :]).then_inc(cross_route_by_dve, 1)
                    dve.wait_ge(cross_route_by_dve, n * 17 + 6)
                    dve.sem_inc(cross_dve_passed, 1)
                    nc.vector.max(m8a[:, :], ppa[:, 0:8]).then_inc(cross_route_by_dve, 1)
                    dve.wait_ge(cross_route_by_dve, n * 17 + 7)
                    nc.vector.tensor_scalar(ppb[:, 0:8], peb[:, :], prb[:, 0:1], None, ALU.mult).then_inc(cross_route_by_dve, 1)
                    dve.wait_ge(cross_route_by_dve, n * 17 + 8)
                    nc.vector.reduce_sum(csa[:, :], m8a[:, 0:2], AX.X)
                    dve.wait_ge(cross_route_by_dve, n * 17 + 9)
                    dve.sem_inc(cross_dve_passed, 1)
                    nc.vector.max(m8b[:, :], ppb[:, 0:8]).then_inc(cross_route_by_dve, 1)
                    nc.vector.tensor_copy(topa[:, 0:2], m8a[:, 0:2]).then_inc(cross_route_by_dve, 1)
                    dve.wait_ge(cross_route_by_dve, n * 17 + 10)
                    nc.vector.reduce_sum(csb[:, :], m8b[:, 0:2], AX.X)
                    dve.wait_ge(cross_route_by_dve, n * 17 + 11)
                    dve.sem_inc(cross_dve_passed, 1)
                    nc.vector.match_replace(pza[:, :], topa[:, :], ppa[:, :], 0.0).then_inc(cross_route_by_dve, 1)
                    nc.vector.tensor_scalar(csa[:, :], csa[:, :], 1e-20, None, ALU.add)
                    nc.vector.tensor_copy(topb[:, 0:2], m8b[:, 0:2]).then_inc(cross_route_by_dve, 1)
                    dve.wait_ge(cross_route_by_dve, n * 17 + 12)
                    nc.vector.tensor_tensor(c8a[:, :], ppa[:, 0:8], pza[:, 0:8], ALU.subtract)
                    dve.wait_ge(cross_route_by_dve, n * 17 + 13)
                    dve.sem_inc(cross_dve_passed, 1)
                    nc.vector.match_replace(pzb[:, :], topb[:, :], ppb[:, :], 0.0).then_inc(cross_route_by_dve, 1)
                    nc.vector.tensor_scalar(csb[:, :], csb[:, :], 1e-20, None, ALU.add).then_inc(cross_route_by_dve, 1)
                    nc.vector.reciprocal(cra[:, :], csa[:, :]).then_inc(cross_route_by_dve, 1)
                    dve.wait_ge(cross_route_by_dve, n * 17 + 14)
                    nc.vector.tensor_tensor(c8b[:, :], ppb[:, 0:8], pzb[:, 0:8], ALU.subtract)
                    dve.wait_ge(cross_route_by_dve, n * 17 + 15)
                    nc.vector.reciprocal(crb[:, :], csb[:, :])
                    dve.wait_ge(cross_route_by_dve, n * 17 + 16)
                    nc.vector.tensor_scalar(CW1[:, bass.ds((n * 2 + 0), 1), 0:8].rearrange("p i e -> p (i e)"), c8a[:, :], cra[:, 0:1], None, ALU.mult).then_inc(cross_route_by_dve, 1)
                    dve.wait_ge(cross_route_by_dve, n * 17 + 17)
                    nc.vector.tensor_scalar(CW1[:, bass.ds((n * 2 + 1), 1), 0:8].rearrange("p i e -> p (i e)"), c8b[:, :], crb[:, 0:1], None, ALU.mult)

            @block.scalar
            def _(act):
                act.wait_ge(cross_setup_loads_sp, 112)
                act.wait_ge(cross_setup_by_dve, 1)
                act.wait_ge(cross_setup_by_pool, 1)
                with act.Fori(0, 16) as i:
                    n = i
                    act.wait_ge(cross_turned_by_pe, n * 8 + 9)
                    nc.scalar.activation(cTa[:, :, :].rearrange("p c t -> p (c t)"), PS[1][:, 0:256], ACT.Copy).then_inc(cross_turned_by_act, 1)
                    act.wait_ge(cross_turned_by_pe, n * 8 + 10)
                    nc.scalar.activation(cTb[:, :, :].rearrange("p c t -> p (c t)"), PS[5][:, 0:256], ACT.Copy).then_inc(cross_turned_by_act, 1)
                    act.wait_ge(cross_projected_by_pe, n * 4 + 1)
                    nc.scalar.activation(kTa[:, :, :].rearrange("p c t -> p (c t)"), PS[1][:, 0:256], ACT.Copy).then_inc(cross_keys_by_act, 1)
                    act.wait_ge(cross_projected_by_pe, n * 4 + 2)
                    nc.scalar.activation(kTb[:, :, :].rearrange("p c t -> p (c t)"), PS[5][:, 0:256], ACT.Copy).then_inc(cross_keys_by_act, 1)
                    act.wait_ge(cross_turned_by_pe, n * 8 + 11)
                    nc.scalar.activation(xTa[:, :, :].rearrange("p c t -> p (c t)"), PS[0][:, 0:256], ACT.Copy).then_inc(cross_turned_by_act, 1)
                    act.wait_ge(cross_turned_by_pe, n * 8 + 12)
                    nc.scalar.activation(xTb[:, :, :].rearrange("p c t -> p (c t)"), PS[4][:, 0:256], ACT.Copy).then_inc(cross_turned_by_act, 1)
                    act.wait_ge(cross_projected_by_pe, n * 4 + 3)
                    nc.scalar.activation(qTa[:, :, :].rearrange("p c t -> p (c t)"), PS[0][:, 0:256], ACT.Copy).then_inc(cross_queries_by_act, 1)
                    act.wait_ge(cross_projected_by_pe, n * 4 + 4)
                    nc.scalar.activation(qTb[:, :, :].rearrange("p c t -> p (c t)"), PS[4][:, 0:256], ACT.Copy).then_inc(cross_queries_by_act, 1)
                    act.wait_ge(cross_max_by_dve, n * 4 + 2)
                    for k in range(16):
                        last = nc.scalar.activation(SCa[:, k, :], SCa[:, k, :], ACT.Exp, bias=nmxa[:, k:k + 1])
                    last.then_inc(cross_exp_by_act, 1)
                    act.wait_ge(cross_max_by_dve, n * 4 + 4)
                    for k in range(16):
                        last = nc.scalar.activation(SCb[:, k, :], SCb[:, k, :], ACT.Exp, bias=nmxb[:, k:k + 1])
                    last.then_inc(cross_exp_by_act, 1)
                    act.wait_ge(cross_pturn_by_pe, n * 8 + 1)
                    nc.scalar.activation(PWa[:, 0:4, :].rearrange("p k s -> p (k s)"), PS[0][:, :], ACT.Copy)
                    act.wait_ge(cross_pturn_by_pe, n * 8 + 3)
                    nc.scalar.activation(PWa[:, 8:12, :].rearrange("p k s -> p (k s)"), PS[2][:, :], ACT.Copy).then_inc(cross_pturn_by_act, 1)
                    act.wait_ge(cross_pturn_by_pe, n * 8 + 5)
                    nc.scalar.activation(PWb[:, 0:4, :].rearrange("p k s -> p (k s)"), PS[4][:, :], ACT.Copy)
                    act.wait_ge(cross_pturn_by_pe, n * 8 + 7)
                    nc.scalar.activation(PWb[:, 8:12, :].rearrange("p k s -> p (k s)"), PS[6][:, :], ACT.Copy).then_inc(cross_pturn_by_act, 1)
                    act.wait_ge(cross_turned_by_pe, n * 8 + 13)
                    nc.scalar.activation(cTa[:, :, :].rearrange("p c t -> p (c t)"), PS[1][:, 0:256], ACT.Copy).then_inc(cross_turned_by_act, 1)
                    act.wait_ge(cross_turned_by_pe, n * 8 + 14)
                    nc.scalar.activation(cTb[:, :, :].rearrange("p c t -> p (c t)"), PS[5][:, 0:256], ACT.Copy).then_inc(cross_turned_by_act, 1)
                    act.wait_ge(cross_turned_by_pe, n * 8 + 15)
                    nc.scalar.activation(xTa[:, :, :].rearrange("p c t -> p (c t)"), PS[0][:, 0:256], ACT.Copy).then_inc(cross_turned_by_act, 1)
                    act.wait_ge(cross_turned_by_pe, n * 8 + 16)
                    nc.scalar.activation(xTb[:, :, :].rearrange("p c t -> p (c t)"), PS[4][:, 0:256], ACT.Copy).then_inc(cross_turned_by_act, 1)
                    act.wait_ge(cross_route_by_dve, n * 17 + 2)
                    nc.scalar.activation(pea[:, :], PS[3][:, 256:264], ACT.Exp, bias=tna[:, 0:1], accum_out=psa[:, 0:1]).then_inc(cross_route_by_act, 1)
                    act.wait_ge(cross_route_by_dve, n * 17 + 4)
                    nc.scalar.activation(peb[:, :], PS[7][:, 256:264], ACT.Exp, bias=tnb[:, 0:1], accum_out=psb[:, 0:1]).then_inc(cross_route_by_act, 1)

            @block.gpsimd
            def _(pool):
                nc.gpsimd.memset(NEGHALF[:, :], -0.5)
                nc.gpsimd.memset(onerow[:, :], 1.0)
                nc.gpsimd.memset(VXa[:, :, :], 1.0)
                nc.gpsimd.memset(VXb[:, :, :], 1.0)
                nc.gpsimd.memset(topa[:, :], -1.0)
                nc.gpsimd.memset(ppa[:, :], -1.0)
                nc.gpsimd.memset(topb[:, :], -1.0)
                nc.gpsimd.memset(ppb[:, :], -1.0)
                nc.gpsimd.memset(CW1[:, :, 8:9], 1.0).then_inc(cross_setup_by_pool, 1)
                pool.wait_ge(cross_setup_loads_sp, 112)
                pool.wait_ge(cross_setup_by_dve, 1)
                pool.wait_ge(cross_setup_by_pool, 1)
                with pool.Fori(0, 16) as i:
                    n = i
                    pool.wait_ge(cross_norm_by_dve, n * 12 + 5)
                    nc.gpsimd.tensor_tensor(rstda[:, :], varea[:, :], NEGHALF[:, 0:1], ALU.pow).then_inc(cross_rstd_by_pool, 1)
                    pool.wait_ge(cross_norm_by_dve, n * 12 + 6)
                    nc.gpsimd.tensor_tensor(rstdb[:, :], vareb[:, :], NEGHALF[:, 0:1], ALU.pow).then_inc(cross_rstd_by_pool, 1)
                    pool.wait_ge(cross_keys_by_act, n * 2 + 1)
                    nc.gpsimd.tensor_tensor(HXa[:, 8:16, :], kTa[:, 1, :].unsqueeze(1).to_broadcast([128, 8, 128]),
                                           HM[:, :].unsqueeze(2).to_broadcast([128, 8, 128]), ALU.mult).then_inc(cross_expand_by_pool, 1)
                    pool.wait_ge(cross_keys_by_act, n * 2 + 2)
                    nc.gpsimd.tensor_tensor(HXb[:, 8:16, :], kTb[:, 1, :].unsqueeze(1).to_broadcast([128, 8, 128]),
                                           HM[:, :].unsqueeze(2).to_broadcast([128, 8, 128]), ALU.mult).then_inc(cross_expand_by_pool, 1)
                    pool.wait_ge(cross_biased_by_dve, n * 8 + 1)
                    nc.gpsimd.tensor_tensor(SCa[:, 0:4, :], SCa[:, 0:4, :], mba[:, :].unsqueeze(1).to_broadcast([128, 4, 128]), ALU.add)
                    pool.wait_ge(cross_biased_by_dve, n * 8 + 2)
                    nc.gpsimd.tensor_tensor(SCa[:, 4:8, :], SCa[:, 4:8, :], mba[:, :].unsqueeze(1).to_broadcast([128, 4, 128]), ALU.add).then_inc(cross_masked_by_pool, 1)
                    pool.wait_ge(cross_biased_by_dve, n * 8 + 5)
                    nc.gpsimd.tensor_tensor(SCb[:, 0:4, :], SCb[:, 0:4, :], mbb[:, :].unsqueeze(1).to_broadcast([128, 4, 128]), ALU.add)
                    pool.wait_ge(cross_biased_by_dve, n * 8 + 6)
                    nc.gpsimd.tensor_tensor(SCb[:, 4:8, :], SCb[:, 4:8, :], mbb[:, :].unsqueeze(1).to_broadcast([128, 4, 128]), ALU.add).then_inc(cross_masked_by_pool, 1)
                    pool.wait_ge(cross_norm_by_dve, n * 12 + 10)
                    nc.gpsimd.tensor_tensor(rstda[:, :], varea[:, :], NEGHALF[:, 0:1], ALU.pow).then_inc(cross_rstd_by_pool, 1)
                    pool.wait_ge(cross_norm_by_dve, n * 12 + 12)
                    nc.gpsimd.tensor_tensor(rstdb[:, :], vareb[:, :], NEGHALF[:, 0:1], ALU.pow).then_inc(cross_rstd_by_pool, 1)
                    pool.wait_ge(cross_turned_by_act, n * 8 + 7)
                    pool.sem_inc(cross_pool_passed, 1)
                    nc.gpsimd.tensor_copy(H1T[:, :, bass.ds((n * 2 + 0) * 128, 128)], xTa[:, :, :]).then_inc(cross_kept_by_pool, 1)
                    pool.wait_ge(cross_turned_by_act, n * 8 + 8)
                    pool.wait_ge(cross_kept_by_pool, n * 1 + 1)
                    pool.sem_inc(cross_pool_passed, 1)
                    nc.gpsimd.tensor_copy(H1T[:, :, bass.ds((n * 2 + 1) * 128, 128)], xTb[:, :, :])

            @block.sync
            def _(sp):
                nc.sync.dma_start(HM[:, :], io["head_mask"]).then_inc(cross_setup_loads_sp, 16)
                nc.sync.dma_start(WQ[:, :, :], io["x1_wq"]).then_inc(cross_setup_loads_sp, 16)
                nc.sync.dma_start(WKV[:, :, :], io["x1_wkv"]).then_inc(cross_setup_loads_sp, 16)
                nc.sync.dma_start(WO[:, :, :], io["x1_wo"]).then_inc(cross_setup_loads_sp, 16)
                nc.sync.dma_start(WR[:, :, :], io["f1_router"]).then_inc(cross_setup_loads_sp, 16)
                nc.sync.dma_start(ALI[:, :], io["alibi"]).then_inc(cross_setup_loads_sp, 16)
                nc.sync.dma_start(MK8[:, :], io["mask"]).then_inc(cross_setup_loads_sp, 16)
                sp.wait_ge(cross_setup_loads_sp, 112)
                sp.wait_ge(cross_setup_by_dve, 1)
                sp.wait_ge(cross_setup_by_pool, 1)
                with sp.Fori(0, 16) as i:
                    n = i
                    sp.wait_ge(cross_turned_by_pe, n * 8 + 1)
                    sp.sem_inc(cross_sp_passed, 1)
                    nc.sync.dma_start(cxa[:, :], io["ctx"][bass.ds((n * 2 + 0) * 128, 128), :]).then_inc(cross_context_a_dma, 16)
                    sp.wait_ge(cross_turned_by_pe, n * 8 + 2)
                    sp.sem_inc(cross_sp_passed, 1)
                    nc.sync.dma_start(cxb[:, :], io["ctx"][bass.ds((n * 2 + 1) * 128, 128), :]).then_inc(cross_context_b_dma, 16)

        nc.clear_and_free_semaphores(signals)
        nc.all_engine_barrier()

def ffn1b(nc, io, X, PS, IDENT, shared):
    ctx = ExitStack()
    with ctx:
        def sb(name, shape, dt=F32):
            return ctx.enter_context(nc.sbuf_tensor("ffn1b_" + name, shape, dt))

        signals = []

        def signal(name):
            signals.append(nc.alloc_semaphore(name))
            return signals[-1]

        H1T, CW1 = shared
        CWf = CW1[:, :, :].rearrange("p i e -> p (i e)")
        sl = sb("sl", [128, 3, 512])
        act_ = sb("act", [128, 9, 512])
        WG = sb("WG", [128, 2, 1920])
        WU = sb("WU", [128, 2, 1920])
        WD = sb("WD", [128, 15, 256])

        ffn1b_setup_loads_sp = signal("ffn1b_setup_loads_sp")
        ffn1b_hidden_by_pe = signal("ffn1b_hidden_by_pe")
        ffn1b_silu_by_act = signal("ffn1b_silu_by_act")
        ffn1b_hidden_by_dve = signal("ffn1b_hidden_by_dve")
        ffn1b_down_by_pe = signal("ffn1b_down_by_pe")
        ffn1b_combine_by_dve = signal("ffn1b_combine_by_dve")
        with nc.Block() as block:

            @block.tensor
            def _(pe):
                pe.wait_ge(ffn1b_setup_loads_sp, 48)
                with pe.Fori(0, 8) as g:
                    n = g
                    for w, bank in ((WG, PS[0]), (WU, PS[2])):
                        for c in range(2):
                            last = nc.tensor.matmul(bank[0:128, :], w[:, c, 0:128], H1T[:, c, bass.ds(g * 512, 512)], start=(c == 0), stop=(c == 1))
                    last.then_inc(ffn1b_hidden_by_pe, 1)
                    for w, bank in ((WG, PS[1]), (WU, PS[3])):
                        for c in range(2):
                            last = nc.tensor.matmul(bank[0:128, :], w[:, c, 128:256], H1T[:, c, bass.ds(g * 512, 512)], start=(c == 0), stop=(c == 1))
                    last.then_inc(ffn1b_hidden_by_pe, 1)
                    pe.wait_ge(ffn1b_hidden_by_dve, n * 12 + 1)
                    for w, bank in ((WG, PS[0]), (WU, PS[2])):
                        for c in range(2):
                            last = nc.tensor.matmul(bank[0:112, :], w[:, c, 256:368], H1T[:, c, bass.ds(g * 512, 512)], start=(c == 0), stop=(c == 1))
                    last.then_inc(ffn1b_hidden_by_pe, 1)
                    pe.wait_ge(ffn1b_hidden_by_dve, n * 12 + 2)
                    for w, bank in ((WG, PS[1]), (WU, PS[3])):
                        for c in range(2):
                            last = nc.tensor.matmul(bank[0:128, :], w[:, c, 384:512], H1T[:, c, bass.ds(g * 512, 512)], start=(c == 0), stop=(c == 1))
                    last.then_inc(ffn1b_hidden_by_pe, 1)
                    pe.wait_ge(ffn1b_hidden_by_dve, n * 12 + 3)
                    for w, bank in ((WG, PS[0]), (WU, PS[2])):
                        for c in range(2):
                            last = nc.tensor.matmul(bank[0:128, :], w[:, c, 512:640], H1T[:, c, bass.ds(g * 512, 512)], start=(c == 0), stop=(c == 1))
                    last.then_inc(ffn1b_hidden_by_pe, 1)
                    pe.wait_ge(ffn1b_hidden_by_dve, n * 12 + 4)
                    for w, bank in ((WG, PS[1]), (WU, PS[3])):
                        for c in range(2):
                            last = nc.tensor.matmul(bank[0:112, :], w[:, c, 640:752], H1T[:, c, bass.ds(g * 512, 512)], start=(c == 0), stop=(c == 1))
                    last.then_inc(ffn1b_hidden_by_pe, 1)
                    pe.wait_ge(ffn1b_hidden_by_dve, n * 12 + 5)
                    for w, bank in ((WG, PS[0]), (WU, PS[2])):
                        for c in range(2):
                            last = nc.tensor.matmul(bank[0:128, :], w[:, c, 768:896], H1T[:, c, bass.ds(g * 512, 512)], start=(c == 0), stop=(c == 1))
                    last.then_inc(ffn1b_hidden_by_pe, 1)
                    for j in range(4):
                        for k, (slot, chunk, lo, hi) in enumerate([(0, 0, 0, 128), (2, 2, 0, 48)]):
                            last = nc.tensor.matmul(PS[4 + j // 2][:, (j % 2) * 256:(j % 2) * 256 + 256], act_[lo:hi, slot, j * 128:(j + 1) * 128], WD[lo:hi, chunk, :], start=(k == 0), stop=(k == 1))
                    last.then_inc(ffn1b_down_by_pe, 1)
                    pe.wait_ge(ffn1b_hidden_by_dve, n * 12 + 6)
                    for w, bank in ((WG, PS[1]), (WU, PS[3])):
                        for c in range(2):
                            last = nc.tensor.matmul(bank[0:128, :], w[:, c, 896:1024], H1T[:, c, bass.ds(g * 512, 512)], start=(c == 0), stop=(c == 1))
                    last.then_inc(ffn1b_hidden_by_pe, 1)
                    pe.wait_ge(ffn1b_hidden_by_dve, n * 12 + 7)
                    for w, bank in ((WG, PS[0]), (WU, PS[2])):
                        for c in range(2):
                            last = nc.tensor.matmul(bank[0:112, :], w[:, c, 1024:1136], H1T[:, c, bass.ds(g * 512, 512)], start=(c == 0), stop=(c == 1))
                    last.then_inc(ffn1b_hidden_by_pe, 1)
                    for j in range(4):
                        for k, (slot, chunk, lo, hi) in enumerate([(1, 1, 0, 128), (2, 2, 64, 112)]):
                            last = nc.tensor.matmul(PS[6 + j // 2][:, (j % 2) * 256:(j % 2) * 256 + 256], act_[lo:hi, slot, j * 128:(j + 1) * 128], WD[lo:hi, chunk, :], start=(k == 0), stop=(k == 1))
                    last.then_inc(ffn1b_down_by_pe, 1)
                    pe.wait_ge(ffn1b_combine_by_dve, n * 8 + 1)
                    for j in range(4):
                        for k, (slot, chunk, lo, hi) in enumerate([(3, 3, 0, 128), (5, 5, 0, 48)]):
                            last = nc.tensor.matmul(PS[4 + j // 2][:, (j % 2) * 256:(j % 2) * 256 + 256], act_[lo:hi, slot, j * 128:(j + 1) * 128], WD[lo:hi, chunk, :], start=(k == 0), stop=(k == 1))
                    last.then_inc(ffn1b_down_by_pe, 1)
                    pe.wait_ge(ffn1b_hidden_by_dve, n * 12 + 8)
                    for w, bank in ((WG, PS[1]), (WU, PS[3])):
                        for c in range(2):
                            last = nc.tensor.matmul(bank[0:128, :], w[:, c, 1152:1280], H1T[:, c, bass.ds(g * 512, 512)], start=(c == 0), stop=(c == 1))
                    last.then_inc(ffn1b_hidden_by_pe, 1)
                    for w, bank in ((WG, PS[0]), (WU, PS[2])):
                        for c in range(2):
                            last = nc.tensor.matmul(bank[0:128, :], w[:, c, 1280:1408], H1T[:, c, bass.ds(g * 512, 512)], start=(c == 0), stop=(c == 1))
                    last.then_inc(ffn1b_hidden_by_pe, 1)
                    pe.wait_ge(ffn1b_combine_by_dve, n * 8 + 2)
                    for j in range(4):
                        for k, (slot, chunk, lo, hi) in enumerate([(4, 4, 0, 128), (5, 5, 64, 112)]):
                            last = nc.tensor.matmul(PS[6 + j // 2][:, (j % 2) * 256:(j % 2) * 256 + 256], act_[lo:hi, slot, j * 128:(j + 1) * 128], WD[lo:hi, chunk, :], start=(k == 0), stop=(k == 1))
                    last.then_inc(ffn1b_down_by_pe, 1)
                    pe.wait_ge(ffn1b_hidden_by_dve, n * 12 + 9)
                    for w, bank in ((WG, PS[1]), (WU, PS[3])):
                        for c in range(2):
                            last = nc.tensor.matmul(bank[0:112, :], w[:, c, 1408:1520], H1T[:, c, bass.ds(g * 512, 512)], start=(c == 0), stop=(c == 1))
                    last.then_inc(ffn1b_hidden_by_pe, 1)
                    pe.wait_ge(ffn1b_hidden_by_dve, n * 12 + 10)
                    for w, bank in ((WG, PS[0]), (WU, PS[2])):
                        for c in range(2):
                            last = nc.tensor.matmul(bank[0:128, :], w[:, c, 1536:1664], H1T[:, c, bass.ds(g * 512, 512)], start=(c == 0), stop=(c == 1))
                    last.then_inc(ffn1b_hidden_by_pe, 1)
                    for j in range(4):
                        for k, (slot, chunk, lo, hi) in enumerate([(0, 6, 0, 128), (2, 8, 0, 48)]):
                            last = nc.tensor.matmul(PS[4 + j // 2][:, (j % 2) * 256:(j % 2) * 256 + 256], act_[lo:hi, slot, j * 128:(j + 1) * 128], WD[lo:hi, chunk, :], start=(k == 0), stop=(k == 1))
                    last.then_inc(ffn1b_down_by_pe, 1)
                    pe.wait_ge(ffn1b_hidden_by_dve, n * 12 + 11)
                    for w, bank in ((WG, PS[1]), (WU, PS[3])):
                        for c in range(2):
                            last = nc.tensor.matmul(bank[0:128, :], w[:, c, 1664:1792], H1T[:, c, bass.ds(g * 512, 512)], start=(c == 0), stop=(c == 1))
                    last.then_inc(ffn1b_hidden_by_pe, 1)
                    pe.wait_ge(ffn1b_hidden_by_dve, n * 12 + 12)
                    for w, bank in ((WG, PS[0]), (WU, PS[2])):
                        for c in range(2):
                            last = nc.tensor.matmul(bank[0:96, :], w[:, c, 1792:1888], H1T[:, c, bass.ds(g * 512, 512)], start=(c == 0), stop=(c == 1))
                    last.then_inc(ffn1b_hidden_by_pe, 1)
                    for j in range(4):
                        for k, (slot, chunk, lo, hi) in enumerate([(1, 7, 0, 128), (2, 8, 64, 112)]):
                            last = nc.tensor.matmul(PS[6 + j // 2][:, (j % 2) * 256:(j % 2) * 256 + 256], act_[lo:hi, slot, j * 128:(j + 1) * 128], WD[lo:hi, chunk, :], start=(k == 0), stop=(k == 1))
                    last.then_inc(ffn1b_down_by_pe, 1)
                    pe.wait_ge(ffn1b_combine_by_dve, n * 8 + 5)
                    for j in range(4):
                        for k, (slot, chunk, lo, hi) in enumerate([(3, 9, 0, 128), (5, 11, 0, 48)]):
                            last = nc.tensor.matmul(PS[4 + j // 2][:, (j % 2) * 256:(j % 2) * 256 + 256], act_[lo:hi, slot, j * 128:(j + 1) * 128], WD[lo:hi, chunk, :], start=(k == 0), stop=(k == 1))
                    last.then_inc(ffn1b_down_by_pe, 1)
                    pe.wait_ge(ffn1b_combine_by_dve, n * 8 + 6)
                    for j in range(4):
                        for k, (slot, chunk, lo, hi) in enumerate([(4, 10, 0, 128), (5, 11, 64, 112)]):
                            last = nc.tensor.matmul(PS[6 + j // 2][:, (j % 2) * 256:(j % 2) * 256 + 256], act_[lo:hi, slot, j * 128:(j + 1) * 128], WD[lo:hi, chunk, :], start=(k == 0), stop=(k == 1))
                    last.then_inc(ffn1b_down_by_pe, 1)
                    pe.wait_ge(ffn1b_combine_by_dve, n * 8 + 7)
                    for j in range(4):
                        for k, (slot, chunk, lo, hi) in enumerate([(6, 12, 0, 128), (7, 13, 0, 128), (8, 14, 0, 96)]):
                            last = nc.tensor.matmul(PS[4 + j // 2][:, (j % 2) * 256:(j % 2) * 256 + 256], act_[lo:hi, slot, j * 128:(j + 1) * 128], WD[lo:hi, chunk, :], start=(k == 0), stop=(k == 2))
                    last.then_inc(ffn1b_down_by_pe, 1)

            @block.vector
            def _(dve):
                dve.wait_ge(ffn1b_setup_loads_sp, 48)
                with dve.Fori(0, 8) as g:
                    n = g
                    dve.wait_ge(ffn1b_silu_by_act, n * 14 + 1)
                    nc.vector.tensor_tensor(act_[0:128, 0, :], sl[0:128, 0, :], PS[2][0:128, :], ALU.mult).then_inc(ffn1b_hidden_by_dve, 1)
                    dve.wait_ge(ffn1b_silu_by_act, n * 14 + 2)
                    nc.vector.tensor_tensor(act_[0:128, 1, :], sl[0:128, 1, :], PS[3][0:128, :], ALU.mult).then_inc(ffn1b_hidden_by_dve, 1)
                    dve.wait_ge(ffn1b_silu_by_act, n * 14 + 3)
                    nc.vector.tensor_tensor(act_[0:112, 2, :], sl[0:112, 2, :], PS[2][0:112, :], ALU.mult).then_inc(ffn1b_hidden_by_dve, 1)
                    dve.wait_ge(ffn1b_silu_by_act, n * 14 + 4)
                    nc.vector.tensor_tensor(act_[0:128, 3, :], sl[0:128, 0, :], PS[3][0:128, :], ALU.mult).then_inc(ffn1b_hidden_by_dve, 1)
                    dve.wait_ge(ffn1b_silu_by_act, n * 14 + 5)
                    nc.vector.tensor_tensor(act_[0:128, 4, :], sl[0:128, 1, :], PS[2][0:128, :], ALU.mult).then_inc(ffn1b_hidden_by_dve, 1)
                    dve.wait_ge(ffn1b_silu_by_act, n * 14 + 6)
                    nc.vector.tensor_tensor(act_[0:112, 5, :], sl[0:112, 2, :], PS[3][0:112, :], ALU.mult).then_inc(ffn1b_hidden_by_dve, 1)
                    dve.wait_ge(ffn1b_down_by_pe, n * 9 + 1)
                    dve.wait_ge(ffn1b_silu_by_act, n * 14 + 7)
                    nc.vector.tensor_tensor(act_[0:128, 0, :], sl[0:128, 0, :], PS[2][0:128, :], ALU.mult).then_inc(ffn1b_hidden_by_dve, 1)
                    for j in range(4):
                        xs = X[:, bass.ds(g * 1024 + j * 256, 256)]
                        last = nc.vector.scalar_tensor_tensor(xs, PS[4 + j // 2][:, (j % 2) * 256:(j % 2) * 256 + 256], CWf[:, bass.ds(g * 36 + 0 + j * 9, 1)], xs, ALU.mult, ALU.add)
                    last.then_inc(ffn1b_combine_by_dve, 1)
                    dve.wait_ge(ffn1b_down_by_pe, n * 9 + 2)
                    dve.wait_ge(ffn1b_silu_by_act, n * 14 + 8)
                    nc.vector.tensor_tensor(act_[0:112, 2, :], sl[0:112, 2, :], PS[2][0:112, :], ALU.mult)
                    nc.vector.tensor_tensor(act_[0:128, 1, :], sl[0:128, 1, :], PS[3][0:128, :], ALU.mult).then_inc(ffn1b_hidden_by_dve, 1)
                    dve.wait_ge(ffn1b_combine_by_dve, n * 8 + 1)
                    for j in range(4):
                        xs = X[:, bass.ds(g * 1024 + j * 256, 256)]
                        last = nc.vector.scalar_tensor_tensor(xs, PS[6 + j // 2][:, (j % 2) * 256:(j % 2) * 256 + 256], CWf[:, bass.ds(g * 36 + 1 + j * 9, 1)], xs, ALU.mult, ALU.add)
                    last.then_inc(ffn1b_combine_by_dve, 1)
                    dve.wait_ge(ffn1b_down_by_pe, n * 9 + 3)
                    dve.wait_ge(ffn1b_combine_by_dve, n * 8 + 2)
                    for j in range(4):
                        xs = X[:, bass.ds(g * 1024 + j * 256, 256)]
                        last = nc.vector.scalar_tensor_tensor(xs, PS[4 + j // 2][:, (j % 2) * 256:(j % 2) * 256 + 256], CWf[:, bass.ds(g * 36 + 2 + j * 9, 1)], xs, ALU.mult, ALU.add)
                    last.then_inc(ffn1b_combine_by_dve, 1)
                    dve.wait_ge(ffn1b_silu_by_act, n * 14 + 9)
                    nc.vector.tensor_tensor(act_[0:128, 3, :], sl[0:128, 0, :], PS[3][0:128, :], ALU.mult).then_inc(ffn1b_hidden_by_dve, 1)
                    dve.wait_ge(ffn1b_down_by_pe, n * 9 + 4)
                    dve.wait_ge(ffn1b_silu_by_act, n * 14 + 10)
                    nc.vector.tensor_tensor(act_[0:128, 4, :], sl[0:128, 1, :], PS[2][0:128, :], ALU.mult).then_inc(ffn1b_hidden_by_dve, 1)
                    dve.wait_ge(ffn1b_combine_by_dve, n * 8 + 3)
                    for j in range(4):
                        xs = X[:, bass.ds(g * 1024 + j * 256, 256)]
                        last = nc.vector.scalar_tensor_tensor(xs, PS[6 + j // 2][:, (j % 2) * 256:(j % 2) * 256 + 256], CWf[:, bass.ds(g * 36 + 3 + j * 9, 1)], xs, ALU.mult, ALU.add)
                    last.then_inc(ffn1b_combine_by_dve, 1)
                    dve.wait_ge(ffn1b_silu_by_act, n * 14 + 11)
                    nc.vector.tensor_tensor(act_[0:112, 5, :], sl[0:112, 2, :], PS[3][0:112, :], ALU.mult).then_inc(ffn1b_hidden_by_dve, 1)
                    dve.wait_ge(ffn1b_silu_by_act, n * 14 + 12)
                    nc.vector.tensor_tensor(act_[0:128, 6, :], sl[0:128, 0, :], PS[2][0:128, :], ALU.mult).then_inc(ffn1b_hidden_by_dve, 1)
                    dve.wait_ge(ffn1b_combine_by_dve, n * 8 + 4)
                    dve.wait_ge(ffn1b_down_by_pe, n * 9 + 5)
                    for j in range(4):
                        xs = X[:, bass.ds(g * 1024 + j * 256, 256)]
                        last = nc.vector.scalar_tensor_tensor(xs, PS[4 + j // 2][:, (j % 2) * 256:(j % 2) * 256 + 256], CWf[:, bass.ds(g * 36 + 4 + j * 9, 1)], xs, ALU.mult, ALU.add)
                    last.then_inc(ffn1b_combine_by_dve, 1)
                    dve.wait_ge(ffn1b_silu_by_act, n * 14 + 13)
                    nc.vector.tensor_tensor(act_[0:128, 7, :], sl[0:128, 1, :], PS[3][0:128, :], ALU.mult)
                    dve.wait_ge(ffn1b_silu_by_act, n * 14 + 14)
                    nc.vector.tensor_tensor(act_[0:96, 8, :], sl[0:96, 2, :], PS[2][0:96, :], ALU.mult)
                    dve.wait_ge(ffn1b_combine_by_dve, n * 8 + 5)
                    dve.wait_ge(ffn1b_down_by_pe, n * 9 + 6)
                    for j in range(4):
                        xs = X[:, bass.ds(g * 1024 + j * 256, 256)]
                        last = nc.vector.scalar_tensor_tensor(xs, PS[6 + j // 2][:, (j % 2) * 256:(j % 2) * 256 + 256], CWf[:, bass.ds(g * 36 + 5 + j * 9, 1)], xs, ALU.mult, ALU.add)
                    last.then_inc(ffn1b_combine_by_dve, 1)
                    dve.wait_ge(ffn1b_down_by_pe, n * 9 + 7)
                    dve.wait_ge(ffn1b_combine_by_dve, n * 8 + 6)
                    for j in range(4):
                        xs = X[:, bass.ds(g * 1024 + j * 256, 256)]
                        last = nc.vector.scalar_tensor_tensor(xs, PS[4 + j // 2][:, (j % 2) * 256:(j % 2) * 256 + 256], CWf[:, bass.ds(g * 36 + 6 + j * 9, 1)], xs, ALU.mult, ALU.add)
                    last.then_inc(ffn1b_combine_by_dve, 1)
                    dve.wait_ge(ffn1b_down_by_pe, n * 9 + 8)
                    dve.wait_ge(ffn1b_combine_by_dve, n * 8 + 7)
                    for j in range(4):
                        xs = X[:, bass.ds(g * 1024 + j * 256, 256)]
                        last = nc.vector.scalar_tensor_tensor(xs, PS[6 + j // 2][:, (j % 2) * 256:(j % 2) * 256 + 256], CWf[:, bass.ds(g * 36 + 7 + j * 9, 1)], xs, ALU.mult, ALU.add)
                    last.then_inc(ffn1b_combine_by_dve, 1)
                    dve.wait_ge(ffn1b_down_by_pe, n * 9 + 9)
                    dve.wait_ge(ffn1b_combine_by_dve, n * 8 + 8)
                    for j in range(4):
                        xs = X[:, bass.ds(g * 1024 + j * 256, 256)]
                        last = nc.vector.scalar_tensor_tensor(xs, PS[4 + j // 2][:, (j % 2) * 256:(j % 2) * 256 + 256], CWf[:, bass.ds(g * 36 + 8 + j * 9, 1)], xs, ALU.mult, ALU.add)

            @block.scalar
            def _(act):
                act.wait_ge(ffn1b_setup_loads_sp, 48)
                with act.Fori(0, 8) as g:
                    n = g
                    act.wait_ge(ffn1b_hidden_by_pe, n * 15 + 1)
                    nc.scalar.activation(sl[0:128, 0, :], PS[0][0:128, :], ACT.Silu).then_inc(ffn1b_silu_by_act, 1)
                    act.wait_ge(ffn1b_hidden_by_pe, n * 15 + 2)
                    nc.scalar.activation(sl[0:128, 1, :], PS[1][0:128, :], ACT.Silu).then_inc(ffn1b_silu_by_act, 1)
                    act.wait_ge(ffn1b_hidden_by_pe, n * 15 + 3)
                    nc.scalar.activation(sl[0:112, 2, :], PS[0][0:112, :], ACT.Silu).then_inc(ffn1b_silu_by_act, 1)
                    act.wait_ge(ffn1b_hidden_by_pe, n * 15 + 4)
                    nc.scalar.activation(sl[0:128, 0, :], PS[1][0:128, :], ACT.Silu).then_inc(ffn1b_silu_by_act, 1)
                    act.wait_ge(ffn1b_hidden_by_pe, n * 15 + 5)
                    nc.scalar.activation(sl[0:128, 1, :], PS[0][0:128, :], ACT.Silu).then_inc(ffn1b_silu_by_act, 1)
                    act.wait_ge(ffn1b_hidden_by_pe, n * 15 + 6)
                    nc.scalar.activation(sl[0:112, 2, :], PS[1][0:112, :], ACT.Silu).then_inc(ffn1b_silu_by_act, 1)
                    act.wait_ge(ffn1b_hidden_by_pe, n * 15 + 7)
                    nc.scalar.activation(sl[0:128, 0, :], PS[0][0:128, :], ACT.Silu).then_inc(ffn1b_silu_by_act, 1)
                    act.wait_ge(ffn1b_hidden_by_pe, n * 15 + 8)
                    nc.scalar.activation(sl[0:128, 1, :], PS[1][0:128, :], ACT.Silu)
                    act.wait_ge(ffn1b_hidden_by_pe, n * 15 + 9)
                    nc.scalar.activation(sl[0:112, 2, :], PS[0][0:112, :], ACT.Silu).then_inc(ffn1b_silu_by_act, 1)
                    act.wait_ge(ffn1b_hidden_by_pe, n * 15 + 10)
                    nc.scalar.activation(sl[0:128, 0, :], PS[1][0:128, :], ACT.Silu).then_inc(ffn1b_silu_by_act, 1)
                    act.wait_ge(ffn1b_hidden_by_pe, n * 15 + 11)
                    nc.scalar.activation(sl[0:128, 1, :], PS[0][0:128, :], ACT.Silu).then_inc(ffn1b_silu_by_act, 1)
                    act.wait_ge(ffn1b_hidden_by_pe, n * 15 + 12)
                    nc.scalar.activation(sl[0:112, 2, :], PS[1][0:112, :], ACT.Silu).then_inc(ffn1b_silu_by_act, 1)
                    act.wait_ge(ffn1b_hidden_by_pe, n * 15 + 13)
                    nc.scalar.activation(sl[0:128, 0, :], PS[0][0:128, :], ACT.Silu).then_inc(ffn1b_silu_by_act, 1)
                    act.wait_ge(ffn1b_hidden_by_pe, n * 15 + 14)
                    nc.scalar.activation(sl[0:128, 1, :], PS[1][0:128, :], ACT.Silu).then_inc(ffn1b_silu_by_act, 1)
                    act.wait_ge(ffn1b_hidden_by_pe, n * 15 + 15)
                    nc.scalar.activation(sl[0:96, 2, :], PS[0][0:96, :], ACT.Silu).then_inc(ffn1b_silu_by_act, 1)

            @block.gpsimd
            def _(pool):
                pass

            @block.sync
            def _(sp):
                nc.sync.dma_start(WG[:, :, :], io["e1_gate"]).then_inc(ffn1b_setup_loads_sp, 16)
                nc.sync.dma_start(WU[:, :, :], io["e1_up"]).then_inc(ffn1b_setup_loads_sp, 16)
                nc.sync.dma_start(WD[:, :, :], io["e1_down"]).then_inc(ffn1b_setup_loads_sp, 16)

        nc.clear_and_free_semaphores(signals)
        nc.all_engine_barrier()

def decoder(nc, io, out):
    ctx = ExitStack()
    with ctx:
        X = ctx.enter_context(nc.sbuf_tensor("X", [128, 32 * 256], F32))
        IDENT = ctx.enter_context(nc.sbuf_tensor("IDENT", [128, 128], F32))
        PS = [ctx.enter_context(nc.psum_tensor(f"PS{k}", [128, 512], F32)) for k in range(8)]
        x_loaded = nc.alloc_semaphore("x_loaded")
        x_stored = nc.alloc_semaphore("x_stored")
        with nc.Block() as block:
            @block.sync
            def _(sp):
                sp.dma_start(IDENT[:, :], io["ident"]).then_inc(x_loaded, 16)
                sp.dma_start(X[:, :].rearrange("p (i d) -> p i d", d=256), io["x"].rearrange("(i p) d -> p i d", p=128)).then_inc(x_loaded, 16)
                sp.wait_ge(x_loaded, 32)
        with ExitStack() as layer:
            def keep(name, shape):
                return layer.enter_context(nc.sbuf_tensor(name, shape, F32))
            shared = (keep("XT", [128, 2, 4096]), keep("F1T", [128, 4096]), keep("G1T", [128, 4096]), keep("BETA", [128, 16, 32]))
            prep(nc, io, X, PS, IDENT, shared)
            gsa(nc, io, X, PS, IDENT, shared)
        with ExitStack() as layer:
            def keep(name, shape):
                return layer.enter_context(nc.sbuf_tensor(name, shape, F32))
            shared = None
            mlstm(nc, io, X, PS, IDENT, shared)
        with ExitStack() as layer:
            def keep(name, shape):
                return layer.enter_context(nc.sbuf_tensor(name, shape, F32))
            shared = (keep("H0T", [128, 2, 4096]), keep("CW0", [128, 32, 9]))
            ffn0a(nc, io, X, PS, IDENT, shared)
            ffn0b(nc, io, X, PS, IDENT, shared)
        with ExitStack() as layer:
            def keep(name, shape):
                return layer.enter_context(nc.sbuf_tensor(name, shape, F32))
            shared = None
            infini(nc, io, X, PS, IDENT, shared)
        with ExitStack() as layer:
            def keep(name, shape):
                return layer.enter_context(nc.sbuf_tensor(name, shape, F32))
            shared = (keep("H1T", [128, 2, 4096]), keep("CW1", [128, 32, 9]))
            cross(nc, io, X, PS, IDENT, shared)
            ffn1b(nc, io, X, PS, IDENT, shared)

        with nc.Block() as block:
            @block.sync
            def _(sp):
                sp.dma_start(out.rearrange("(i p) d -> p i d", p=128), X[:, :].rearrange("p (i d) -> p i d", d=256)).then_inc(x_stored, 16)
                sp.wait_ge(x_stored, 16)


def rows(w):
    k, n = w.shape
    return w.reshape(k // 128, 128, n).transpose(1, 0, 2)


def chunks(experts, shared):
    k = experts.shape[1]
    n = shared.shape[1]
    out = np.zeros((k, 12 + -(-n // 128), 128), experts.dtype)
    for q in range(4):
        for x in range(2):
            out[:, 3 * q + x] = experts[2 * q + x][:, :128]
            out[:, 3 * q + 2, 64 * x:64 * x + 48] = experts[2 * q + x][:, 128:]
    out = out.reshape(k, -1)
    out[:, 12 * 128:12 * 128 + n] = shared
    return out


def level_masks():
    j = np.arange(128)[:, None]
    out = []
    for lv in range(6):
        b = 2 ** lv
        t = np.array([x for x in range(128) if (x // b) % 2 == 1])[None, :]
        out.append(np.tile((j // b == t // b - 1).astype(np.float32), (1, 4)))
    return np.stack(out, 1)


def layout(inputs):
    a = {k: np.asarray(v) for k, v in inputs.items()}
    d = {}
    d["x"] = a["x"].reshape(4096, 256)
    d["ident"] = np.eye(128, dtype=np.float32)
    d["wf1"], d["wg1"], d["wb"] = (rows(a["L0_attn_" + k]) for k in ("Wf1", "Wg1", "Wb"))
    per_head = [rows(a["L0_attn_" + k]).reshape(128, 2, 16, 128) for k in ("Wq", "Wk", "Wv", "Ww")]
    d["w_heads"] = np.stack(per_head, 3).transpose(0, 2, 1, 3, 4).reshape(128, 16 * 1024)
    d["w_gates"] = np.stack([a["L0_attn_" + k].reshape(128, 16, 128) for k in ("Wf2", "Wg2")], 2).reshape(128, 16 * 256)
    d["w_conv"] = np.stack([a["L0_attn_" + k].reshape(16, 128, 4) for k in ("cq", "ck", "cv")], 2).transpose(1, 0, 2, 3).reshape(128, 16 * 12)
    d["wo_heads"] = a["L0_attn_Wo"].reshape(16, 128, 256).transpose(1, 0, 2).reshape(128, 16 * 256)
    d["bg2"] = a["L0_attn_bg2"].reshape(16, 128).T
    d["norm_w"] = a["L0_attn_norm_w"].reshape(128, 1)
    d["masks"] = level_masks()
    d["eyes"] = np.tile(np.eye(128, dtype=np.float32), (1, 4))

    t = np.arange(128)
    same = t[:, None] // 64 == t[None, :] // 64
    causal = np.where(same & (t[None, :] <= t[:, None]), 0.0, -1e30).astype(np.float32)
    d["neg_causal"] = np.tile(causal, (1, 4))
    d["neg_causal_t"] = np.tile(causal.T, (1, 4))
    d["block_mean"] = np.where(same, 1.0 / 64, 0.0).astype(np.float32)
    d["head_mask"] = np.where(t[:, None] // 16 == np.arange(8)[None, :], 0.25, 0.0).astype(np.float32)
    first = (t % 64 == 0)
    d["resets"] = np.tile(np.concatenate([np.where(first, 0.0, 1.0), np.where(first, -1e30, 0.0)])[None].astype(np.float32), (16, 1))
    d["select"] = np.repeat(np.eye(16, dtype=np.float32), 128, axis=1)
    inv = (np.float32(1.0) / np.float32(1000000.0) ** (np.arange(0, 16, 2, dtype=np.float32) / np.float32(16))).astype(np.float32)
    angle = np.tile(np.arange(64, dtype=np.float32)[:, None] * inv[None, :], (2, 2)).T
    d["cos"] = np.tile(np.cos(angle), (8, 2)).astype(np.float32)
    d["sin"] = np.tile(np.sin(angle), (8, 2)).astype(np.float32)
    slopes = (np.float32(2.0 ** -0.5) ** np.arange(1, 17, dtype=np.float32)).astype(np.float32)
    rel = (t[None, :] - t[:, None]).astype(np.float32)
    d["alibi"] = np.concatenate([np.where(same, slopes[h] * rel, np.float32(-3e38)) for h in range(16)], 1).astype(np.float32)
    d["ctx"] = a["ctx_2048"].reshape(4096, 256)
    d["w_if"] = np.concatenate([rows(a["L0_xattn_Wi"]), rows(a["L0_xattn_Wf"])], 2)
    d["b_if"] = np.stack([a["L0_xattn_bi"], a["L0_xattn_bf"]], 1)
    d["ln_scale"] = a["L0_xattn_ln_scale"].reshape(1, 256)
    for k in "qkvo":
        d["f0_w" + k] = rows(a["L0_ffn_w" + k])
    d["f0_router"] = rows(np.concatenate([a["L0_ffn_w_router"], a["L0_ffn_w_sh_eg"]], 1))
    d["f0_bqkv"] = np.concatenate([a["L0_ffn_b" + k] for k in "qkv"]).reshape(1, 768)
    d["f0_ln"] = np.concatenate([a["L0_ffn_w_ln1"].reshape(2, 128), a["L0_ffn_w_ln2"].reshape(2, 128)], 0).T
    d["e0_gate"] = rows(chunks(a["L0_ffn_w_gate_e"], a["L0_ffn_w_sh_gate"]))
    d["e0_up"] = rows(chunks(a["L0_ffn_w_up_e"], a["L0_ffn_w_sh_up"]))
    d["e0_down"] = rows(chunks(a["L0_ffn_w_down_e"].transpose(0, 2, 1), a["L0_ffn_w_sh_down"].T).T)
    for k in "qkvo":
        d["l1_w" + k] = rows(a["L1_attn_w_" + k].T)
    d["memories"] = rows(a["L1_attn_memories"].transpose(1, 0, 2).reshape(256, 1024))
    d["memory_norms"] = rows(a["L1_attn_memory_norms"].T)
    d["gate"] = np.broadcast_to(a["L1_attn_gate"].reshape(1, 1), (128, 1))
    d["x1_wq"], d["x1_wo"] = rows(a["L1_xattn_Wq"]), rows(a["L1_xattn_Wo"])
    d["x1_wkv"] = rows(np.concatenate([a["L1_xattn_Wk"], a["L1_xattn_Wv"]], 1))
    d["mask"] = a["mask_BxS2_bf1"].reshape(1, 4096).view(np.uint8)
    d["f1_router"] = rows(a["L1_ffn_gate_weight"].T)
    d["e1_gate"] = rows(chunks(a["L1_ffn_w_gate"].transpose(0, 2, 1), a["L1_ffn_sw_gate"].T))
    d["e1_up"] = rows(chunks(a["L1_ffn_w_up"].transpose(0, 2, 1), a["L1_ffn_sw_up"].T))
    d["e1_down"] = rows(chunks(a["L1_ffn_w_down"], a["L1_ffn_sw_down"]).T)
    return {k: np.ascontiguousarray(v) for k, v in d.items()}


def kernel(**inputs):
    import concourse.bacc as bacc
    from concourse.bass_utils import run_bass_kernel_spmd

    nc = bacc.Bacc("TRN2", target_bir_lowering=False, num_devices=1)
    arrays, io = {}, {}
    for name, array in layout(inputs).items():
        arrays["in_" + name] = array
        io[name] = nc.dram_tensor("in_" + name, array.shape, mybir.dt.from_np(array.dtype), kind="ExternalInput").ap()
    out = nc.dram_tensor("out_x", (4096, 256), F32, kind="ExternalOutput").ap()
    decoder(nc, io, out)
    r = run_bass_kernel_spmd(nc, [arrays], core_ids=[0])
    return r.results[0]["out_x"].reshape(64, 64, 256)
```
